# Optimizing a Trainium2 kernel written in Bass

```python
import numpy as np
import jax
import jax.numpy as jnp

def _softmax(x, axis=-1):
    return jax.nn.softmax(x, axis=axis)

def _gelu(x):
    return jax.nn.gelu(x, approximate=True)

def _silu(x):
    return jax.nn.silu(x)

def _sigmoid(x):
    return jax.nn.sigmoid(x)

def _layernorm(x, axis=-1, eps=1e-05):
    m = jnp.mean(x, axis=axis, keepdims=True)
    v = jnp.var(x, axis=axis, keepdims=True)
    return (x - m) / jnp.sqrt(v + eps)

def _scatter_add(tgt, idx, src, axis=0):
    return tgt.at[idx].add(src)

def _segment_sum(src, seg, n):
    return jax.ops.segment_sum(src, seg, n)
kernel_name = 'mk_vit_tower_postln_d1_tok_img1024_r4_62a6d5'

def setup_inputs(seed: int=0):
    np.random.seed(seed)
    _w = jnp.asarray

    def _rec_inputs():
        import jax
        import jax.numpy as jnp
        _rk = jax.random.key(seed)
        x = -0.00016672 + 0.999947 * jax.random.normal(jax.random.fold_in(_rk, 1), (64, 3, 96, 96), jnp.float32)
        return x
    x = _rec_inputs()

    def _L0_tok_setup():
        import jax, jax.numpy as jnp
        import numpy as np
        IMAGE_SIZE = 96
        PATCH = 16
        N_EMBD = 256
        C = 3
        N_PATCHES = (IMAGE_SIZE // PATCH) ** 2
        PATCH_DIM = C * PATCH * PATCH
        key = jax.random.key(seed)
        kx, kw, kb, kp = jax.random.split(key, 4)
        B = 64
        x = jax.random.normal(kx, (B, C, IMAGE_SIZE, IMAGE_SIZE), dtype=jnp.float32)
        bound = 1.0 / np.sqrt(PATCH_DIM)
        W = jax.random.uniform(kw, (N_EMBD, PATCH_DIM), minval=-bound, maxval=bound, dtype=jnp.float32)
        b = jax.random.uniform(kb, (N_EMBD,), minval=-bound, maxval=bound, dtype=jnp.float32)
        pos_embd = jax.random.normal(kp, (1, N_PATCHES, N_EMBD), dtype=jnp.float32) * 0.02
        return {'x': x, 'W': W, 'b': b, 'pos_embd': pos_embd}
    _L0_tok_all = _L0_tok_setup()
    _L0_tok_in = {k: v for k, v in _L0_tok_all.items() if k in ('W', 'b', 'pos_embd')}
    del _L0_tok_all

    def _L0_attn_setup():
        import jax, jax.numpy as jnp
        import numpy as np
        import math
        NUM_HEADS = 16
        ATTN_WIDTH = 64
        key = jax.random.key(seed)
        ks = jax.random.split(key, 5)
        B, S, C, H = (2, 512, 256, 256)
        scale = 0.02
        return {'x': jax.random.normal(ks[0], (B, S, C), dtype=jnp.float32), 'Wq': jax.random.normal(ks[1], (C, H), dtype=jnp.float32) * scale, 'Wk': jax.random.normal(ks[2], (C, H), dtype=jnp.float32) * scale, 'Wv': jax.random.normal(ks[3], (C, H), dtype=jnp.float32) * scale, 'Wo': jax.random.normal(ks[4], (H, C), dtype=jnp.float32) * scale}
    _L0_attn_all = _L0_attn_setup()
    _L0_attn_in = {k: v for k, v in _L0_attn_all.items() if k in ('Wq', 'Wk', 'Wv', 'Wo')}
    del _L0_attn_all

    def _L0_ffn_setup():
        import jax, jax.numpy as jnp
        import numpy as np
        D = 256
        H = 16
        KV = 8
        HD = D // H
        M = 896
        E = 8
        TOPK = 2
        EPS = 1e-06
        ROPE_THETA = 10000.0

        def _rmsnorm(x, w, eps=EPS):
            xf = x.astype(jnp.float32)
            var = jnp.mean(xf * xf, axis=-1, keepdims=True)
            return (xf * jax.lax.rsqrt(var + eps)).astype(x.dtype) * w

        def _rope(q, k):
            S = q.shape[1]
            inv_freq = 1.0 / ROPE_THETA ** (jnp.arange(0, HD, 2, dtype=jnp.float32) / HD)
            ang = jnp.arange(S, dtype=jnp.float32)[:, None] * inv_freq[None, :]
            cos = jnp.concatenate([jnp.cos(ang), jnp.cos(ang)], axis=-1)[None, :, None, :]
            sin = jnp.concatenate([jnp.sin(ang), jnp.sin(ang)], axis=-1)[None, :, None, :]

            def rot_half(t):
                t1, t2 = jnp.split(t, 2, axis=-1)
                return jnp.concatenate([-t2, t1], axis=-1)
            return (q * cos + rot_half(q) * sin, k * cos + rot_half(k) * sin)
        key = jax.random.key(seed)
        ks = jax.random.split(key, 12)
        s = 0.02
        B, S = (2, 256)
        return {'x': jax.random.normal(ks[0], (B, S, D), jnp.float32), 'ln1_w': jnp.ones((D,), jnp.float32), 'ln2_w': jnp.ones((D,), jnp.float32), 'wq': jax.random.normal(ks[1], (D, H * HD), jnp.float32) * s, 'wk': jax.random.normal(ks[2], (D, KV * HD), jnp.float32) * s, 'wv': jax.random.normal(ks[3], (D, KV * HD), jnp.float32) * s, 'wo': jax.random.normal(ks[4], (H * HD, D), jnp.float32) * s, 'router_w': jax.random.normal(ks[5], (D, E), jnp.float32) * s, 'w_gate': jax.random.normal(ks[6], (E, D, M), jnp.float32) * s, 'w_up': jax.random.normal(ks[7], (E, D, M), jnp.float32) * s, 'w_down': jax.random.normal(ks[8], (E, M, D), jnp.float32) * s}
    _L0_ffn_all = _L0_ffn_setup()
    _L0_ffn_in = {k: v for k, v in _L0_ffn_all.items() if k in ('ln1_w', 'ln2_w', 'wq', 'wk', 'wv', 'wo', 'router_w', 'w_gate', 'w_up', 'w_down')}
    del _L0_ffn_all
    return {'x': x, 'L0_tok_W': _L0_tok_in['W'], 'L0_tok_b': _L0_tok_in['b'], 'L0_tok_pos_embd': _L0_tok_in['pos_embd'], 'L0_attn_Wq': _L0_attn_in['Wq'], 'L0_attn_Wk': _L0_attn_in['Wk'], 'L0_attn_Wv': _L0_attn_in['Wv'], 'L0_attn_Wo': _L0_attn_in['Wo'], 'L0_ffn_ln1_w': _L0_ffn_in['ln1_w'], 'L0_ffn_ln2_w': _L0_ffn_in['ln2_w'], 'L0_ffn_wq': _L0_ffn_in['wq'], 'L0_ffn_wk': _L0_ffn_in['wk'], 'L0_ffn_wv': _L0_ffn_in['wv'], 'L0_ffn_wo': _L0_ffn_in['wo'], 'L0_ffn_router_w': _L0_ffn_in['router_w'], 'L0_ffn_w_gate': _L0_ffn_in['w_gate'], 'L0_ffn_w_up': _L0_ffn_in['w_up'], 'L0_ffn_w_down': _L0_ffn_in['w_down']}

def reference(x, L0_tok_W, L0_tok_b, L0_tok_pos_embd, L0_attn_Wq, L0_attn_Wk, L0_attn_Wv, L0_attn_Wo, L0_ffn_ln1_w, L0_ffn_ln2_w, L0_ffn_wq, L0_ffn_wk, L0_ffn_wv, L0_ffn_wo, L0_ffn_router_w, L0_ffn_w_gate, L0_ffn_w_up, L0_ffn_w_down):
    import jax
    import jax.numpy as jnp

    def _L0_tok_ref(x, W, b, pos_embd):
        import jax, jax.numpy as jnp
        import numpy as np
        IMAGE_SIZE = 96
        PATCH = 16
        N_EMBD = 256
        C = 3
        N_PATCHES = (IMAGE_SIZE // PATCH) ** 2
        PATCH_DIM = C * PATCH * PATCH
        B, Cc, H, Wd = x.shape
        p = PATCH
        Hp, Wp = (H // p, Wd // p)
        patches = x.reshape(B, Cc, Hp, p, Wp, p)
        patches = patches.transpose(0, 2, 4, 1, 3, 5)
        patches = patches.reshape(B, Hp * Wp, Cc * p * p)
        out = jnp.einsum('bnd,ed->bne', patches, W) + b + pos_embd
        return out

    def _L0_attn_ref(x, Wq, Wk, Wv, Wo):
        import jax, jax.numpy as jnp
        import numpy as np
        import math
        NUM_HEADS = 16
        ATTN_WIDTH = 64
        B, S, C = x.shape
        H = NUM_HEADS
        dh = Wq.shape[1] // H

        def split_heads(t):
            return t.reshape(B, S, H, dh).transpose(0, 2, 1, 3)
        q = split_heads(x @ Wq)
        k = split_heads(x @ Wk)
        v = split_heads(x @ Wv)
        scores = jnp.einsum('bhqd,bhkd->bhqk', q, k) / math.sqrt(dh)
        scores = jnp.exp(scores - jnp.max(scores, axis=-1, keepdims=True))
        i = jnp.arange(S)[:, None]
        j = jnp.arange(S)[None, :]
        d = j - i
        half = ATTN_WIDTH // 2
        mask = (d <= half - 1) & (d >= -half)
        scores = jnp.where(mask, scores, 0.0)
        weights = jax.nn.softmax(scores, axis=-1)
        out = jnp.einsum('bhqk,bhkd->bhqd', weights, v)
        out = out.transpose(0, 2, 1, 3).reshape(B, S, H * dh)
        return out @ Wo

    def _L0_ffn_ref(x, ln1_w, ln2_w, wq, wk, wv, wo, router_w, w_gate, w_up, w_down):
        import jax, jax.numpy as jnp
        import numpy as np
        D = 256
        H = 16
        KV = 8
        HD = D // H
        M = 896
        E = 8
        TOPK = 2
        EPS = 1e-06
        ROPE_THETA = 10000.0

        def _rmsnorm(x, w, eps=EPS):
            xf = x.astype(jnp.float32)
            var = jnp.mean(xf * xf, axis=-1, keepdims=True)
            return (xf * jax.lax.rsqrt(var + eps)).astype(x.dtype) * w

        def _rope(q, k):
            S = q.shape[1]
            inv_freq = 1.0 / ROPE_THETA ** (jnp.arange(0, HD, 2, dtype=jnp.float32) / HD)
            ang = jnp.arange(S, dtype=jnp.float32)[:, None] * inv_freq[None, :]
            cos = jnp.concatenate([jnp.cos(ang), jnp.cos(ang)], axis=-1)[None, :, None, :]
            sin = jnp.concatenate([jnp.sin(ang), jnp.sin(ang)], axis=-1)[None, :, None, :]

            def rot_half(t):
                t1, t2 = jnp.split(t, 2, axis=-1)
                return jnp.concatenate([-t2, t1], axis=-1)
            return (q * cos + rot_half(q) * sin, k * cos + rot_half(k) * sin)
        B, S, _ = x.shape
        h = _rmsnorm(x, ln1_w)
        q = (h @ wq).reshape(B, S, H, HD)
        k = (h @ wk).reshape(B, S, KV, HD)
        v = (h @ wv).reshape(B, S, KV, HD)
        q, k = _rope(q, k)
        rep = H // KV
        k = jnp.repeat(k, rep, axis=2)
        v = jnp.repeat(v, rep, axis=2)
        scores = jnp.einsum('bqhd,bkhd->bhqk', q, k) / jnp.sqrt(jnp.float32(HD))
        causal = jnp.tril(jnp.ones((S, S), bool))
        scores = jnp.where(causal[None, None], scores, jnp.finfo(scores.dtype).min)
        attn = jax.nn.softmax(scores, axis=-1)
        ao = jnp.einsum('bhqk,bkhd->bqhd', attn, v).reshape(B, S, H * HD)
        x = x + ao @ wo
        h = _rmsnorm(x, ln2_w)
        logits = h @ router_w
        probs = jax.nn.softmax(logits, axis=-1)
        topv, topi = jax.lax.top_k(probs, TOPK)
        topv = topv / jnp.sum(topv, axis=-1, keepdims=True)
        weights = jnp.sum(jax.nn.one_hot(topi, E, dtype=h.dtype) * topv[..., None], axis=-2)
        gate = jnp.einsum('bsd,edm->bsem', h, w_gate)
        up = jnp.einsum('bsd,edm->bsem', h, w_up)
        act = jax.nn.silu(gate) * up * weights[..., None]
        moe = jnp.einsum('bsem,emd->bsd', act, w_down)
        return x + moe
    h = _L0_tok_ref(x, L0_tok_W, L0_tok_b, L0_tok_pos_embd)
    h = _layernorm(h + _L0_attn_ref(h, L0_attn_Wq, L0_attn_Wk, L0_attn_Wv, L0_attn_Wo), axis=-1)
    h = _layernorm(h + _L0_ffn_ref(h, L0_ffn_ln1_w, L0_ffn_ln2_w, L0_ffn_wq, L0_ffn_wk, L0_ffn_wv, L0_ffn_wo, L0_ffn_router_w, L0_ffn_w_gate, L0_ffn_w_up, L0_ffn_w_down), axis=-1)
    return h

_drawn_inputs = setup_inputs


def setup_inputs(seed=0):
    import zlib

    import numpy as np

    out = dict(_drawn_inputs(seed))
    spreads = {'L0_ffn_ln1_w': (1.0, 0.6), 'L0_ffn_ln2_w': (1.0, 0.6)}
    factors = {'L0_attn_Wq': 8.0,
     'L0_attn_Wk': 8.0,
     'L0_attn_Wv': 3.228,
     'L0_attn_Wo': 3.174,
     'L0_ffn_wq': 8.0,
     'L0_ffn_wk': 8.0,
     'L0_ffn_wv': 2.991,
     'L0_ffn_wo': 2.987,
     'L0_ffn_router_w': 5.086,
     'L0_ffn_w_gate': 4.536,
     'L0_ffn_w_up': 4.475,
     'L0_ffn_w_down': 4.476}
    for name, (base, spread) in spreads.items():
        noise = np.random.default_rng([zlib.crc32(name.encode()), seed]).standard_normal(out[name].shape)
        drawn = base * np.exp(spread * noise) if base else spread * noise
        out[name] = jnp.asarray(drawn.astype(out[name].dtype))
    for name, factor in factors.items():
        out[name] = (out[name] * factor).astype(out[name].dtype)
    return out
```

```python
import concourse.bass as bass
from concourse import mybir
from contextlib import ExitStack

IMAGES, SEQ, DIM, HEADS, HD = 64, 36, 256, 16, 16
PATCH_DIM = 768
FF, EXPERTS = 896, 8
IPG = 3
ROWS = IPG * SEQ
GROUPS = -(-IMAGES // IPG)
LAST_ROWS = (IMAGES - IPG * (GROUPS - 1)) * SEQ
TOKENS = IMAGES * SEQ
KT = DIM // 128
PT_TILES = PATCH_DIM // 128
TILE = 128
TILES = (2 * TOKENS + EXPERTS * (TILE - 1)) // TILE
REGION = TOKENS + TILE
SPARE_TILES = TILES - 2 * TOKENS // TILE
XS_ROWS = EXPERTS * REGION + SPARE_TILES * TILE
CHUNKS = 6
CH = 3 * SEQ
DOWN_TILES = FF // 128
EXPERT_COLS = KT * 2 * FF + DOWN_TILES * DIM
HALF = (512, FF - 512)
EARLY = 4
LN_EPS, RMS_EPS = 1e-5, 1e-6
PEEL = 4
STEPS = GROUPS + 2


def program(nc, patches, tok_w, tok_b, pos, a_wqk, a_wv, a_wo, b_wqk, b_wv, b_wo, ln1, ln2, router,
            expert_w, headmask4, headmask3, imagemask, window, causal, rope_cos, rope_sin, rotate,
            identity, lower, expert_iota, region_base, thresholds, tile_ids, before, partition_ids,
            out):
    f32, bf16, u32 = mybir.dt.float32, mybir.dt.bfloat16, mybir.dt.uint32
    ALU, ACT, AX = mybir.AluOpType, mybir.ActivationFunctionType, mybir.AxisListType
    V, P, T, A = nc.vector, nc.gpsimd, nc.tensor, nc.scalar
    xs = nc.dram_tensor("expert_rows_in", [XS_ROWS, DIM], f32, kind="Internal").ap()
    ys = nc.dram_tensor("expert_rows_out", [TILES * TILE, DIM], f32, kind="Internal").ap()
    residual = nc.dram_tensor("residual", [GROUPS * ROWS, DIM], f32, kind="Internal").ap()

    ctx = ExitStack()
    with ctx:
        def sb(name, shape, dt=f32):
            return ctx.enter_context(nc.sbuf_tensor(name, shape, dt))

        def sem(name):
            return ctx.enter_context(nc.semaphore(name))

        weights = sb("weights", [128, EXPERTS * EXPERT_COLS])
        used = [EARLY * EXPERT_COLS]

        def early(*free):
            n = 1
            for f in free:
                n *= f
            v = weights[:, used[0]:used[0] + n]
            used[0] += n
            assert used[0] <= EXPERTS * EXPERT_COLS
            names = " ".join(f"d{i}" for i in range(len(free)))
            return v.rearrange(f"p ({names}) -> p {names}", **{f"d{i}": f for i, f in enumerate(free)})

        pat = [early(PT_TILES, ROWS) for _ in range(2)]
        tokw = early(PT_TILES, DIM)
        wqk = [early(KT, 512) for _ in range(2)]
        wv = [early(KT, DIM) for _ in range(2)]
        wo = [early(KT, DIM) for _ in range(2)]
        qm = [early(KT, IPG, ROWS) for _ in range(2)]
        vrep = [early(IPG, DIM) for _ in range(2)]
        vx = [early(IPG, CHUNKS * 48) for _ in range(2)]
        kx = [early(KT, 4, ROWS) for _ in range(2)]
        z = [early(HEADS, SEQ) for _ in range(2)]
        pr = [early(CHUNKS * CH) for _ in range(2)]
        posb, tokb, ln1w, ln2w = early(DIM), early(DIM), early(DIM), early(DIM)
        qk_sb, qk_cos, qk_sin = early(512), early(512), early(512)
        hm4, hm3, imk, win, cau = early(4), early(HEADS), early(IPG), early(7), early(SEQ)
        cosT, sinT, rotm = early(2, 128), early(2, 128), early(128)
        routw = early(KT, EXPERTS)
        xt = [early(KT, 128) for _ in range(3)]
        ot = [early(KT, ROWS) for _ in range(2)]
        vs = [early(DIM) for _ in range(2)]
        pt = [sb(f"pt{i}", [128, CHUNKS, ROWS]) for i in range(2)]
        sel = [sb(f"sel{i}", [128, 3, CHUNKS * 48]) for i in range(2)]
        xa, hb = sb("xa", [128, DIM]), sb("hb", [128, DIM])
        h1 = [sb(f"h1_{i}", [128, DIM]) for i in range(2)]
        rr = [sb(f"rr_{i}", [128, DIM]) for i in range(2)]
        h2 = [sb(f"h2_{i}", [128, DIM]) for i in range(2)]
        res = [sb(f"res_{i}", [128, DIM]) for i in range(2)]
        kk = sb("kk", [128, KT, ROWS])
        junk = sb("junk", [128, DIM])
        ident = sb("ident", [128, 128])
        low, eio, rb = sb("low", [128, ROWS]), sb("eio", [128, EXPERTS]), sb("rb", [128, EXPERTS])
        lowb, oneb = sb("lowb", [128, ROWS], bf16), sb("oneb", [128, 128], bf16)
        mx, sm, ri = ([sb(f"{n}{i}", [128, HEADS]) for i in range(2)] for n in ("mx", "sm", "ri"))
        w_all = sb("w_all", [128, GROUPS, 2])
        place_all = sb("place_all", [128, GROUPS, 2])
        exp_all = sb("exp_all", [128, GROUPS, 2])
        slot_all = sb("slot_all", [128, GROUPS, 2], u32)
        eps = sb("eps", [128, 2])
        st = sb("st", [128, 6])
        mv = sb("mv", [128, 2])
        nrm = [sb(f"nrm{i}", [128, 8]) for i in range(3)]
        top, topi = sb("top", [128, 8]), sb("topi", [128, 8], u32)
        topf = sb("topf", [128, 2])
        rt = sb("rt", [128, 8])
        oh = sb("oh", [128, 2, EXPERTS])
        cnt, cntb = sb("cnt", [128, EXPERTS]), sb("cntb", [128, EXPERTS], bf16)
        tot, totb = sb("tot", [128, EXPERTS]), sb("totb", [128, EXPERTS], bf16)
        place, hit = sb("place", [128, EXPERTS]), sb("hit", [128, 2, EXPERTS])
        slotf, slot = sb("slotf", [128, 2]), [sb(f"slot{i}", [128, 2], u32) for i in range(2)]

        S = [ctx.enter_context(nc.psum_tensor(f"S{i}", [128, 2, 512], f32)) for i in range(2)]
        L = [ctx.enter_context(nc.psum_tensor(f"L{i}", [128, 512], f32)) for i in range(2)]
        Rp = ctx.enter_context(nc.psum_tensor("Rp", [128, 2, 512], f32))

        names = ("x_t", "xt", "qk", "v", "qm", "kx", "vs", "vrep", "vx", "s", "mx", "z", "e", "sm", "ri",
                 "p_t", "pt", "o", "o0", "osel", "on", "o_t", "ot", "y")
        AB = [{n: sem(f"{'ab'[i]}_{n}") for n in names} for i in range(2)]
        consts_loaded, setup_dve, setup_pool = sem("consts_loaded"), sem("setup_dve"), sem("setup_pool")
        pat_loaded = [sem(f"pat_loaded{i}") for i in range(2)]
        embedded, x_ready = sem("embedded"), sem("x_ready")
        e1_done, masked, e2_done = sem("e1_done"), sem("masked"), sem("e2_done")
        r_res, r_stat, r_aggr, h1_ready = sem("r_res"), sem("r_stat"), sem("r_aggr"), sem("h1_ready")
        n_sq = [sem(f"n_sq{i}") for i in range(3)]
        n_ln = [sem(f"n_ln{i}") for i in range(3)]
        n_y0 = [sem(f"n_y0{i}") for i in range(3)]
        n_dve = [sem(f"n_dve{i}") for i in range(3)]
        hb_ready, qk_copied, rotated = sem("hb_ready"), sem("qk_copied"), sem("rotated")
        by_cos, by_sin, kk_ready = sem("by_cos"), sem("by_sin"), sem("kk_ready")
        rr_ready, res_ready, h2_ready = sem("rr_ready"), sem("res_ready"), sem("h2_ready")
        res_stored = [sem(f"res_stored{i}") for i in range(2)]
        h2_t, h2t, logits = sem("h2_t"), sem("h2t"), sem("logits")
        top_d, top_i, gap, gap_exp = sem("top_d"), sem("top_i"), sem("gap"), sem("gap_exp")
        gate_sum, index_float, gate_inv, one_hot = sem("gate_sum"), sem("index_float"), sem("gate_inv"), sem("one_hot")
        count_float, gates_kept, counted, ranked = sem("count_float"), sem("gates_kept"), sem("counted"), sem("ranked")
        placed, total_float, totalled, hits = sem("placed"), sem("total_float"), sem("totalled"), sem("hits")
        slot_sum, slots_ready, slots_kept, causal_done = sem("slot_sum"), sem("slots_ready"), sem("slots_kept"), sem("causal_done")
        scattered = [sem(f"scattered{i}") for i in range(2)]
        expert_loaded = [sem(f"expert_loaded{e}") for e in range(EXPERTS)]
        zero_ready, counts_ready, tail_slots, zeroed = sem("zero_ready"), sem("counts_ready"), sem("tail_slots"), sem("zeroed")
        plan, plan_ready, experts_ready = sem("plan"), sem("plan_ready"), sem("experts_ready")
        x_loaded = [sem(f"x_loaded{i}") for i in range(2)]
        mt, mxt = sem("mt"), sem("mxt")
        gu, sg, ac, a_t, at = ([sem(f"{n}{i}") for i in range(2)] for n in ("gu", "sg", "ac", "a_t", "at"))
        y_ready, y_copied = sem("y_ready"), sem("y_copied")
        y_stored = [sem(f"y_stored{i}") for i in range(2)]
        idx_ready, combined, summed = sem("idx_ready"), sem("combined"), sem("summed")
        gathered = [sem(f"gathered{i}") for i in range(2)]
        base_loaded = [sem(f"base_loaded{i}") for i in range(2)]
        out_ready, out_stored = sem("out_ready"), [sem(f"out_stored{i}") for i in range(2)]

        def past(value):
            return not isinstance(value, int) or value > 0

        def alone(eng, value):
            value = value if isinstance(value, int) else eng.compute_val(value)
            eng.wait_ge(setup_dve, 1)
            return value

        def bc(ap, dim, shape):
            return ap.unsqueeze(dim).to_broadcast(shape)

        def row_of(at, step, n=1):
            return bass.ds(at, n) if step is None else slice(at, at + n)

        E4 = [ROWS, HEADS, SEQ]
        xg = [xa, hb]
        xm = [h1[0], h1[1]]
        sgb = [sb("sg0", [128, HALF[0]]), sb("sg1", [128, HALF[1]])]
        acb = [sb("ac0", [128, HALF[0]]), sb("ac1", [128, HALF[1]])]
        atb = [sel[0], sel[1]]
        yb = [rr[0], rr[1]]
        zero = junk
        tails = sb("tails", [128, EXPERTS], u32)
        tailf = sb("tailf", [128, EXPERTS])
        pid = sb("pid", [128, 1])
        thr, tid, bef = sb("thr", [128, TOKENS // TILE]), sb("tid", [1, TILES]), sb("bef", [128, EXPERTS, EXPERTS])
        over, nt = sb("over", [128, EXPERTS, TOKENS // TILE]), sb("nt", [128, EXPERTS])
        pre, cum = sb("pre", [128, EXPERTS, EXPERTS]), sb("cum", [128, EXPERTS])
        shift = sb("shift", [128, EXPERTS])
        own = sel[0][:].rearrange("p a b -> p (a b)")[:, 0:2 * GROUPS * EXPERTS].rearrange("p (g e) -> p g e", e=EXPERTS)
        moved = sb("moved", [128, 2 * GROUPS])
        ge, gt = (pt[i][0:1].rearrange("p a b -> p (a b)")[:, 0:TILES * EXPERTS].rearrange("p (j e) -> p j e", e=EXPERTS)
                  for i in range(2))
        te, tb, tl, tr, tw = (sb(f"t_{n}", [1, TILES]) for n in ("e", "b", "l", "r", "w"))
        row_tab, col_tab, need_tab = (sb(n, [1, TILES], u32) for n in ("row_tab", "col_tab", "need_tab"))
        yg = [[h2[0], h2[1]], [res[0], res[1]]]
        bt = [rr[0], rr[1]]
        ob = [h1[0], h1[1]]
        cidx = [sb(f"cidx{i}", [128, 2], u32) for i in range(2)]
        acc = [xa, hb]

        consts = [(tokw, tok_w), (tokb[0:ROWS], tok_b), (posb[0:ROWS], pos), (wqk[0], a_wqk), (wv[0], a_wv),
                  (wo[0], a_wo), (wqk[1], b_wqk), (wv[1], b_wv), (wo[1], b_wo), (ln1w[0:ROWS], ln1),
                  (ln2w[0:ROWS], ln2), (routw, router), (hm4, headmask4), (hm3[0:ROWS], headmask3),
                  (imk[0:ROWS], imagemask), (win[0:ROWS], window), (cau[0:ROWS], causal), (cosT, rope_cos),
                  (sinT, rope_sin), (rotm, rotate), (ident[:], identity), (low[0:ROWS], lower),
                  (eio[:], expert_iota), (rb[:], region_base),
                  (pid[:], partition_ids), (thr[:], thresholds), (tid[:], tile_ids), (bef[:], before)]

        def steps(eng, body):
            for s in range(PEEL):
                body(s, s % 2, s)
            with eng.Fori(PEEL, GROUPS - 3, 2) as s:
                body(s, 0, None)
                body(s + 1, 1, None)
            for s in range(GROUPS - 2, STEPS):
                body(s, s % 2, s)

        def live(step, lag):
            return step is None or lag <= step < GROUPS + lag

        with nc.Block() as block:
            @block.sync
            def _(sp):
                for dst, src in consts:
                    sp.dma_start(dst, src).then_inc(consts_loaded, 16)
                sp.dma_start(pat[0], patches[:, 0:1].rearrange("p o (t r) -> p (o t) r", r=ROWS)).then_inc(pat_loaded[0], 16)

                for e in range(EARLY):
                    sp.dma_start(weights[:, e * EXPERT_COLS:(e + 1) * EXPERT_COLS], expert_w[:, e])\
                      .then_inc(expert_loaded[e], 16)

                def body(s, par, step):
                    if step is None or step + 1 < GROUPS:
                        if past(s):
                            sp.wait_ge(embedded, s)
                        sp.dma_start(pat[1 - par], patches[:, row_of(s + 1, step)].rearrange("p o (t r) -> p (o t) r", r=ROWS))\
                          .then_inc(pat_loaded[1 - par], 16)
                    for l in range(2):
                        if live(step, l):
                            sp.wait_ge(AB[l]["vs"], s + 1 - l)
                            for h in range(3):
                                for b in range(IPG):
                                    sp.dma_start(vrep[l][SEQ * h:SEQ * (h + 1), b],
                                                 vs[l][SEQ * b:SEQ * (b + 1)]).then_inc(AB[l]["vrep"], 16)
                    if live(step, 1):
                        sp.wait_ge(res_ready, s)
                        sp.dma_start(residual[row_of((s - 1) * ROWS, step, ROWS), :], res[1 - par][0:ROWS]).then_inc(res_stored[1 - par], 16)

                steps(sp, body)

            @block.gpsimd
            def _(pool):
                pool.wait_ge(consts_loaded, 16 * len(consts))
                for l in range(2):
                    P.memset(vx[l], 0.0).then_inc(setup_pool, 1)
                    P.memset(pr[l], 0.0).then_inc(setup_pool, 1)
                    P.memset(qm[l], 0.0).then_inc(setup_pool, 1)
                for i in range(3):
                    P.memset(xt[i], 0.0).then_inc(setup_pool, 1)
                pool.wait_ge(setup_pool, 9)

                def expand_v(l, n):
                    pool.wait_ge(AB[l]["vrep"], 144 * n)
                    shape = [ROWS, IPG, HEADS, HD]
                    P.tensor_tensor(vx[l][0:ROWS, :, 0:DIM].rearrange("p b (h d) -> p b h d", d=HD),
                                    vrep[l][0:ROWS].rearrange("p b (h d) -> p b h d", d=HD),
                                    hm3[0:ROWS].unsqueeze(1).unsqueeze(3).to_broadcast(shape),
                                    ALU.mult).then_inc(AB[l]["vx"], 1)

                def body(s, par, step):
                    if live(step, 1):
                        pool.wait_ge(qk_copied, s)
                        P.tensor_tensor(qk_cos.rearrange("p (w j t) -> p w j t", w=2, j=2),
                                        qk_sb.rearrange("p (w j t) -> p w j t", w=2, j=2),
                                        bc(cosT, 2, [128, 2, 2, 128]), ALU.mult).then_inc(by_cos, 1)
                    if live(step, 0):
                        expand_v(0, s + 1)
                    if live(step, 1):
                        pool.wait_ge(kk_ready, s)
                        for t in range(KT):
                            P.tensor_tensor(kx[1][:, t], bc(kk[:, t], 1, [128, 4, ROWS]), bc(hm4, 2, [128, 4, ROWS]),
                                            ALU.mult).then_inc(AB[1]["kx"], 1)
                        expand_v(1, s)
                        pool.wait_ge(AB[1]["mx"], s)
                        P.tensor_tensor(z[1][0:ROWS], z[1][0:ROWS], bc(mx[1][0:ROWS], 2, E4), ALU.subtract)\
                         .then_inc(AB[1]["z"], 1)
                    if live(step, 2):
                        rows = ROWS if step is None or step < STEPS - 1 else LAST_ROWS
                        pool.wait_ge(slots_ready, alone(pool, s - 1))
                        for k in range(2):
                            P.indirect_dma_start(xs, bass.IndirectOffsetOnAxis(slot[par][0:rows, k:k + 1], 0),
                                                 h2[par][0:rows], None).then_inc(scattered[par], 16)

                steps(pool, body)

            @block.scalar
            def _(act):
                A.preload_act_table_set("natural_log_exp_and_others")
                act.wait_ge(consts_loaded, 16 * len(consts))
                act.wait_ge(setup_pool, 9)
                act.wait_ge(setup_dve, 1)

                def inv_sqrt(i, src, n, rows=ROWS):
                    e = 0 if i == 2 else 1
                    if i != 2:
                        A.activation(junk[0:rows], src, ACT.Square, accum_out=nrm[i][0:rows, 0:1]).then_inc(n_sq[i], 1)
                        act.wait_ge(n_sq[i], n)
                        A.activation(nrm[i][0:rows, 1:2], nrm[i][0:rows, 0:1], ACT.Ln, bias=eps[0:rows, 1:2],
                                     scale=1.0 / DIM).then_inc(n_ln[i], 1)
                    else:
                        A.activation(nrm[i][0:rows, 1:2], mv[0:rows, 1:2], ACT.Ln, bias=eps[0:rows, 0:1]).then_inc(n_ln[i], 1)
                    act.wait_ge(n_ln[i], n)
                    A.activation(nrm[i][0:rows, 2:3], nrm[i][0:rows, 1:2], ACT.Exp, scale=-0.5).then_inc(n_y0[i], 1)

                def xt_copy(i, ready, n, done, rows=ROWS):
                    ps = L[i] if i < 2 else Rp[:, 0]
                    act.wait_ge(ready, n)
                    A.activation(xt[i][:, :, 0:rows], ps[:, 0:KT * rows].rearrange("p (t r) -> p t r", t=KT),
                                 ACT.Copy).then_inc(done, 1)

                def diag(l):
                    v = qm[l].rearrange("p t b r -> p t (b r)")
                    return bass.AP(tensor=v.tensor, offset=v.offset,
                                   ap=[v.ap[0], [IPG * ROWS, KT], [ROWS + SEQ, IPG], [1, SEQ]])

                def body(s, par, step):
                    a, b, r = live(step, 0), live(step, 1), live(step, 2)
                    rrows = ROWS if step is None or step < STEPS - 1 else LAST_ROWS
                    nA, nB, nR = s + 1, s, s - 1
                    if b:
                        act.wait_ge(h1_ready, nB)
                        inv_sqrt(0, h1[1 - par][0:ROWS], nB)
                    if r:
                        act.wait_ge(rr_ready, nR)
                        inv_sqrt(1, rr[par][0:rrows], nR, rrows)
                    if b:
                        xt_copy(1, AB[1]["x_t"], nB, AB[1]["xt"])
                    if a:
                        xt_copy(0, AB[0]["x_t"], nA, AB[0]["xt"])
                        act.wait_ge(AB[0]["qk"], nA)
                        A.activation(diag(0), S[0][:, 0, 0:256].rearrange("p (t r) -> p t r", t=KT)[:, :, 0:ROWS]
                                     .rearrange("p t (b q) -> p t b q", b=IPG), ACT.Copy, scale=0.25)\
                         .then_inc(AB[0]["qm"], 1)
                        act.wait_ge(AB[0]["v"], nA)
                        A.activation(vs[0][0:ROWS], L[0][0:ROWS, 0:DIM], ACT.Copy).then_inc(AB[0]["vs"], 1)
                    if b:
                        act.wait_ge(AB[1]["qk"], nB)
                        A.activation(qk_sb, S[1][:, 0], ACT.Copy).then_inc(qk_copied, 1)
                        act.wait_ge(AB[1]["v"], nB)
                        A.activation(vs[1][0:ROWS], L[1][0:ROWS, 0:DIM], ACT.Copy).then_inc(AB[1]["vs"], 1)
                    if r:
                        xt_copy(2, h2_t, nR, h2t, rrows)
                    if a:
                        act.wait_ge(AB[0]["z"], nA)
                        A.activation(z[0][0:ROWS], z[0][0:ROWS], ACT.Exp).then_inc(e1_done, 1)
                        act.wait_ge(masked, 2 * nA)
                        A.activation(pr[0][0:ROWS, 0:HEADS * SEQ].rearrange("p (h k) -> p h k", k=SEQ), z[0][0:ROWS],
                                     ACT.Exp).then_inc(AB[0]["e"], 1)
                    if b:
                        act.wait_ge(AB[1]["z"], nB)
                        A.activation(pr[1][0:ROWS, 0:HEADS * SEQ].rearrange("p (h k) -> p h k", k=SEQ), z[1][0:ROWS],
                                     ACT.Exp).then_inc(AB[1]["e"], 1)
                    for l, on, n in ((0, a, nA), (1, b, nB)):
                        if on:
                            act.wait_ge(AB[l]["p_t"], n)
                            A.activation(pt[l][0:CH].rearrange("p (j c) r -> p j (c r)", j=2),
                                         S[l][0:CH, :, 0:3 * ROWS], ACT.Copy).then_inc(AB[l]["pt"], 1)
                    if r:
                        act.wait_ge(gap, nR)
                        A.activation(rt[0:rrows, 1:2], rt[0:rrows, 0:1], ACT.Exp).then_inc(gap_exp, 1)
                    for l, on, n in ((0, a, nA), (1, b, nB)):
                        if on:
                            act.wait_ge(AB[l]["o"], n)
                            A.activation(sel[l][0:ROWS, 0].rearrange("p (j d) -> p j d", j=2),
                                         S[l][0:ROWS, :, 0:144],
                                         ACT.Copy, scale=imk[0:ROWS, 0:1]).then_inc(AB[l]["o0"], 1)
                    for l, on, n in ((0, a, nA), (1, b, nB)):
                        if on:
                            act.wait_ge(AB[l]["o_t"], n)
                            A.activation(ot[l], L[l][:, 0:KT * ROWS].rearrange("p (t r) -> p t r", t=KT),
                                         ACT.Copy).then_inc(AB[l]["ot"], 1)
                    if a:
                        act.wait_ge(r_aggr, nA)
                        inv_sqrt(2, None, nA)

                steps(act, body)

            @block.vector
            def _(dve):
                V.memset(eps[:, 0:1], LN_EPS)
                V.memset(oneb[:], 1.0)
                V.memset(tot[:], 0.0)
                V.memset(place_all[:], 0.0)
                V.memset(exp_all[:], 0.0)
                V.memset(totb[:], 0.0)
                V.memset(eps[:, 1:2], RMS_EPS).then_inc(setup_dve, 1)
                dve.wait_ge(consts_loaded, 16 * len(consts))
                dve.wait_ge(setup_pool, 9)
                V.tensor_tensor(posb[0:ROWS], posb[0:ROWS], tokb[0:ROWS], ALU.add).then_inc(setup_dve, 1)
                V.tensor_copy(lowb[0:ROWS], low[0:ROWS]).then_inc(setup_dve, 1)
                dve.wait_ge(setup_dve, 3)

                def newton(i, n, rows=ROWS):
                    q = nrm[i][0:rows]
                    if i == 2:
                        V.tensor_scalar(q[:, 3:4], mv[0:rows, 1:2], LN_EPS, None, ALU.add).then_inc(n_dve[i], 1)
                    else:
                        dve.wait_ge(n_sq[i], n)
                        V.tensor_scalar(q[:, 3:4], q[:, 0:1], 1.0 / DIM, RMS_EPS, ALU.mult, ALU.add).then_inc(n_dve[i], 1)
                    dve.wait_ge(n_y0[i], n)
                    dve.wait_ge(n_dve[i], 4 * n - 3)
                    V.scalar_tensor_tensor(q[:, 4:5], q[:, 2:3], q[:, 2:3], q[:, 3:4], ALU.mult, ALU.mult).then_inc(n_dve[i], 1)
                    dve.wait_ge(n_dve[i], 4 * n - 2)
                    V.tensor_scalar(q[:, 5:6], q[:, 4:5], -0.5, 1.5, ALU.mult, ALU.add).then_inc(n_dve[i], 1)
                    dve.wait_ge(n_dve[i], 4 * n - 1)
                    V.tensor_tensor(q[:, 6:7], q[:, 5:6], q[:, 2:3], ALU.mult).then_inc(n_dve[i], 1)
                    dve.wait_ge(n_dve[i], 4 * n)

                def row_sum(l, n):
                    dve.wait_ge(AB[l]["e"], n)
                    V.tensor_reduce(sm[l][0:ROWS], pr[l][0:ROWS, 0:HEADS * SEQ].rearrange("p (h k) -> p h k", k=SEQ),
                                    AX.X, ALU.add).then_inc(AB[l]["sm"], 1)
                    dve.wait_ge(AB[l]["sm"], n)
                    V.reciprocal(ri[l][0:ROWS], sm[l][0:ROWS]).then_inc(AB[l]["ri"], 1)

                def select(l, n):
                    for b in (1, 2):
                        dve.wait_ge(AB[l]["o0"] if b == 1 else AB[l]["osel"], n if b == 1 else 2 * n - 1)
                        V.scalar_tensor_tensor(
                            sel[l][0:ROWS, b].rearrange("p (j d) -> p j d", j=2), S[l][0:ROWS, :, 144 * b:144 * (b + 1)],
                            imk[0:ROWS, b:b + 1], sel[l][0:ROWS, b - 1].rearrange("p (j d) -> p j d", j=2),
                            ALU.mult, ALU.add).then_inc(AB[l]["osel"], 1)
                    dve.wait_ge(AB[l]["osel"], 2 * n)
                    dve.wait_ge(AB[l]["ri"], n)
                    V.tensor_tensor(sel[l][0:ROWS, 0, 0:DIM].rearrange("p (h d) -> p h d", d=HD),
                                    sel[l][0:ROWS, 2, 0:DIM].rearrange("p (h d) -> p h d", d=HD),
                                    bc(ri[l][0:ROWS], 2, [ROWS, HEADS, HD]), ALU.mult).then_inc(AB[l]["on"], 1)

                def body(s, par, step):
                    a, b, r = live(step, 0), live(step, 1), live(step, 2)
                    rows = ROWS if step is None or step < STEPS - 1 else LAST_ROWS
                    nA, nB, nR = s + 1, s, s - 1
                    if b:
                        newton(0, nB)
                        V.scalar_tensor_tensor(hb[0:ROWS], h1[1 - par][0:ROWS], nrm[0][0:ROWS, 6:7], ln1w[0:ROWS],
                                               ALU.mult, ALU.mult).then_inc(hb_ready, 1)
                    if r:
                        newton(1, nR, rows)
                        if past(16 * s - 32 - 16 * par):
                            dve.wait_ge(scattered[par], 16 * s - 32 - 16 * par)
                        V.scalar_tensor_tensor(h2[par][0:rows], rr[par][0:rows], nrm[1][0:rows, 6:7], ln2w[0:rows],
                                               ALU.mult, ALU.mult).then_inc(h2_ready, 1)
                    if a:
                        dve.wait_ge(embedded, nA)
                        V.tensor_tensor(xa[0:ROWS], L[0][0:ROWS, 0:DIM], posb[0:ROWS], ALU.add).then_inc(x_ready, 1)
                        dve.wait_ge(AB[0]["qk"], nA)
                        V.tensor_tensor(
                            kx[0], S[0][:, 1, 0:256].rearrange("p (t r) -> p t r", t=KT)[:, :, 0:ROWS].unsqueeze(2)
                            .to_broadcast([128, KT, 4, ROWS]),
                            hm4.unsqueeze(1).unsqueeze(3).to_broadcast([128, KT, 4, ROWS]), ALU.mult)\
                         .then_inc(AB[0]["kx"], 2)
                    if b:
                        dve.wait_ge(rotated, nB)
                        V.tensor_tensor(qk_sin.rearrange("p (w j t) -> p w j t", w=2, j=2),
                                        S[1][:, 1].rearrange("p (w j t) -> p w j t", w=2, j=2),
                                        bc(sinT, 2, [128, 2, 2, 128]), ALU.mult).then_inc(by_sin, 1)
                        dve.wait_ge(by_sin, nB)
                        dve.wait_ge(by_cos, nB)
                        c4, s4 = (x.rearrange("p (j t) -> p j t", j=4)[:, :, 0:ROWS] for x in (qk_cos, qk_sin))
                        v = qm[1].rearrange("p t b r -> p t (b r)")
                        dg = bass.AP(tensor=v.tensor, offset=v.offset,
                                     ap=[v.ap[0], [IPG * ROWS, KT], [ROWS + SEQ, IPG], [1, SEQ]])
                        V.tensor_tensor(kk[:], c4[:, 2:4], s4[:, 2:4], ALU.add).then_inc(kk_ready, 1)
                        V.tensor_tensor(dg, c4[:, 0:2].rearrange("p t (b q) -> p t b q", b=IPG),
                                        s4[:, 0:2].rearrange("p t (b q) -> p t b q", b=IPG), ALU.add).then_inc(AB[1]["qm"], 1)
                    if a:
                        dve.wait_ge(AB[0]["s"], nA)
                        s4 = S[0][0:ROWS, :, 0:8 * SEQ].rearrange("p j (h k) -> p j h k", k=SEQ)
                        V.tensor_reduce(mx[0][0:ROWS].rearrange("p (j h) -> p j h", j=2), s4, AX.X, ALU.max)\
                         .then_inc(AB[0]["mx"], 1)
                        dve.wait_ge(AB[0]["mx"], nA)
                        V.tensor_tensor(z[0][0:ROWS].rearrange("p (j h) k -> p j h k", j=2), s4,
                                        mx[0][0:ROWS].rearrange("p (j h) -> p j h", j=2).unsqueeze(3)
                                        .to_broadcast([ROWS, 2, 8, SEQ]), ALU.subtract).then_inc(AB[0]["z"], 1)
                    if r:
                        dve.wait_ge(logits, alone(dve, nR))
                        V.max(top[0:rows], Rp[0:rows, 1, 0:EXPERTS]).then_inc(top_d, 1)
                        dve.wait_ge(top_d, alone(dve, nR))
                        V.max_index(topi[0:rows], top[0:rows], Rp[0:rows, 1, 0:EXPERTS]).then_inc(top_i, 1)
                        V.tensor_tensor(rt[0:rows, 0:1], top[0:rows, 1:2], top[0:rows, 0:1], ALU.subtract).then_inc(gap, 1)
                    if a:
                        dve.wait_ge(e1_done, nA)
                        V.tensor_tensor(z[0][0:ROWS, :, 0:3], z[0][0:ROWS, :, 0:3], bc(win[0:ROWS, 0:3], 1, [ROWS, HEADS, 3]),
                                        ALU.mult).then_inc(masked, 1)
                        V.tensor_tensor(z[0][0:ROWS, :, 32:36], z[0][0:ROWS, :, 32:36], bc(win[0:ROWS, 3:7], 1, [ROWS, HEADS, 4]),
                                        ALU.mult).then_inc(masked, 1)
                    if b:
                        dve.wait_ge(AB[1]["s"], nB)
                        V.tensor_tensor(z[1][0:ROWS].rearrange("p (j h) k -> p j h k", j=2),
                                        S[1][0:ROWS, :, 0:8 * SEQ].rearrange("p j (h k) -> p j h k", k=SEQ),
                                        cau[0:ROWS].unsqueeze(1).unsqueeze(1).to_broadcast([ROWS, 2, 8, SEQ]),
                                        ALU.add).then_inc(causal_done, 1)
                        dve.wait_ge(causal_done, nB)
                        V.tensor_reduce(mx[1][0:ROWS], z[1][0:ROWS], AX.X, ALU.max).then_inc(AB[1]["mx"], 1)
                    if a:
                        row_sum(0, nA)
                    if r:
                        dve.wait_ge(gap_exp, nR)
                        V.tensor_scalar(rt[0:rows, 2:3], rt[0:rows, 1:2], 1.0, None, ALU.add).then_inc(gate_sum, 1)
                        dve.wait_ge(top_i, nR)
                        V.tensor_copy(topf[0:rows], topi[0:rows, 0:2]).then_inc(index_float, 1)
                        dve.wait_ge(gate_sum, nR)
                        V.reciprocal(rt[0:rows, 3:4], rt[0:rows, 2:3]).then_inc(gate_inv, 1)
                        dve.wait_ge(index_float, nR)
                        for k in range(2):
                            V.tensor_scalar(oh[0:rows, k], eio[0:rows], topf[0:rows, k:k + 1], None, ALU.is_equal)\
                             .then_inc(one_hot, 1)
                        dve.wait_ge(one_hot, 2 * nR)
                        V.tensor_tensor(cnt[0:rows], oh[0:rows, 0], oh[0:rows, 1], ALU.add).then_inc(count_float, 1)
                        g = row_of(s - 2, step)
                        dve.wait_ge(gate_inv, nR)
                        V.tensor_copy(w_all[0:rows, g, 0], rt[0:rows, 3:4])
                        V.tensor_tensor(w_all[0:rows, g, 1], rt[0:rows, 3:4], rt[0:rows, 1:2], ALU.mult)\
                         .then_inc(gates_kept, 1)
                        dve.wait_ge(count_float, nR)
                        V.tensor_copy(cntb[0:rows], cnt[0:rows]).then_inc(counted, 1)
                    if b:
                        row_sum(1, nB)
                    if a:
                        select(0, nA)
                    if r:
                        dve.wait_ge(ranked, nR)
                        V.tensor_tensor(place[0:rows], Rp[0:rows, 0, 256:256 + EXPERTS], rb[0:rows], ALU.add)\
                         .then_inc(placed, 1)
                        V.tensor_tensor(tot[0:rows], tot[0:rows], cnt[0:rows], ALU.add).then_inc(total_float, 1)
                        dve.wait_ge(total_float, nR)
                        V.tensor_copy(totb[0:rows], tot[0:rows]).then_inc(totalled, 1)
                        dve.wait_ge(placed, nR)
                        V.tensor_tensor(hit[0:rows], oh[0:rows], bc(place[0:rows], 1, [rows, 2, EXPERTS]), ALU.mult)\
                         .then_inc(hits, 1)
                        dve.wait_ge(hits, nR)
                        V.tensor_reduce(slotf[0:rows], hit[0:rows], AX.X, ALU.add).then_inc(slot_sum, 1)
                        dve.wait_ge(slot_sum, nR)
                        V.tensor_copy(slot[par][0:rows], slotf[0:rows]).then_inc(slots_ready, 1)
                        V.tensor_copy(exp_all[0:rows, g].rearrange("p o k -> p (o k)"), topf[0:rows])
                        V.tensor_copy(place_all[0:rows, g].rearrange("p o k -> p (o k)"), slotf[0:rows])\
                         .then_inc(slots_kept, 1)
                    if b:
                        select(1, nB)
                    if a:
                        dve.wait_ge(AB[0]["y"], nA)
                        V.tensor_tensor(xa[0:ROWS], L[0][0:ROWS, 0:DIM], xa[0:ROWS], ALU.add).then_inc(r_res, 1)
                        dve.wait_ge(r_res, nA)
                        V.bn_stats(st[0:ROWS], xa[0:ROWS]).then_inc(r_stat, 1)
                        dve.wait_ge(r_stat, alone(dve, nA))
                        V.bn_aggr(mv[0:ROWS], st[0:ROWS]).then_inc(r_aggr, 1)
                    if b:
                        dve.wait_ge(AB[1]["y"], nB)
                        V.tensor_tensor(rr[1 - par][0:ROWS], L[1][0:ROWS, 0:DIM], h1[1 - par][0:ROWS], ALU.add).then_inc(rr_ready, 1)
                        dve.wait_ge(rr_ready, nB)
                        if past(8 * s - 16 + 8 * par):
                            dve.wait_ge(res_stored[1 - par], 8 * s - 16 + 8 * par)
                        V.tensor_tensor(res[1 - par][0:ROWS], rr[1 - par][0:ROWS], h1[1 - par][0:ROWS], ALU.add).then_inc(res_ready, 1)
                    if a:
                        dve.wait_ge(r_aggr, nA)
                        newton(2, nA)
                        V.tensor_scalar(h1[par][0:ROWS], xa[0:ROWS], mv[0:ROWS, 0:1], nrm[2][0:ROWS, 6:7],
                                        ALU.subtract, ALU.mult).then_inc(h1_ready, 1)

                steps(dve, body)

            @block.tensor
            def _(pe):
                pe.wait_ge(consts_loaded, 16 * len(consts))
                pe.wait_ge(setup_pool, 9)
                pe.wait_ge(setup_dve, 3)

                def transpose_x(i, src, ready, n, done, rows=ROWS):
                    ps = L[i] if i < 2 else Rp[:, 0]
                    pe.wait_ge(ready, n)
                    for t in range(KT):
                        last = T.transpose(ps[:, t * rows:(t + 1) * rows], src[0:rows, t * 128:(t + 1) * 128],
                                           ident[0:rows, 0:rows])
                    last.then_inc(done, 1)

                def project(l, n):
                    pe.wait_ge(AB[l]["xt"], n)
                    for j in range(4):
                        o = S[0][:, j // 2, (j % 2) * 128:(j % 2 + 1) * 128] if l == 0 else S[1][:, 0, j * 128:(j + 1) * 128]
                        for t in range(KT):
                            last = T.matmul(o, wqk[l][:, t, j * 128:(j + 1) * 128], xt[l][:, t], start=t == 0, stop=t == KT - 1)
                    last.then_inc(AB[l]["qk"], 1)
                    for t in range(KT):
                        last = T.matmul(L[l][0:ROWS, 0:DIM], xt[l][:, t, 0:ROWS], wv[l][:, t], start=t == 0, stop=t == KT - 1)
                    last.then_inc(AB[l]["v"], 1)

                def scores(l, n):
                    pe.wait_ge(AB[l]["qm"], n)
                    pe.wait_ge(AB[l]["kx"], 2 * n)
                    for t in range(KT):
                        for r in range(2):
                            for b in range(IPG):
                                last = T.matmul(S[l][0:ROWS, r, t * 144:(t + 1) * 144], qm[l][64 * r:64 * r + 64, t, b],
                                                kx[l][64 * r:64 * r + 64, t, :, SEQ * b:SEQ * (b + 1)],
                                                start=b == 0, stop=b == IPG - 1)
                    last.then_inc(AB[l]["s"], 1)

                def transpose_p(l, n):
                    pe.wait_ge(AB[l]["e"], n)
                    for c in range(CHUNKS):
                        last = T.transpose(S[l][0:CH, c // 3, (c % 3) * ROWS:(c % 3 + 1) * ROWS],
                                           pr[l][0:ROWS, c * CH:(c + 1) * CH], ident[0:ROWS, 0:ROWS])
                    last.then_inc(AB[l]["p_t"], 1)

                def values(l, n):
                    pe.wait_ge(AB[l]["pt"], n)
                    pe.wait_ge(AB[l]["vx"], n)
                    for c in range(CHUNKS):
                        last = T.matmul(S[l][0:ROWS, c // 3, 0:432].rearrange("p (b c d) -> p b c d", b=3, c=3)[:, :, c % 3], pt[l][0:CH, c],
                                        vx[l][0:CH, :, 48 * c:48 * (c + 1)], start=True, stop=True)
                    last.then_inc(AB[l]["o"], 1)

                def transpose_o(l, n):
                    pe.wait_ge(AB[l]["on"], n)
                    for t in range(KT):
                        last = T.transpose(L[l][:, t * ROWS:(t + 1) * ROWS], sel[l][0:ROWS, 0, t * 128:(t + 1) * 128],
                                           ident[0:ROWS, 0:ROWS])
                    last.then_inc(AB[l]["o_t"], 1)

                def project_out(l, n):
                    pe.wait_ge(AB[l]["ot"], n)
                    for t in range(KT):
                        last = T.matmul(L[l][0:ROWS, 0:DIM], ot[l][:, t], wo[l][:, t], start=t == 0, stop=t == KT - 1)
                    last.then_inc(AB[l]["y"], 1)

                def body(s, par, step):
                    a, b, r = live(step, 0), live(step, 1), live(step, 2)
                    rows = ROWS if step is None or step < STEPS - 1 else LAST_ROWS
                    nA, nB, nR = s + 1, s, s - 1
                    if a:
                        pe.wait_ge(pat_loaded[par], 8 * s + 16 - 8 * par)
                        if past(s):
                            pe.wait_ge(r_res, s)
                        for t in range(PT_TILES):
                            last = T.matmul(L[0][0:ROWS, 0:DIM], pat[par][:, t], tokw[:, t], start=t == 0, stop=t == PT_TILES - 1)
                        last.then_inc(embedded, 1)
                    if b:
                        transpose_x(1, hb, hb_ready, nB, AB[1]["x_t"])
                    if a:
                        transpose_x(0, xa, x_ready, nA, AB[0]["x_t"])
                    if b:
                        project(1, nB)
                    if a:
                        project(0, nA)
                    if b:
                        pe.wait_ge(qk_copied, nB)
                        T.matmul(S[1][:, 1], rotm, qk_sb, start=True, stop=True).then_inc(rotated, 1)
                    if r:
                        transpose_x(2, h2[par], h2_ready, nR, h2_t, rows)
                    if a:
                        scores(0, nA)
                    if r:
                        pe.wait_ge(h2t, nR)
                        for t in range(KT):
                            last = T.matmul(Rp[0:rows, 1, 0:EXPERTS], xt[2][:, t, 0:rows], routw[:, t], start=t == 0, stop=t == KT - 1)
                        last.then_inc(logits, 1)
                    if b:
                        scores(1, nB)
                    if a:
                        transpose_p(0, nA)
                    if b:
                        transpose_p(1, nB)
                    if a:
                        values(0, nA)
                    if r:
                        pe.wait_ge(counted, nR)
                        if past(nR - 1):
                            pe.wait_ge(totalled, nR - 1)
                        T.matmul(Rp[0:rows, 0, 256:256 + EXPERTS], lowb[0:rows, 0:rows], cntb[0:rows], start=True, stop=False)
                        T.matmul(Rp[0:rows, 0, 256:256 + EXPERTS], oneb[0:ROWS, 0:rows], totb[0:ROWS], start=False, stop=True)\
                         .then_inc(ranked, 1)
                    if b:
                        values(1, nB)
                    if a:
                        transpose_o(0, nA)
                    if b:
                        transpose_o(1, nB)
                    if a:
                        project_out(0, nA)
                    if b:
                        project_out(1, nB)

                steps(pe, body)

        late = range(EARLY, EXPERTS)
        HEAD = (0, HALF[0])
        N_PLAN = 12

        def pair(eng, body, first, last, start):
            for j in range(first, start):
                body(j, j % 2, j)
            with eng.Fori(start, last - 1, 2) as j:
                body(j, start % 2, None)
                body(j + 1, 1 - start % 2, None)

        with nc.Block() as block:
            @block.sync
            def _(sp):
                for e in late:
                    sp.dma_start(weights[:, e * EXPERT_COLS:(e + 1) * EXPERT_COLS], expert_w[:, e])\
                      .then_inc(expert_loaded[e], 16)
                sp.wait_ge(plan_ready, 1)
                sp.wait_ge(zeroed, 16 * (EXPERTS + SPARE_TILES))
                for i in range(2):
                    sp.wait_ge(scattered[i], 16 * GROUPS)

                def load(j, par, at):
                    row = sp.value_load(row_tab[0:1, row_of(j, at)], min_val=0, max_val=XS_ROWS - TILE)
                    sp.dma_start(xg[par][:], xs[bass.ds(row, TILE), :]).then_inc(x_loaded[par], 16)

                def body(j, par, at):
                    if at is None or at + 1 < TILES:
                        if past(j):
                            sp.wait_ge(mt, alone(sp, j))
                        load(j + 1, 1 - par, None if at is None else at + 1)
                    if at is None or at > 0:
                        store(j - 1, 1 - par, at)

                def store(j, par, at):
                    sp.wait_ge(y_copied, j + 1)
                    sp.dma_start(ys[row_of(j * TILE, at, TILE), :], yb[par][:]).then_inc(y_stored[par], 16)

                load(0, 0, 0)
                pair(sp, body, 0, TILES - 1, 2)
                body(TILES - 1, (TILES - 1) % 2, TILES - 1)
                store(TILES - 1, (TILES - 1) % 2, 0)

            @block.gpsimd
            def _(pool):
                P.memset(zero[:], 0.0).then_inc(zero_ready, 1)
                pool.wait_ge(zero_ready, 1)
                for i in range(SPARE_TILES):
                    r0 = EXPERTS * REGION + i * TILE
                    pool.dma_start(xs[r0:r0 + TILE, :], zero[:]).then_inc(zeroed, 16)
                pool.wait_ge(tail_slots, 1)
                for e in range(EXPERTS):
                    P.indirect_dma_start(xs, bass.IndirectOffsetOnAxis(tails[:, e:e + 1], 0), zero[:], None)\
                     .then_inc(zeroed, 16)
                for e in range(EXPERTS):
                    pool.wait_ge(expert_loaded[e], 16)
                    pool.sem_inc(experts_ready, 1)

            @block.scalar
            def _(act):
                def copy_x(j, n):
                    act.wait_ge(mt, n)
                    A.activation(xm[j][:], Rp[:, 0, 0:DIM], ACT.Copy).then_inc(mxt, 1)

                def silu(h, n):
                    act.wait_ge(gu[h], n)
                    A.activation(sgb[h][:], S[h][:, 0, 0:HALF[h]], ACT.Silu).then_inc(sg[h], 1)

                def copy_y(par, n):
                    act.wait_ge(y_ready, n)
                    if past(8 * n - 8 - 8 * par):
                        act.wait_ge(y_stored[par], 8 * n - 8 - 8 * par)
                    A.activation(yb[par][:], Rp[:, 1, 0:DIM], ACT.Copy).then_inc(y_copied, 1)

                def body(j, par, at):
                    silu(0, j + 1)
                    if at is None or at + 1 < TILES:
                        copy_x(1 - par, j + 2)
                    silu(1, j + 1)
                    if at is None or at > 0:
                        copy_y(1 - par, j)

                copy_x(0, 1)
                pair(act, body, 0, TILES - 1, 2)
                body(TILES - 1, (TILES - 1) % 2, TILES - 1)
                copy_y((TILES - 1) % 2, TILES)

            @block.vector
            def _(dve):
                done = [0]

                def step(ins):
                    done[0] += 1
                    ins.then_inc(plan, 1)
                    dve.wait_ge(plan, done[0])

                dve.wait_ge(counts_ready, 1)
                n_e = Rp[:, 1, 0:EXPERTS]
                step(V.tensor_tensor(tailf[:], n_e, rb[:], ALU.add))
                step(V.tensor_scalar(tailf[:], tailf[:], pid[:], None, ALU.add))
                V.tensor_copy(tails[:], tailf[:]).then_inc(tail_slots, 1)
                eq, ee = [128, EXPERTS, TOKENS // TILE], [128, EXPERTS, EXPERTS]
                step(V.tensor_tensor(over[:], bc(n_e, 2, eq), bc(thr[:], 1, eq), ALU.is_gt))
                step(V.tensor_reduce(nt[:], over[:], AX.X, ALU.add))
                step(V.tensor_tensor(pre[:], bc(nt[:], 1, ee), bef[:], ALU.mult))
                step(V.tensor_reduce(cum[:], pre[:], AX.X, ALU.add))
                je = [1, TILES, EXPERTS]
                step(V.tensor_tensor(ge, bc(tid[:], 2, je), bc(cum[0:1], 1, je), ALU.is_ge))
                step(V.tensor_reduce(te[:], ge, AX.X, ALU.add))
                step(V.tensor_tensor(gt, ge, bc(nt[0:1], 1, je), ALU.mult))
                step(V.tensor_reduce(tb[:], gt, AX.X, ALU.add))
                step(V.tensor_tensor(tl[:], tid[:], tb[:], ALU.subtract))
                step(V.tensor_scalar(tl[:], tl[:], float(TILE), None, ALU.mult))
                step(V.scalar_tensor_tensor(tr[:], te[:], float(REGION), tl[:], ALU.mult, ALU.add))
                step(V.tensor_copy(row_tab[:], tr[:]))
                step(V.tensor_scalar(tw[:], te[:], float(EXPERTS - 1), float(EXPERT_COLS), ALU.min, ALU.mult))
                step(V.tensor_copy(col_tab[:], tw[:]))
                step(V.tensor_scalar(tw[:], te[:], float(EXPERTS - 1), 1.0, ALU.min, ALU.add))
                V.tensor_copy(need_tab[:], tw[:]).then_inc(plan_ready, 1)
                ke = [128, 2 * GROUPS, EXPERTS]
                step(V.tensor_tensor(shift[:], cum[:], nt[:], ALU.subtract))
                step(V.scalar_tensor_tensor(shift[:], shift[:], float(TILE), rb[:], ALU.mult, ALU.subtract))
                step(V.tensor_tensor(own, bc(exp_all[:].rearrange("p g k -> p (g k)"), 2, ke), bc(eio[:], 1, ke), ALU.is_equal))
                step(V.tensor_tensor(own, own, bc(shift[:], 1, ke), ALU.mult))
                step(V.tensor_reduce(moved[:], own, AX.X, ALU.add))
                step(V.tensor_tensor(moved[:], moved[:], place_all[:].rearrange("p g k -> p (g k)"), ALU.add))
                step(V.tensor_copy(slot_all[:].rearrange("p g k -> p (g k)"), moved[:]))

                def times_up(h, n):
                    dve.wait_ge(sg[h], n)
                    V.tensor_tensor(acb[h][:], sgb[h][:], S[h][:, 1, 0:HALF[h]], ALU.mult).then_inc(ac[h], 1)

                def copy_at(h, n):
                    dve.wait_ge(a_t[h], n)
                    V.tensor_copy(atb[h][:].rearrange("p a b -> p (a b)")[:, 0:HALF[h]], L[h][:, 0:HALF[h]]).then_inc(at[h], 1)

                def body(j, par, at_):
                    if at_ is None or at_ > 0:
                        copy_at(1, j)
                    times_up(0, j + 1)
                    copy_at(0, j + 1)
                    times_up(1, j + 1)

                pair(dve, body, 0, TILES - 1, 2)
                body(TILES - 1, (TILES - 1) % 2, TILES - 1)
                copy_at(1, TILES)

            @block.tensor
            def _(pe):
                T.matmul(Rp[:, 1, 0:EXPERTS], oneb[0:ROWS, :], totb[0:ROWS], start=True, stop=True).then_inc(counts_ready, 1)

                def transpose_tile(par, n):
                    pe.wait_ge(x_loaded[par], 8 * n + 8 - 8 * par)
                    for t in range(KT):
                        last = T.transpose(Rp[:, 0, t * TILE:(t + 1) * TILE], xg[par][:, t * 128:(t + 1) * 128], ident[:])
                    last.then_inc(mt, 1)

                def gate_up(par, h, n, col):
                    pe.wait_ge(mxt, n)
                    if past(n - 1):
                        pe.wait_ge(ac[h], n - 1)
                    for u in range(2):
                        for t in range(KT):
                            c0 = (2 * t + u) * FF + HEAD[h]
                            last = T.matmul(S[h][:, u, 0:HALF[h]], xm[par][:, t * 128:(t + 1) * 128],
                                            weights[:, bass.ds(col + c0, HALF[h])], start=t == 0, stop=t == KT - 1)
                    last.then_inc(gu[h], 1)

                def transpose_act(h, n):
                    pe.wait_ge(ac[h], n)
                    for c in range(HALF[h] // 128):
                        last = T.transpose(L[h][:, c * 128:(c + 1) * 128], acb[h][:, c * 128:(c + 1) * 128], ident[:])
                    last.then_inc(a_t[h], 1)

                def down(h, n, col):
                    pe.wait_ge(at[h], n)
                    if h == 0:
                        if past(n - 1):
                            pe.wait_ge(y_copied, n - 1)
                    a = atb[h][:].rearrange("p a b -> p (a b)")
                    for c in range(HALF[h] // 128):
                        c0 = KT * 2 * FF + (HEAD[h] // 128 + c) * DIM
                        last = T.matmul(Rp[:, 1, 0:DIM], a[:, c * 128:(c + 1) * 128], weights[:, bass.ds(col + c0, DIM)],
                                        start=h == 0 and c == 0, stop=h == 1 and c == HALF[1] // 128 - 1)
                    if h == 1:
                        last.then_inc(y_ready, 1)

                def body(j, par, at_):
                    col = pe.value_load(col_tab[0:1, row_of(j, at_)], min_val=0, max_val=(EXPERTS - 1) * EXPERT_COLS)
                    need = pe.value_load(need_tab[0:1, row_of(j, at_)], min_val=1, max_val=EXPERTS)
                    pe.wait_ge(experts_ready, need)
                    gate_up(par, 0, j + 1, col)
                    if at_ is None or at_ > 0:
                        before_ = pe.value_load(col_tab[0:1, row_of(j - 1, at_)],
                                                min_val=0, max_val=(EXPERTS - 1) * EXPERT_COLS)
                        transpose_act(1, j)
                        down(0, j, before_)
                    if at_ is None or at_ + 1 < TILES:
                        transpose_tile(1 - par, j + 2)
                    gate_up(par, 1, j + 1, col)
                    transpose_act(0, j + 1)
                    if at_ is None or at_ > 0:
                        down(1, j, before_)

                pe.wait_ge(plan_ready, 1)
                transpose_tile(0, 1)
                pair(pe, body, 0, TILES - 1, 2)
                body(TILES - 1, (TILES - 1) % 2, TILES - 1)
                col = pe.value_load(col_tab[0:1, TILES - 1:TILES], min_val=0, max_val=(EXPERTS - 1) * EXPERT_COLS)
                transpose_act(1, TILES)
                down(0, TILES, col)
                down(1, TILES, col)

        def groups(eng, body):
            for g in range(2):
                body(g, g % 2, g)
            with eng.Fori(2, GROUPS - 3, 2) as g:
                body(g, 0, None)
                body(g + 1, 1, None)
            for g in range(GROUPS - 2, GROUPS):
                body(g, g % 2, g)

        def group_rows(at_):
            return LAST_ROWS if at_ == GROUPS - 1 else ROWS

        with nc.Block() as block:
            @block.gpsimd
            def _(pool):
                for i in range(2):
                    pool.wait_ge(y_stored[i], 16 * (TILES // 2 + (TILES % 2) * (1 - i)))

                def body(g, par, at_):
                    rows = group_rows(at_)
                    if past(2 * g - 2):
                        pool.wait_ge(summed, 2 * g - 2)
                    P.tensor_copy(cidx[par][0:rows], slot_all[0:rows, row_of(g, at_)].rearrange("p o k -> p (o k)"))\
                     .then_inc(idx_ready, 1)
                    pool.wait_ge(idx_ready, alone(pool, g + 1))
                    for k in range(2):
                        P.indirect_dma_start(yg[k][par][0:rows], None, ys,
                                             bass.IndirectOffsetOnAxis(cidx[par][0:rows, k:k + 1], 0))\
                         .then_inc(gathered[par], 16)

                groups(pool, body)

            @block.sync
            def _(sp):
                for i in range(2):
                    sp.wait_ge(res_stored[i], 8 * GROUPS)
                    sp.wait_ge(y_stored[i], 16 * (TILES // 2 + (TILES % 2) * (1 - i)))

                def load(g, par, at_):
                    rows = group_rows(at_)
                    sp.dma_start(bt[par][0:rows], residual[row_of(g * ROWS, at_, rows), :]).then_inc(base_loaded[par], 16)

                def body(g, par, at_):
                    rows = group_rows(at_)
                    if at_ is None or at_ + 1 < GROUPS:
                        if past(2 * g):
                            sp.wait_ge(summed, 2 * g)
                        load(g + 1, 1 - par, None if at_ is None else at_ + 1)
                    sp.wait_ge(out_ready, g + 1)
                    sp.dma_start(out[row_of(g * ROWS, at_, rows), :], ob[par][0:rows]).then_inc(out_stored[par], 16)

                load(0, 0, 0)
                groups(sp, body)
                for i in range(2):
                    sp.wait_ge(out_stored[i], 8 * GROUPS)

            @block.scalar
            def _(act):
                def body(g, par, at_):
                    rows = group_rows(at_)
                    n = g + 1
                    act.wait_ge(r_aggr, GROUPS + n)
                    q = nrm[2]
                    A.activation(q[0:rows, 1:2], mv[0:rows, 1:2], ACT.Ln, bias=eps[0:rows, 0:1]).then_inc(n_ln[2], 1)
                    act.wait_ge(n_ln[2], GROUPS + n)
                    A.activation(q[0:rows, 2:3], q[0:rows, 1:2], ACT.Exp, scale=-0.5).then_inc(n_y0[2], 1)

                A.preload_act_table_set("natural_log_exp_and_others")
                groups(act, body)

            @block.vector
            def _(dve):
                def body(g, par, at_):
                    rows = group_rows(at_)
                    n = g + 1
                    gs = row_of(g, at_)
                    dve.wait_ge(base_loaded[par], 8 * g + 16 - 8 * par)
                    dve.wait_ge(gathered[par], 16 * g + 32 - 16 * par)
                    for k in range(2):
                        if k:
                            dve.wait_ge(summed, 2 * n - 1)
                        V.scalar_tensor_tensor(acc[par][0:rows], yg[k][par][0:rows],
                                               w_all[0:rows, gs, k:k + 1].rearrange("p o k -> p (o k)"),
                                               (acc if k else bt)[par][0:rows], ALU.mult, ALU.add).then_inc(summed, 1)
                    dve.wait_ge(summed, 2 * n)
                    V.bn_stats(st[0:rows], acc[par][0:rows]).then_inc(r_stat, 1)
                    dve.wait_ge(r_stat, alone(dve, GROUPS + n))
                    V.bn_aggr(mv[0:rows], st[0:rows]).then_inc(r_aggr, 1)
                    dve.wait_ge(r_aggr, GROUPS + n)
                    q, m = nrm[2][0:rows], 4 * (GROUPS + n)
                    V.tensor_scalar(q[:, 3:4], mv[0:rows, 1:2], LN_EPS, None, ALU.add).then_inc(n_dve[2], 1)
                    dve.wait_ge(n_y0[2], GROUPS + n)
                    dve.wait_ge(n_dve[2], m - 3)
                    V.scalar_tensor_tensor(q[:, 4:5], q[:, 2:3], q[:, 2:3], q[:, 3:4], ALU.mult, ALU.mult).then_inc(n_dve[2], 1)
                    dve.wait_ge(n_dve[2], m - 2)
                    V.tensor_scalar(q[:, 5:6], q[:, 4:5], -0.5, 1.5, ALU.mult, ALU.add).then_inc(n_dve[2], 1)
                    dve.wait_ge(n_dve[2], m - 1)
                    V.tensor_tensor(q[:, 6:7], q[:, 5:6], q[:, 2:3], ALU.mult).then_inc(n_dve[2], 1)
                    dve.wait_ge(n_dve[2], m)
                    if past(8 * g - 8 * par):
                        dve.wait_ge(out_stored[par], 8 * g - 8 * par)
                    V.tensor_scalar(ob[par][0:rows], acc[par][0:rows], mv[0:rows, 0:1], q[:, 6:7],
                                    ALU.subtract, ALU.mult).then_inc(out_ready, 1)

                groups(dve, body)


def kernel(**inputs):
    import numpy as np
    import concourse.bacc as bacc
    from concourse.bass_utils import run_bass_kernel_spmd

    given = {k: np.asarray(v) for k, v in inputs.items()}
    rows = lambda v: np.ascontiguousarray(np.broadcast_to(v, (ROWS, v.shape[-1])))
    tiles = lambda w: np.ascontiguousarray(w.reshape(-1, 128, w.shape[1]).transpose(1, 0, 2))

    x, p = given["x"], 16
    x = x.reshape(IMAGES, 3, 6, p, 6, p).transpose(1, 3, 5, 0, 2, 4).reshape(PATCH_DIM, TOKENS)
    fill = GROUPS * ROWS - TOKENS
    x = np.concatenate([x, x[:, :fill]], 1)
    patches = np.ascontiguousarray(x.reshape(PT_TILES, 128, GROUPS, ROWS).transpose(1, 2, 0, 3)
                                   .reshape(128, GROUPS, PT_TILES * ROWS))

    rep = lambda w: np.repeat(w.reshape(DIM, 8, 1, HD), 2, 2).reshape(DIM, DIM)
    slots = np.arange(HEADS).reshape(2, 2, 4).transpose(1, 0, 2).reshape(-1)
    by_slot = (slots[:, None] * HD + np.arange(HD)).reshape(-1)
    bq, bk, bv = given["L0_ffn_wq"], rep(given["L0_ffn_wk"]), rep(given["L0_ffn_wv"])
    gate, up, down = (given[f"L0_ffn_w_{n}"] for n in ("gate", "up", "down"))
    gu = np.stack([gate, up], 2).reshape(EXPERTS, KT, 128, 2 * FF).transpose(2, 0, 1, 3).reshape(128, EXPERTS, -1)
    dn = down.reshape(EXPERTS, DOWN_TILES, 128, DIM).transpose(2, 0, 1, 3).reshape(128, EXPERTS, -1)

    f = np.float32
    row, ch, q = np.arange(ROWS), np.arange(128), np.arange(ROWS) % SEQ
    headmask4 = (ch[:, None] % 64 // HD == np.arange(4)).astype(f)
    headmask3 = (row[:, None] // SEQ == np.arange(HEADS) % 3).astype(f)
    imagemask = (row[:, None] // SEQ == np.arange(IPG)).astype(f)
    d = np.arange(SEQ)[None] - q[:, None]
    window = ((d <= 31) & (d >= -32)).astype(f)[:, [0, 1, 2, 32, 33, 34, 35]]
    causal = np.where(d <= 0, f(0), f(-3e38)).astype(f)
    inv = (f(1) / f(10000.0) ** (np.arange(0, HD, 2, dtype=f) / f(HD))).astype(f)
    ang = (np.arange(128) % SEQ).astype(f)[None] * inv[ch % 8][:, None]
    rotate = np.zeros((128, 128), f)
    for m in range(128):
        rotate[m + 8 if m % HD < 8 else m - 8, m] = -1 if m % HD < 8 else 1
    scaled = lambda t: np.stack([t * f(HD ** -0.5), t], 1)
    e = np.arange(EXPERTS)
    args = dict(
        patches=patches, tok_w=tiles(given["L0_tok_W"].T), tok_b=rows(given["L0_tok_b"]),
        pos=np.ascontiguousarray(np.tile(given["L0_tok_pos_embd"][0], (IPG, 1))),
        a_wqk=tiles(np.concatenate([given["L0_attn_Wq"], given["L0_attn_Wk"]], 1)),
        a_wv=tiles(given["L0_attn_Wv"][:, by_slot]), a_wo=tiles(given["L0_attn_Wo"][by_slot]),
        b_wqk=tiles(np.concatenate([bq, bk], 1)), b_wv=tiles(bv[:, by_slot]), b_wo=tiles(given["L0_ffn_wo"][by_slot]),
        ln1=rows(given["L0_ffn_ln1_w"]), ln2=rows(given["L0_ffn_ln2_w"]), router=tiles(given["L0_ffn_router_w"]),
        expert_w=np.ascontiguousarray(np.concatenate([gu, dn], 2)),
        headmask4=headmask4, headmask3=headmask3, imagemask=imagemask, window=window, causal=causal,
        rope_cos=scaled(np.cos(ang).astype(f)), rope_sin=scaled(np.sin(ang).astype(f)), rotate=rotate,
        identity=np.eye(128, dtype=f), lower=(row[:, None] < row[None]).astype(f),
        expert_iota=np.tile(e.astype(f), (128, 1)), region_base=np.tile((e * REGION).astype(f), (128, 1)),
        thresholds=np.tile((np.arange(TOKENS // TILE) * TILE).astype(f), (128, 1)), tile_ids=np.arange(TILES, dtype=f)[None],
        before=np.tile((e[None] <= e[:, None]).astype(f), (128, 1, 1)), partition_ids=np.arange(128, dtype=f)[:, None],
    )
    nc = bacc.Bacc("TRN2", target_bir_lowering=False, num_devices=1)
    aps = {n: nc.dram_tensor(f"in_{n}", a.shape, mybir.dt.from_np(a.dtype), kind="ExternalInput").ap()
           for n, a in args.items()}
    out = nc.dram_tensor("out", (TOKENS, DIM), mybir.dt.float32, kind="ExternalOutput").ap()
    program(nc, out=out, **aps)
    r = run_bass_kernel_spmd(nc, [{f"in_{n}": a for n, a in args.items()}], core_ids=[0])
    return r.results[0]["out"].reshape(IMAGES, SEQ, DIM)
```

```python
import concourse.bass as bass
from concourse import mybir
from contextlib import ExitStack

IMAGES, SEQ, DIM, HEADS, HD = 64, 36, 256, 16, 16
PATCH_DIM = 768
FF, EXPERTS = 896, 8
IPG = 3
ROWS = IPG * SEQ
GROUPS = -(-IMAGES // IPG)
LAST_ROWS = (IMAGES - IPG * (GROUPS - 1)) * SEQ
TOKENS = IMAGES * SEQ
KT = DIM // 128
PT_TILES = PATCH_DIM // 128
TILE = 128
TILES = (2 * TOKENS + EXPERTS * (TILE - 1)) // TILE
REGION = TOKENS + TILE
SPARE_TILES = TILES - 2 * TOKENS // TILE
XS_ROWS = EXPERTS * REGION + SPARE_TILES * TILE
CHUNKS = 6
CH = 3 * SEQ
DOWN_TILES = FF // 128
EXPERT_COLS = KT * 2 * FF + DOWN_TILES * DIM
HALF = (512, FF - 512)
RING = 3
RAW = 2
WORK_COLS = 24576
LN_EPS, RMS_EPS = 1e-5, 1e-6
PEEL = 6
STEPS = GROUPS + 4
LOOP_END = GROUPS - 2


def program(nc, patches, tok_w, tok_b, pos, a_wqk, a_wv, a_wo, b_wqk, b_wv, b_wo, ln1, ln2, router,
            expert_w, headmask4, headmask3, imagemask, window, causal, rope_cos, rope_sin, rotate,
            identity, lower, expert_iota, region_base, thresholds, tile_ids, before, partition_ids, col_step,
            out):
    f32, bf16, u32 = mybir.dt.float32, mybir.dt.bfloat16, mybir.dt.uint32
    f32r = mybir.dt.float32r
    ALU, ACT, AX = mybir.AluOpType, mybir.ActivationFunctionType, mybir.AxisListType
    V, P, T, A = nc.vector, nc.gpsimd, nc.tensor, nc.scalar
    xs = nc.dram_tensor("expert_rows_in", [XS_ROWS, DIM], f32, kind="Internal").ap()
    ys = nc.dram_tensor("expert_rows_out", [TILES * TILE, DIM], f32, kind="Internal").ap()
    residual = nc.dram_tensor("residual", [GROUPS * ROWS, DIM], f32, kind="Internal").ap()

    ctx = ExitStack()
    with ctx:
        def sb(name, shape, dt=f32):
            return ctx.enter_context(nc.sbuf_tensor(name, shape, dt))

        def sem(name):
            return ctx.enter_context(nc.semaphore(name))

        xa = [sb(f"xa_{i}", [128, DIM]) for i in range(2)]
        hb, h1, rr = sb("hb", [128, DIM]), sb("h1", [128, DIM]), sb("rr", [128, DIM])
        hc = [sb(f"hc_{i}", [128, DIM]) for i in range(2)]
        h2 = [sb(f"h2_{i}", [128, DIM]) for i in range(2)]
        res = [sb(f"res_{i}", [128, DIM]) for i in range(2)]
        kk = sb("kk", [128, KT, ROWS])
        junk = sb("junk", [128, DIM])
        ident = sb("ident", [128, 128])
        low, eio, rb = sb("low", [128, ROWS]), sb("eio", [128, EXPERTS]), sb("rb", [128, EXPERTS])
        lowb, oneb = sb("lowb", [128, ROWS], bf16), sb("oneb", [128, 128], bf16)
        mx, sm, ri = ([sb(f"{n}{i}", [128, HEADS]) for i in range(2)] for n in ("mx", "sm", "ri"))
        w_all = sb("w_all", [128, GROUPS, 2])
        place_all = sb("place_all", [128, GROUPS, 2])
        exp_all = sb("exp_all", [128, GROUPS, 2])
        slot_all = sb("slot_all", [128, GROUPS, 2], u32)
        eps = sb("eps", [128, 2])
        nil = sb("nil", [128, 1])
        st = sb("st", [128, 6])
        mv = sb("mv", [128, 2])
        nrm = [sb(f"nrm{i}", [128, 8]) for i in range(3)]
        top, topi = sb("top", [128, 8]), sb("topi", [128, 8], u32)
        topf = sb("topf", [128, 2])
        rt = sb("rt", [128, 8])
        oh = sb("oh", [128, 2, EXPERTS])
        cnt, cntb = sb("cnt", [128, EXPERTS]), sb("cntb", [128, EXPERTS], bf16)
        tot, totb = sb("tot", [128, EXPERTS]), sb("totb", [128, EXPERTS], bf16)
        place, hit = sb("place", [128, EXPERTS]), sb("hit", [128, 2, EXPERTS])
        slotf, slot = sb("slotf", [128, 2]), [sb(f"slot{i}", [128, 2], u32) for i in range(2)]

        raw = [sb(f"raw{i}", [128, EXPERT_COLS]) for i in range(RAW)]

        X, Y = (ctx.enter_context(nc.psum_tensor(n, [128, 2, 512], f32)) for n in ("X", "Y"))
        Lb = [ctx.enter_context(nc.psum_tensor(f"L{i}", [128, 512], f32)) for i in range(4)]
        S, L = [X, Y], Lb[0:2]

        names = ("x_t", "xt", "qk", "v", "qm", "kx", "vs", "vrep", "vx", "s", "mx", "z", "e", "sm", "ri",
                 "p_t", "pt", "o", "o0", "osel", "on", "o_t", "ot", "y")
        AB = [{n: sem(f"{'ab'[i]}_{n}") for n in names} for i in range(2)]
        consts_loaded, setup_dve, setup_pool = sem("consts_loaded"), sem("setup_dve"), sem("setup_pool")
        pat_loaded = [sem(f"pat_loaded{i}") for i in range(2)]
        embedded, x_ready = sem("embedded"), sem("x_ready")
        e1_done, masked = sem("e1_done"), sem("masked")
        r_res, r_stat, r_aggr, h1_ready = sem("r_res"), sem("r_stat"), sem("r_aggr"), sem("h1_ready")
        n_sq = [sem(f"n_sq{i}") for i in range(3)]
        n_ln = [sem(f"n_ln{i}") for i in range(3)]
        n_y0 = [sem(f"n_y0{i}") for i in range(3)]
        n_dve = [sem(f"n_dve{i}") for i in range(3)]
        hc_ready, hb_ready, qk_copied, rotated = sem("hc_ready"), sem("hb_ready"), sem("qk_copied"), sem("rotated")
        by_cos, by_sin, kk_ready = sem("by_cos"), sem("by_sin"), sem("kk_ready")
        rr_ready, res_ready, h2_ready = sem("rr_ready"), sem("res_ready"), sem("h2_ready")
        res_stored = [sem(f"res_stored{i}") for i in range(2)]
        h2_t, h2t, logits = sem("h2_t"), sem("h2t"), sem("logits")
        top_d, top_i, gap, gap_exp = sem("top_d"), sem("top_i"), sem("gap"), sem("gap_exp")
        gate_sum, index_float, gate_inv, one_hot = sem("gate_sum"), sem("index_float"), sem("gate_inv"), sem("one_hot")
        count_float, gates_kept, counted, ranked = sem("count_float"), sem("gates_kept"), sem("counted"), sem("ranked")
        placed, total_float, totalled, hits = sem("placed"), sem("total_float"), sem("totalled"), sem("hits")
        slot_sum, slots_ready, slots_kept, causal_done = sem("slot_sum"), sem("slots_ready"), sem("slots_kept"), sem("causal_done")
        scattered = [sem(f"scattered{i}") for i in range(2)]
        expert_loaded = [sem(f"expert_loaded{e}") for e in range(RAW)]
        zero_ready, counts_ready, tail_slots, zeroed = sem("zero_ready"), sem("counts_ready"), sem("tail_slots"), sem("zeroed")
        plan, plan_ready, experts_ready = sem("plan"), sem("plan_ready"), sem("experts_ready")
        high_part = sem("high_part")
        x_loaded = [sem(f"x_loaded{i}") for i in range(2)]
        mt, mxh, mxt = sem("mt"), sem("mxh"), sem("mxt")
        ath = [sem(f"ath{i}") for i in range(2)]
        gu, sg, ac, a_t, at = ([sem(f"{n}{i}") for i in range(2)] for n in ("gu", "sg", "ac", "a_t", "at"))
        y_ready, y_copied = sem("y_ready"), sem("y_copied")
        y_stored = [sem(f"y_stored{i}") for i in range(2)]
        idx_ready, summed = sem("idx_ready"), sem("summed")
        gathered = [sem(f"gathered{i}") for i in range(2)]
        base_loaded = [sem(f"base_loaded{i}") for i in range(2)]
        out_ready, out_stored = sem("out_ready"), [sem(f"out_stored{i}") for i in range(2)]

        def past(value):
            return not isinstance(value, int) or value > 0

        def alone(eng, value):
            value = value if isinstance(value, int) else eng.compute_val(value)
            eng.wait_ge(setup_dve, 1)
            return value

        def bc(ap, dim, shape):
            return ap.unsqueeze(dim).to_broadcast(shape)

        def row_of(at, step, n=1):
            return bass.ds(at, n) if step is None else slice(at, at + n)

        E4 = [ROWS, HEADS, SEQ]
        xg = xa
        sgb = [sb("sg0", [128, HALF[0]]), sb("sg1", [128, HALF[1]])]
        acb = [sb("ac0", [128, HALF[0]]), sb("ac1", [128, HALF[1]])]
        yb = [rr, hc[0]]
        zero = sb("zero", [128, DIM])
        tails = sb("tails", [128, EXPERTS], u32)
        tailf = sb("tailf", [128, EXPERTS])
        pid = sb("pid", [128, 1])
        thr, tid, bef = sb("thr", [128, TOKENS // TILE]), sb("tid", [1, TILES]), sb("bef", [128, EXPERTS, EXPERTS])
        over, nt = sb("over", [128, EXPERTS, TOKENS // TILE]), sb("nt", [128, EXPERTS])
        pre, cum = sb("pre", [128, EXPERTS, EXPERTS]), sb("cum", [128, EXPERTS])
        shift = sb("shift", [128, EXPERTS])
        own = sgb[0][:, 0:2 * GROUPS * EXPERTS].rearrange("p (g e) -> p g e", e=EXPERTS)
        moved = sb("moved", [128, 2 * GROUPS])
        ge, gt = (x[0:1, 0:TILES * EXPERTS].rearrange("p (j e) -> p j e", e=EXPERTS) for x in (sgb[0], acb[0]))
        te, tb, tl, tr, tw = (sb(f"t_{n}", [1, TILES]) for n in ("e", "b", "l", "r", "w"))
        row_tab, col_tab, need_tab = (sb(n, [1, TILES], u32) for n in ("row_tab", "col_tab", "need_tab"))
        cstep, end_tab = sb("cstep", [1, EXPERTS]), sb("end_tab", [1, EXPERTS], u32)
        endf = sb("endf", [1, EXPERTS])
        yg = [[h2[0], h2[1]], [res[0], res[1]]]
        bt = [rr, hc[0]]
        ob = [h1, hb]
        cidx = [sb(f"cidx{i}", [128, 2], u32) for i in range(2)]
        acc = xa

        attention = ctx.enter_context(ExitStack())
        work = attention.enter_context(nc.sbuf_tensor("work", [128, WORK_COLS], f32))
        used = [0]

        def early(*free):
            n = 1
            for f in free:
                n *= f
            v = work[:, used[0]:used[0] + n]
            used[0] += n
            assert used[0] <= WORK_COLS
            names = " ".join(f"d{i}" for i in range(len(free)))
            return v.rearrange(f"p ({names}) -> p {names}", **{f"d{i}": f for i, f in enumerate(free)})

        pat = [early(PT_TILES, ROWS) for _ in range(2)]
        tokw = early(PT_TILES, DIM)
        wqk = [early(KT, 512) for _ in range(2)]
        wv = [early(KT, DIM) for _ in range(2)]
        wo = [early(KT, DIM) for _ in range(2)]
        qm = [early(KT, IPG, ROWS) for _ in range(2)]
        vrep = [early(IPG, DIM) for _ in range(2)]
        vx = [early(IPG, CHUNKS * 48) for _ in range(2)]
        kx = [early(KT, 4, ROWS) for _ in range(2)]
        z = [early(HEADS, SEQ) for _ in range(2)]
        pr = [early(CHUNKS * CH) for _ in range(2)]
        posb, tokb, ln1w, ln2w = early(DIM), early(DIM), early(DIM), early(DIM)
        qk_sb, qk_cos, qk_sin = early(512), early(512), early(512)
        hm4, hm3, imk, win, cau = early(4), early(HEADS), early(IPG), early(7), early(SEQ)
        cosT, sinT, rotm = early(2, 128), early(2, 128), early(128)
        routw = early(KT, EXPERTS)
        xt = [early(KT, 128) for _ in range(3)]
        ot = [early(KT, ROWS) for _ in range(2)]
        vs = [early(DIM) for _ in range(2)]
        pt = [early(CHUNKS, ROWS) for _ in range(2)]
        sel = [early(3, CHUNKS * 48) for _ in range(2)]

        consts = [(tokw, tok_w), (tokb[0:ROWS], tok_b), (posb[0:ROWS], pos), (wqk[0], a_wqk), (wv[0], a_wv),
                  (wo[0], a_wo), (wqk[1], b_wqk), (wv[1], b_wv), (wo[1], b_wo), (ln1w[0:ROWS], ln1),
                  (ln2w[0:ROWS], ln2), (routw, router), (hm4, headmask4), (hm3[0:ROWS], headmask3),
                  (imk[0:ROWS], imagemask), (win[0:ROWS], window), (cau[0:ROWS], causal), (cosT, rope_cos),
                  (sinT, rope_sin), (rotm, rotate), (ident[:], identity), (low[0:ROWS], lower),
                  (eio[:], expert_iota), (rb[:], region_base),
                  (pid[:], partition_ids), (thr[:], thresholds), (tid[:], tile_ids), (bef[:], before),
                  (cstep[:], col_step)]

        def steps(eng, body):
            for s in range(PEEL):
                body(s, s % 2, s)
            with eng.Fori(PEEL, LOOP_END - 1, 2) as s:
                body(s, 0, None)
                body(s + 1, 1, None)
            for s in range(LOOP_END, STEPS):
                body(s, s % 2, s)

        def live(step, lag):
            return step is None or lag <= step < GROUPS + lag

        def last_rows(step, lag):
            return LAST_ROWS if step == GROUPS - 1 + lag else ROWS

        with nc.Block() as block:
            @block.sync
            def _(sp):
                for dst, src in consts:
                    sp.dma_start(dst, src).then_inc(consts_loaded, 16)
                sp.dma_start(pat[0], patches[:, 0:1].rearrange("p o (t r) -> p (o t) r", r=ROWS)).then_inc(pat_loaded[0], 16)

                def spread_v(l):
                    for h in range(3):
                        for b in range(IPG):
                            sp.dma_start(vrep[l][SEQ * h:SEQ * (h + 1), b],
                                         vs[l][SEQ * b:SEQ * (b + 1)]).then_inc(AB[l]["vrep"], 16)

                def body(s, par, step):
                    if step is None or step + 1 < GROUPS:
                        if past(s):
                            sp.wait_ge(embedded, s)
                        sp.dma_start(pat[1 - par], patches[:, row_of(s + 1, step)].rearrange("p o (t r) -> p (o t) r", r=ROWS))\
                          .then_inc(pat_loaded[1 - par], 16)
                    if live(step, 4):
                        sp.wait_ge(res_ready, s - 3)
                        sp.dma_start(residual[row_of((s - 4) * ROWS, step, ROWS), :], res[par][0:ROWS]).then_inc(res_stored[par], 16)
                    if live(step, 0):
                        sp.wait_ge(AB[0]["vs"], s + 1)
                        if past(s):
                            sp.wait_ge(AB[0]["vx"], s)
                        spread_v(0)
                    if live(step, 2):
                        now, before_it = alone(sp, s - 1), alone(sp, s - 2)
                        sp.wait_ge(AB[1]["vs"], now)
                        if past(before_it):
                            sp.wait_ge(AB[1]["vx"], before_it)
                        spread_v(1)

                steps(sp, body)

            @block.gpsimd
            def _(pool):
                pool.wait_ge(consts_loaded, 16 * len(consts))
                P.memset(nil[:], 0.0)
                for l in range(2):
                    P.memset(vx[l], 0.0).then_inc(setup_pool, 1)
                    P.memset(pr[l], 0.0).then_inc(setup_pool, 1)
                    P.memset(qm[l], 0.0).then_inc(setup_pool, 1)
                for i in range(3):
                    P.memset(xt[i], 0.0).then_inc(setup_pool, 1)
                pool.wait_ge(setup_pool, 9)
                P.memset(zero[:], 0.0).then_inc(zero_ready, 1)
                pool.wait_ge(zero_ready, 1)
                for i in range(SPARE_TILES):
                    r0 = EXPERTS * REGION + i * TILE
                    pool.dma_start(xs[r0:r0 + TILE, :], zero[:]).then_inc(zeroed, 16)

                def expand_v(l, n):
                    pool.wait_ge(AB[l]["vrep"], 144 * n)
                    if past(n - 1):
                        pool.wait_ge(AB[l]["o"], n - 1)
                    shape = [ROWS, IPG, HEADS, HD]
                    P.tensor_tensor(vx[l][0:ROWS, :, 0:DIM].rearrange("p b (h d) -> p b h d", d=HD),
                                    vrep[l][0:ROWS].rearrange("p b (h d) -> p b h d", d=HD),
                                    hm3[0:ROWS].unsqueeze(1).unsqueeze(3).to_broadcast(shape),
                                    ALU.mult).then_inc(AB[l]["vx"], 1)

                def body(s, par, step):
                    if live(step, 3):
                        pool.wait_ge(AB[1]["mx"], s - 2)
                        P.tensor_tensor(z[1][0:ROWS], z[1][0:ROWS], bc(mx[1][0:ROWS], 2, E4), ALU.subtract)\
                         .then_inc(AB[1]["z"], 1)
                    if live(step, 2):
                        if past(s - 3):
                            pool.wait_ge(res_ready, s - 3)
                        pool.wait_ge(h1_ready, s - 1)
                        P.tensor_tensor(hc[par][0:ROWS], h1[0:ROWS], nil[0:ROWS].to_broadcast([ROWS, DIM]), ALU.add)\
                         .then_inc(hc_ready, 1)
                    if live(step, 0):
                        expand_v(0, s + 1)
                    if live(step, 2):
                        pool.wait_ge(qk_copied, s - 1)
                        P.tensor_tensor(qk_cos.rearrange("p (w j t) -> p w j t", w=2, j=2),
                                        qk_sb.rearrange("p (w j t) -> p w j t", w=2, j=2),
                                        bc(cosT, 2, [128, 2, 2, 128]), ALU.mult).then_inc(by_cos, 1)
                        pool.wait_ge(kk_ready, s - 1)
                        for t in range(KT):
                            P.tensor_tensor(kx[1][:, t], bc(kk[:, t], 1, [128, 4, ROWS]), bc(hm4, 2, [128, 4, ROWS]),
                                            ALU.mult).then_inc(AB[1]["kx"], 1)
                    if live(step, 4):
                        rows = last_rows(step, 4)
                        pool.wait_ge(slots_ready, alone(pool, s - 3))
                        for k in range(2):
                            P.indirect_dma_start(xs, bass.IndirectOffsetOnAxis(slot[par][0:rows, k:k + 1], 0),
                                                 h2[par][0:rows], None).then_inc(scattered[par], 16)
                    if live(step, 2):
                        expand_v(1, s - 1)
                    if step == 0:
                        for e in range(RAW):
                            pool.dma_start(raw[e][:], expert_w[:, e]).then_inc(expert_loaded[e], 16)

                steps(pool, body)

            @block.scalar
            def _(act):
                A.preload_act_table_set("natural_log_exp_and_others")
                act.wait_ge(consts_loaded, 16 * len(consts))
                act.wait_ge(setup_pool, 9)
                act.wait_ge(setup_dve, 1)

                def inv_sqrt(i, src, n, rows=ROWS):
                    if i != 2:
                        A.activation(junk[0:rows], src, ACT.Square, accum_out=nrm[i][0:rows, 0:1]).then_inc(n_sq[i], 1)
                        act.wait_ge(n_sq[i], n)
                        A.activation(nrm[i][0:rows, 1:2], nrm[i][0:rows, 0:1], ACT.Ln, bias=eps[0:rows, 1:2],
                                     scale=1.0 / DIM).then_inc(n_ln[i], 1)
                    else:
                        A.activation(nrm[i][0:rows, 1:2], mv[0:rows, 1:2], ACT.Ln, bias=eps[0:rows, 0:1]).then_inc(n_ln[i], 1)
                    act.wait_ge(n_ln[i], n)
                    A.activation(nrm[i][0:rows, 2:3], nrm[i][0:rows, 1:2], ACT.Exp, scale=-0.5).then_inc(n_y0[i], 1)

                def xt_copy(i, ps, ready, n, done, rows=ROWS):
                    act.wait_ge(ready, n)
                    A.activation(xt[i][:, :, 0:rows], ps[:, 0:KT * rows].rearrange("p (t r) -> p t r", t=KT),
                                 ACT.Copy).then_inc(done, 1)

                def diag(l):
                    v = qm[l].rearrange("p t b r -> p t (b r)")
                    return bass.AP(tensor=v.tensor, offset=v.offset,
                                   ap=[v.ap[0], [IPG * ROWS, KT], [ROWS + SEQ, IPG], [1, SEQ]])

                def exp_scores(l, n):
                    A.activation(pr[l][0:ROWS, 0:HEADS * SEQ].rearrange("p (h k) -> p h k", k=SEQ), z[l][0:ROWS],
                                 ACT.Exp).then_inc(AB[l]["e"], 1)

                def copy_pt(l, ps, n):
                    act.wait_ge(AB[l]["p_t"], n)
                    A.activation(pt[l][0:CH].rearrange("p (j c) r -> p j (c r)", j=2),
                                 ps[0:CH, :, 0:3 * ROWS], ACT.Copy).then_inc(AB[l]["pt"], 1)

                def first_image(l, ps, n):
                    act.wait_ge(AB[l]["o"], n)
                    A.activation(sel[l][0:ROWS, 0].rearrange("p (j d) -> p j d", j=2), ps[0:ROWS, :, 0:144],
                                 ACT.Copy, scale=imk[0:ROWS, 0:1]).then_inc(AB[l]["o0"], 1)

                def copy_ot(l, ps, n):
                    act.wait_ge(AB[l]["o_t"], n)
                    A.activation(ot[l], ps[:, 0:KT * ROWS].rearrange("p (t r) -> p t r", t=KT),
                                 ACT.Copy).then_inc(AB[l]["ot"], 1)

                def body(s, par, step):
                    rrows = last_rows(step, 4)
                    if live(step, 1):
                        act.wait_ge(AB[0]["z"], s)
                        A.activation(z[0][0:ROWS], z[0][0:ROWS], ACT.Exp).then_inc(e1_done, 1)
                    if live(step, 2):
                        act.wait_ge(r_aggr, s - 1)
                        inv_sqrt(2, None, s - 1)
                    if live(step, 1):
                        act.wait_ge(masked, 2 * s)
                        exp_scores(0, s)
                    if live(step, 4):
                        copy_ot(1, Lb[1], s - 3)
                    if live(step, 2):
                        act.wait_ge(h1_ready, s - 1)
                        inv_sqrt(0, h1[0:ROWS], s - 1)
                    if live(step, 0):
                        xt_copy(0, Lb[0], AB[0]["x_t"], s + 1, AB[0]["xt"])
                    if live(step, 2):
                        xt_copy(1, Lb[2], AB[1]["x_t"], s - 1, AB[1]["xt"])
                    if live(step, 1):
                        copy_pt(0, X, s)
                    if live(step, 4):
                        act.wait_ge(rr_ready, s - 3)
                        inv_sqrt(1, rr[0:rrows], s - 3, rrows)
                    if live(step, 0):
                        act.wait_ge(AB[0]["qk"], s + 1)
                        A.activation(diag(0), Lb[3][:, 0:256].rearrange("p (t r) -> p t r", t=KT)[:, :, 0:ROWS]
                                     .rearrange("p t (b q) -> p t b q", b=IPG), ACT.Copy, scale=0.25)\
                         .then_inc(AB[0]["qm"], 1)
                        if past(s):
                            act.wait_ge(AB[0]["vrep"], 144 * s)
                        act.wait_ge(AB[0]["v"], s + 1)
                        A.activation(vs[0][0:ROWS], Lb[0][0:ROWS, 0:DIM], ACT.Copy).then_inc(AB[0]["vs"], 1)
                    if live(step, 3):
                        act.wait_ge(AB[1]["z"], s - 2)
                        exp_scores(1, s - 2)
                    if live(step, 1):
                        first_image(0, Y, s)
                    if live(step, 2):
                        act.wait_ge(AB[1]["qk"], s - 1)
                        A.activation(qk_sb, Lb[1][:], ACT.Copy).then_inc(qk_copied, 1)
                        if past(s - 2):
                            act.wait_ge(AB[1]["vrep"], 144 * s - 288)
                        act.wait_ge(AB[1]["v"], s - 1)
                        A.activation(vs[1][0:ROWS], Lb[2][0:ROWS, 0:DIM], ACT.Copy).then_inc(AB[1]["vs"], 1)
                    if live(step, 3):
                        copy_pt(1, X, s - 2)
                    if live(step, 4):
                        xt_copy(2, Lb[3], h2_t, s - 3, h2t, rrows)
                    if live(step, 1):
                        copy_ot(0, Lb[0], s)
                    if live(step, 4):
                        act.wait_ge(gap, s - 3)
                        A.activation(rt[0:rrows, 1:2], rt[0:rrows, 0:1], ACT.Exp).then_inc(gap_exp, 1)
                    if live(step, 3):
                        first_image(1, X, s - 2)

                steps(act, body)

            @block.vector
            def _(dve):
                V.memset(eps[:, 0:1], LN_EPS)
                V.memset(oneb[:], 1.0)
                V.memset(tot[:], 0.0)
                V.memset(place_all[:], 0.0)
                V.memset(exp_all[:], 0.0)
                V.memset(totb[:], 0.0)
                V.memset(eps[:, 1:2], RMS_EPS).then_inc(setup_dve, 1)
                dve.wait_ge(consts_loaded, 16 * len(consts))
                dve.wait_ge(setup_pool, 9)
                V.tensor_tensor(posb[0:ROWS], posb[0:ROWS], tokb[0:ROWS], ALU.add).then_inc(setup_dve, 1)
                V.tensor_copy(lowb[0:ROWS], low[0:ROWS]).then_inc(setup_dve, 1)
                dve.wait_ge(setup_dve, 3)

                def newton(i, n, rows=ROWS):
                    q = nrm[i][0:rows]
                    if i == 2:
                        V.tensor_scalar(q[:, 3:4], mv[0:rows, 1:2], LN_EPS, None, ALU.add).then_inc(n_dve[i], 1)
                    else:
                        dve.wait_ge(n_sq[i], n)
                        V.tensor_scalar(q[:, 3:4], q[:, 0:1], 1.0 / DIM, RMS_EPS, ALU.mult, ALU.add).then_inc(n_dve[i], 1)
                    dve.wait_ge(n_y0[i], n)
                    dve.wait_ge(n_dve[i], 4 * n - 3)
                    V.scalar_tensor_tensor(q[:, 4:5], q[:, 2:3], q[:, 2:3], q[:, 3:4], ALU.mult, ALU.mult).then_inc(n_dve[i], 1)
                    dve.wait_ge(n_dve[i], 4 * n - 2)
                    V.tensor_scalar(q[:, 5:6], q[:, 4:5], -0.5, 1.5, ALU.mult, ALU.add).then_inc(n_dve[i], 1)
                    dve.wait_ge(n_dve[i], 4 * n - 1)
                    V.tensor_tensor(q[:, 6:7], q[:, 5:6], q[:, 2:3], ALU.mult).then_inc(n_dve[i], 1)
                    dve.wait_ge(n_dve[i], 4 * n)

                def row_sum(l, n):
                    dve.wait_ge(AB[l]["e"], n)
                    V.tensor_reduce(sm[l][0:ROWS], pr[l][0:ROWS, 0:HEADS * SEQ].rearrange("p (h k) -> p h k", k=SEQ),
                                    AX.X, ALU.add).then_inc(AB[l]["sm"], 1)
                    dve.wait_ge(AB[l]["sm"], n)
                    V.reciprocal(ri[l][0:ROWS], sm[l][0:ROWS]).then_inc(AB[l]["ri"], 1)

                def select(l, ps, n):
                    for b in (1, 2):
                        if b == 1:
                            dve.wait_ge(AB[l]["o0"], n)
                        else:
                            dve.wait_ge(AB[l]["osel"], 2 * n - 1)
                        V.scalar_tensor_tensor(
                            sel[l][0:ROWS, b].rearrange("p (j d) -> p j d", j=2), ps[0:ROWS, :, 144 * b:144 * (b + 1)],
                            imk[0:ROWS, b:b + 1], sel[l][0:ROWS, b - 1].rearrange("p (j d) -> p j d", j=2),
                            ALU.mult, ALU.add).then_inc(AB[l]["osel"], 1)
                    dve.wait_ge(AB[l]["osel"], 2 * n)
                    dve.wait_ge(AB[l]["ri"], n)
                    V.tensor_tensor(sel[l][0:ROWS, 0, 0:DIM].rearrange("p (h d) -> p h d", d=HD),
                                    sel[l][0:ROWS, 2, 0:DIM].rearrange("p (h d) -> p h d", d=HD),
                                    bc(ri[l][0:ROWS], 2, [ROWS, HEADS, HD]), ALU.mult).then_inc(AB[l]["on"], 1)

                def body(s, par, step):
                    rows = last_rows(step, 4)
                    nR = s - 3
                    if live(step, 2):
                        dve.wait_ge(AB[0]["y"], s - 1)
                        V.tensor_tensor(xa[par][0:ROWS], Lb[0][0:ROWS, 0:DIM], xa[par][0:ROWS], ALU.add).then_inc(r_res, 1)
                        dve.wait_ge(r_res, s - 1)
                        V.bn_stats(st[0:ROWS], xa[par][0:ROWS]).then_inc(r_stat, 1)
                        dve.wait_ge(r_stat, alone(dve, s - 1))
                        V.bn_aggr(mv[0:ROWS], st[0:ROWS]).then_inc(r_aggr, 1)
                    if live(step, 1):
                        dve.wait_ge(e1_done, s)
                        V.tensor_tensor(z[0][0:ROWS, :, 0:3], z[0][0:ROWS, :, 0:3], bc(win[0:ROWS, 0:3], 1, [ROWS, HEADS, 3]),
                                        ALU.mult).then_inc(masked, 1)
                        V.tensor_tensor(z[0][0:ROWS, :, 32:36], z[0][0:ROWS, :, 32:36], bc(win[0:ROWS, 3:7], 1, [ROWS, HEADS, 4]),
                                        ALU.mult).then_inc(masked, 1)
                    if live(step, 2):
                        dve.wait_ge(r_aggr, s - 1)
                        newton(2, s - 1)
                        V.tensor_scalar(h1[0:ROWS], xa[par][0:ROWS], mv[0:ROWS, 0:1], nrm[2][0:ROWS, 6:7],
                                        ALU.subtract, ALU.mult).then_inc(h1_ready, 1)
                    if live(step, 0):
                        if past(s - 1):
                            dve.wait_ge(h1_ready, s - 1)
                        dve.wait_ge(embedded, s + 1)
                        V.tensor_tensor(xa[par][0:ROWS], Lb[3][0:ROWS, 0:DIM], posb[0:ROWS], ALU.add).then_inc(x_ready, 1)
                    if live(step, 2):
                        newton(0, s - 1)
                        V.scalar_tensor_tensor(hb[0:ROWS], h1[0:ROWS], nrm[0][0:ROWS, 6:7], ln1w[0:ROWS],
                                               ALU.mult, ALU.mult).then_inc(hb_ready, 1)
                    if live(step, 3):
                        dve.wait_ge(AB[1]["s"], s - 2)
                        V.tensor_tensor(z[1][0:ROWS].rearrange("p (j h) k -> p j h k", j=2),
                                        X[0:ROWS, :, 0:8 * SEQ].rearrange("p j (h k) -> p j h k", k=SEQ),
                                        cau[0:ROWS].unsqueeze(1).unsqueeze(1).to_broadcast([ROWS, 2, 8, SEQ]),
                                        ALU.add).then_inc(causal_done, 1)
                        dve.wait_ge(causal_done, s - 2)
                        V.tensor_reduce(mx[1][0:ROWS], z[1][0:ROWS], AX.X, ALU.max).then_inc(AB[1]["mx"], 1)
                    if live(step, 1):
                        row_sum(0, s)
                    if live(step, 4):
                        dve.wait_ge(AB[1]["y"], nR)
                        V.tensor_tensor(rr[0:ROWS], Lb[1][0:ROWS, 0:DIM], hc[par][0:ROWS], ALU.add).then_inc(rr_ready, 1)
                        dve.wait_ge(rr_ready, nR)
                        if past(8 * s - 32 - 8 * par):
                            dve.wait_ge(res_stored[par], 8 * s - 32 - 8 * par)
                        V.tensor_tensor(res[par][0:ROWS], rr[0:ROWS], hc[par][0:ROWS], ALU.add).then_inc(res_ready, 1)
                        newton(1, nR, rows)
                        if past(16 * s - 64 - 16 * par):
                            dve.wait_ge(scattered[par], 16 * s - 64 - 16 * par)
                        V.scalar_tensor_tensor(h2[par][0:rows], rr[0:rows], nrm[1][0:rows, 6:7], ln2w[0:rows],
                                               ALU.mult, ALU.mult).then_inc(h2_ready, 1)
                    if live(step, 0):
                        dve.wait_ge(AB[0]["qm"], s + 1)
                        V.tensor_tensor(
                            kx[0], Lb[3][:, 256:512].rearrange("p (t r) -> p t r", t=KT)[:, :, 0:ROWS].unsqueeze(2)
                            .to_broadcast([128, KT, 4, ROWS]),
                            hm4.unsqueeze(1).unsqueeze(3).to_broadcast([128, KT, 4, ROWS]), ALU.mult)\
                         .then_inc(AB[0]["kx"], 2)
                    if live(step, 3):
                        row_sum(1, s - 2)
                    if live(step, 1):
                        select(0, Y, s)
                    if live(step, 0):
                        dve.wait_ge(AB[0]["s"], s + 1)
                        s4 = Y[0:ROWS, :, 0:8 * SEQ].rearrange("p j (h k) -> p j h k", k=SEQ)
                        V.tensor_reduce(mx[0][0:ROWS].rearrange("p (j h) -> p j h", j=2), s4, AX.X, ALU.max)\
                         .then_inc(AB[0]["mx"], 1)
                        dve.wait_ge(AB[0]["mx"], s + 1)
                        V.tensor_tensor(z[0][0:ROWS].rearrange("p (j h) k -> p j h k", j=2), s4,
                                        mx[0][0:ROWS].rearrange("p (j h) -> p j h", j=2).unsqueeze(3)
                                        .to_broadcast([ROWS, 2, 8, SEQ]), ALU.subtract).then_inc(AB[0]["z"], 1)
                    if live(step, 4):
                        dve.wait_ge(logits, alone(dve, nR))
                        V.max(top[0:rows], Lb[2][0:rows, 256:256 + EXPERTS]).then_inc(top_d, 1)
                        dve.wait_ge(top_d, alone(dve, nR))
                        V.max_index(topi[0:rows], top[0:rows], Lb[2][0:rows, 256:256 + EXPERTS]).then_inc(top_i, 1)
                        V.tensor_tensor(rt[0:rows, 0:1], top[0:rows, 1:2], top[0:rows, 0:1], ALU.subtract).then_inc(gap, 1)
                    if live(step, 2):
                        dve.wait_ge(rotated, s - 1)
                        V.tensor_tensor(qk_sin.rearrange("p (w j t) -> p w j t", w=2, j=2),
                                        Lb[3][:].rearrange("p (w j t) -> p w j t", w=2, j=2),
                                        bc(sinT, 2, [128, 2, 2, 128]), ALU.mult).then_inc(by_sin, 1)
                        dve.wait_ge(by_sin, s - 1)
                        dve.wait_ge(by_cos, s - 1)
                        c4, s4 = (x.rearrange("p (j t) -> p j t", j=4)[:, :, 0:ROWS] for x in (qk_cos, qk_sin))
                        v = qm[1].rearrange("p t b r -> p t (b r)")
                        dg = bass.AP(tensor=v.tensor, offset=v.offset,
                                     ap=[v.ap[0], [IPG * ROWS, KT], [ROWS + SEQ, IPG], [1, SEQ]])
                        V.tensor_tensor(kk[:], c4[:, 2:4], s4[:, 2:4], ALU.add).then_inc(kk_ready, 1)
                        V.tensor_tensor(dg, c4[:, 0:2].rearrange("p t (b q) -> p t b q", b=IPG),
                                        s4[:, 0:2].rearrange("p t (b q) -> p t b q", b=IPG), ALU.add).then_inc(AB[1]["qm"], 1)
                    if live(step, 4):
                        dve.wait_ge(gap_exp, nR)
                        V.tensor_scalar(rt[0:rows, 2:3], rt[0:rows, 1:2], 1.0, None, ALU.add).then_inc(gate_sum, 1)
                        dve.wait_ge(top_i, nR)
                        V.tensor_copy(topf[0:rows], topi[0:rows, 0:2]).then_inc(index_float, 1)
                        dve.wait_ge(gate_sum, nR)
                        V.reciprocal(rt[0:rows, 3:4], rt[0:rows, 2:3]).then_inc(gate_inv, 1)
                        dve.wait_ge(index_float, nR)
                        for k in range(2):
                            V.tensor_scalar(oh[0:rows, k], eio[0:rows], topf[0:rows, k:k + 1], None, ALU.is_equal)\
                             .then_inc(one_hot, 1)
                        dve.wait_ge(one_hot, 2 * nR)
                        V.tensor_tensor(cnt[0:rows], oh[0:rows, 0], oh[0:rows, 1], ALU.add).then_inc(count_float, 1)
                        g = row_of(s - 4, step)
                        dve.wait_ge(gate_inv, nR)
                        V.tensor_copy(w_all[0:rows, g, 0], rt[0:rows, 3:4])
                        dve.wait_ge(count_float, nR)
                        V.tensor_copy(cntb[0:rows], cnt[0:rows]).then_inc(counted, 1)
                        V.tensor_tensor(w_all[0:rows, g, 1], rt[0:rows, 3:4], rt[0:rows, 1:2], ALU.mult)\
                         .then_inc(gates_kept, 1)
                    if live(step, 3):
                        select(1, X, s - 2)
                    if live(step, 4):
                        dve.wait_ge(ranked, nR)
                        V.tensor_tensor(place[0:rows], Lb[2][0:rows, 264:264 + EXPERTS], rb[0:rows], ALU.add)\
                         .then_inc(placed, 1)
                        V.tensor_tensor(tot[0:rows], tot[0:rows], cnt[0:rows], ALU.add).then_inc(total_float, 1)
                        dve.wait_ge(placed, nR)
                        V.tensor_tensor(hit[0:rows], oh[0:rows], bc(place[0:rows], 1, [rows, 2, EXPERTS]), ALU.mult)\
                         .then_inc(hits, 1)
                        dve.wait_ge(total_float, nR)
                        V.tensor_copy(totb[0:rows], tot[0:rows]).then_inc(totalled, 1)
                        dve.wait_ge(hits, nR)
                        V.tensor_reduce(slotf[0:rows], hit[0:rows], AX.X, ALU.add).then_inc(slot_sum, 1)
                        V.tensor_copy(exp_all[0:rows, g].rearrange("p o k -> p (o k)"), topf[0:rows])
                        dve.wait_ge(slot_sum, nR)
                        V.tensor_copy(slot[par][0:rows], slotf[0:rows]).then_inc(slots_ready, 1)
                        V.tensor_copy(place_all[0:rows, g].rearrange("p o k -> p (o k)"), slotf[0:rows])\
                         .then_inc(slots_kept, 1)

                steps(dve, body)

            @block.tensor
            def _(pe):
                pe.wait_ge(consts_loaded, 16 * len(consts))
                pe.wait_ge(setup_pool, 9)
                pe.wait_ge(setup_dve, 3)

                def transpose_x(ps, src, ready, n, done, rows=ROWS):
                    pe.wait_ge(ready, n)
                    for t in range(KT):
                        last = T.transpose(ps[:, t * rows:(t + 1) * rows], src[0:rows, t * 128:(t + 1) * 128],
                                           ident[0:rows, 0:rows])
                    last.then_inc(done, 1)

                def project(l, qk_bank, v_bank, n):
                    pe.wait_ge(AB[l]["xt"], n)
                    for j in range(4):
                        for t in range(KT):
                            last = T.matmul(qk_bank[:, j * 128:(j + 1) * 128], wqk[l][:, t, j * 128:(j + 1) * 128], xt[l][:, t],
                                            start=t == 0, stop=t == KT - 1)
                    last.then_inc(AB[l]["qk"], 1)
                    for t in range(KT):
                        last = T.matmul(v_bank[0:ROWS, 0:DIM], xt[l][:, t, 0:ROWS], wv[l][:, t], start=t == 0, stop=t == KT - 1)
                    last.then_inc(AB[l]["v"], 1)

                def scores(l, ps, n):
                    pe.wait_ge(AB[l]["qm"], n)
                    pe.wait_ge(AB[l]["kx"], 2 * n)
                    for t in range(KT):
                        for r in range(2):
                            for b in range(IPG):
                                last = T.matmul(ps[0:ROWS, r, t * 144:(t + 1) * 144], qm[l][64 * r:64 * r + 64, t, b],
                                                kx[l][64 * r:64 * r + 64, t, :, SEQ * b:SEQ * (b + 1)],
                                                start=b == 0, stop=b == IPG - 1)
                    last.then_inc(AB[l]["s"], 1)

                def transpose_p(l, ps, n):
                    pe.wait_ge(AB[l]["e"], n)
                    for c in range(CHUNKS):
                        last = T.transpose(ps[0:CH, c // 3, (c % 3) * ROWS:(c % 3 + 1) * ROWS],
                                           pr[l][0:ROWS, c * CH:(c + 1) * CH], ident[0:ROWS, 0:ROWS])
                    last.then_inc(AB[l]["p_t"], 1)

                def values(l, ps, n):
                    pe.wait_ge(AB[l]["pt"], n)
                    pe.wait_ge(AB[l]["vx"], n)
                    for c in range(CHUNKS):
                        last = T.matmul(ps[0:ROWS, c // 3, 0:432].rearrange("p (b c d) -> p b c d", b=3, c=3)[:, :, c % 3],
                                        pt[l][0:CH, c], vx[l][0:CH, :, 48 * c:48 * (c + 1)], start=True, stop=True)
                    last.then_inc(AB[l]["o"], 1)

                def transpose_o(l, ps, n):
                    pe.wait_ge(AB[l]["on"], n)
                    for t in range(KT):
                        last = T.transpose(ps[:, t * ROWS:(t + 1) * ROWS], sel[l][0:ROWS, 0, t * 128:(t + 1) * 128],
                                           ident[0:ROWS, 0:ROWS])
                    last.then_inc(AB[l]["o_t"], 1)

                def project_out(l, ps, n):
                    pe.wait_ge(AB[l]["ot"], n)
                    for t in range(KT):
                        last = T.matmul(ps[0:ROWS, 0:DIM], ot[l][:, t], wo[l][:, t], start=t == 0, stop=t == KT - 1)
                    last.then_inc(AB[l]["y"], 1)

                def body(s, par, step):
                    rows = last_rows(step, 4)
                    nR = s - 3
                    if live(step, 0):
                        pe.wait_ge(pat_loaded[par], 8 * s + 16 - 8 * par)
                        if past(s - 2):
                            pe.wait_ge(AB[1]["qm"], s - 2)
                        for t in range(PT_TILES):
                            last = T.matmul(Lb[3][0:ROWS, 0:DIM], pat[par][:, t], tokw[:, t], start=t == 0, stop=t == PT_TILES - 1)
                        last.then_inc(embedded, 1)
                    if live(step, 4):
                        transpose_o(1, Lb[1], nR)
                    if live(step, 3):
                        scores(1, X, s - 2)
                    if live(step, 4):
                        project_out(1, Lb[1], nR)
                    if live(step, 0):
                        if past(s - 1):
                            pe.wait_ge(r_res, s - 1)
                        transpose_x(Lb[0], xa[par], x_ready, s + 1, AB[0]["x_t"])
                    if live(step, 2):
                        if past(s - 4):
                            pe.wait_ge(placed, s - 4)
                        transpose_x(Lb[2], hb, hb_ready, s - 1, AB[1]["x_t"])
                    if live(step, 1):
                        if past(s - 2):
                            pe.wait_ge(causal_done, s - 2)
                        transpose_p(0, X, s)
                    if live(step, 0):
                        project(0, Lb[3], Lb[0], s + 1)
                    if live(step, 1):
                        if past(s):
                            pe.wait_ge(AB[0]["z"], s)
                        values(0, Y, s)
                    if live(step, 2):
                        if past(s - 3):
                            pe.wait_ge(rr_ready, s - 3)
                        project(1, Lb[1], Lb[2], s - 1)
                    if live(step, 3):
                        if live(step, 1):
                            pe.wait_ge(AB[0]["pt"], s)
                        transpose_p(1, X, s - 2)
                    if live(step, 4):
                        if live(step, 0):
                            pe.wait_ge(AB[0]["kx"], 2 * s + 2)
                        transpose_x(Lb[3], h2[par], h2_ready, nR, h2_t, rows)
                    if live(step, 1):
                        if live(step, 0):
                            pe.wait_ge(AB[0]["vs"], s + 1)
                        transpose_o(0, Lb[0], s)
                    if live(step, 0):
                        if past(s):
                            pe.wait_ge(AB[0]["on"], s)
                        scores(0, Y, s + 1)
                    if live(step, 4):
                        pe.wait_ge(h2t, nR)
                        if live(step, 2):
                            pe.wait_ge(AB[1]["vs"], s - 1)
                        for t in range(KT):
                            last = T.matmul(Lb[2][0:rows, 256:256 + EXPERTS], xt[2][:, t, 0:rows], routw[:, t],
                                            start=t == 0, stop=t == KT - 1)
                        last.then_inc(logits, 1)
                    if live(step, 2):
                        pe.wait_ge(qk_copied, s - 1)
                        T.matmul(Lb[3][:], rotm, qk_sb, start=True, stop=True).then_inc(rotated, 1)
                    if live(step, 3):
                        values(1, X, s - 2)
                    if live(step, 1):
                        project_out(0, Lb[0], s)
                    if live(step, 4):
                        pe.wait_ge(counted, nR)
                        if past(nR - 1):
                            pe.wait_ge(totalled, nR - 1)
                        o = Lb[2][0:rows, 264:264 + EXPERTS]
                        T.matmul(o, lowb[0:rows, 0:rows], cntb[0:rows], start=True, stop=False)
                        T.matmul(o, oneb[0:ROWS, 0:rows], totb[0:ROWS], start=False, stop=True).then_inc(ranked, 1)

                steps(pe, body)

        attention.close()
        high, low_ = (ctx.enter_context(nc.sbuf_tensor(n, [128, RING * EXPERT_COLS], f32r)) for n in ("w_high", "w_low"))
        xm = [tuple(sb(f"x{n}{i}", [128, DIM], f32r) for n in ("high", "low")) for i in range(2)]
        atb = [tuple(sb(f"act_{n}{i}", [128, HALF[i]], f32r) for n in ("high", "low")) for i in range(2)]
        HEAD = (0, HALF[0])
        N_PLAN = 12

        def pair(eng, body, first, last, start):
            for j in range(first, start):
                body(j, j % 2, j)
            with eng.Fori(start, last - 1, 2) as j:
                body(j, start % 2, None)
                body(j + 1, 1 - start % 2, None)

        with nc.Block() as block:
            @block.sync
            def _(sp):
                sp.wait_ge(plan_ready, 1)
                sp.wait_ge(zeroed, 16 * (EXPERTS + SPARE_TILES))
                for i in range(2):
                    sp.wait_ge(scattered[i], 16 * GROUPS)

                def load(j, par, at):
                    row = sp.value_load(row_tab[0:1, row_of(j, at)], min_val=0, max_val=XS_ROWS - TILE)
                    sp.dma_start(xg[par][:], xs[bass.ds(row, TILE), :]).then_inc(x_loaded[par], 16)

                def body(j, par, at):
                    if at is None or at + 1 < TILES:
                        if past(j):
                            sp.wait_ge(mt, alone(sp, j))
                        load(j + 1, 1 - par, None if at is None else at + 1)
                    if at is None or at > 0:
                        store(j - 1, 1 - par, at)

                def store(j, par, at):
                    sp.wait_ge(y_copied, j + 1)
                    sp.dma_start(ys[row_of(j * TILE, at, TILE), :], yb[par][:]).then_inc(y_stored[par], 16)

                load(0, 0, 0)
                pair(sp, body, 0, TILES - 1, 2)
                body(TILES - 1, (TILES - 1) % 2, TILES - 1)
                store(TILES - 1, (TILES - 1) % 2, 0)

            @block.gpsimd
            def _(pool):
                pool.wait_ge(tail_slots, 1)
                for e in range(EXPERTS):
                    P.indirect_dma_start(xs, bass.IndirectOffsetOnAxis(tails[:, e:e + 1], 0), zero[:], None)\
                     .then_inc(zeroed, 16)

                def load(e):
                    pool.wait_ge(experts_ready, e - RAW + 1)
                    pool.dma_start(raw[e % RAW][:], expert_w[:, e]).then_inc(expert_loaded[e % RAW], 16)

                def split(e):
                    if e >= RING:
                        end = pool.value_load(end_tab[0:1, e - RING:e - RING + 1], min_val=1, max_val=TILES + 1)
                    h, l = (x[:, e % RING * EXPERT_COLS:(e % RING + 1) * EXPERT_COLS] for x in (high, low_))
                    pool.wait_ge(expert_loaded[e % RAW], 16 * (e // RAW + 1))
                    if e >= RING:
                        pool.wait_ge(y_ready, end)
                    P.tensor_copy(h, raw[e % RAW][:]).then_inc(high_part, 1)
                    pool.wait_ge(high_part, e + 1)
                    P.tensor_tensor(l, raw[e % RAW][:], h, ALU.subtract).then_inc(experts_ready, 1)

                pool.wait_ge(plan_ready, 1)
                for e in range(1, EXPERTS):
                    if e + 1 < EXPERTS:
                        load(e + 1)
                    split(e)

            @block.scalar
            def _(act):
                act.wait_ge(expert_loaded[0], 16)
                A.activation(high[:, 0:EXPERT_COLS], raw[0][:], ACT.Copy).then_inc(high_part, 1)

                def silu(h, n):
                    act.wait_ge(gu[h], n)
                    A.activation(sgb[h][:], S[h][:, 0, 0:HALF[h]], ACT.Silu).then_inc(sg[h], 1)

                def copy_y(par, n):
                    act.wait_ge(y_ready, n + 1)
                    if past(8 * n - 8 - 8 * par):
                        act.wait_ge(y_stored[par], 8 * n - 8 - 8 * par)
                    A.activation(yb[par][:], Lb[3][:, 0:DIM], ACT.Copy).then_inc(y_copied, 1)

                def body(j, par, at):
                    silu(0, j + 1)
                    silu(1, j + 1)
                    if at is None or at > 0:
                        copy_y(1 - par, j)

                pair(act, body, 0, TILES - 1, 2)
                body(TILES - 1, (TILES - 1) % 2, TILES - 1)
                copy_y((TILES - 1) % 2, TILES)

            @block.vector
            def _(dve):
                done = [0]

                def step(ins):
                    done[0] += 1
                    ins.then_inc(plan, 1)
                    dve.wait_ge(plan, done[0])

                dve.wait_ge(counts_ready, 1)
                n_e = Lb[3][:, 0:EXPERTS]
                step(V.tensor_tensor(tailf[:], n_e, rb[:], ALU.add))
                step(V.tensor_scalar(tailf[:], tailf[:], pid[:], None, ALU.add))
                V.tensor_copy(tails[:], tailf[:]).then_inc(tail_slots, 1)
                eq, ee = [128, EXPERTS, TOKENS // TILE], [128, EXPERTS, EXPERTS]
                step(V.tensor_tensor(over[:], bc(n_e, 2, eq), bc(thr[:], 1, eq), ALU.is_gt))
                step(V.tensor_reduce(nt[:], over[:], AX.X, ALU.add))
                step(V.tensor_tensor(pre[:], bc(nt[:], 1, ee), bef[:], ALU.mult))
                step(V.tensor_reduce(cum[:], pre[:], AX.X, ALU.add))
                je = [1, TILES, EXPERTS]
                step(V.tensor_tensor(ge, bc(tid[:], 2, je), bc(cum[0:1], 1, je), ALU.is_ge))
                step(V.tensor_reduce(te[:], ge, AX.X, ALU.add))
                step(V.tensor_tensor(gt, ge, bc(nt[0:1], 1, je), ALU.mult))
                step(V.tensor_reduce(tb[:], gt, AX.X, ALU.add))
                step(V.tensor_tensor(tl[:], tid[:], tb[:], ALU.subtract))
                step(V.tensor_scalar(tl[:], tl[:], float(TILE), None, ALU.mult))
                step(V.tensor_tensor(gt, ge, bc(cstep[:], 1, je), ALU.mult))
                step(V.tensor_reduce(tw[:], gt, AX.X, ALU.add))
                step(V.tensor_copy(col_tab[:], tw[:]))
                step(V.tensor_scalar(endf[:], cum[0:1], 1.0, None, ALU.add))
                step(V.tensor_copy(end_tab[:], endf[:]))
                step(V.scalar_tensor_tensor(tr[:], te[:], float(REGION), tl[:], ALU.mult, ALU.add))
                step(V.tensor_copy(row_tab[:], tr[:]))
                step(V.tensor_scalar(tw[:], te[:], float(EXPERTS - 1), 1.0, ALU.min, ALU.add))
                V.tensor_copy(need_tab[:], tw[:]).then_inc(plan_ready, 1)
                def times_up(h, n):
                    dve.wait_ge(sg[h], n)
                    V.tensor_tensor(acb[h][:], sgb[h][:], S[h][:, 1, 0:HALF[h]], ALU.mult).then_inc(ac[h], 1)

                def split_psum(high, low, src, high_done, n, low_done):
                    V.tensor_copy(high, src).then_inc(high_done, 1)
                    dve.wait_ge(high_done, n)
                    V.tensor_tensor(low, src, high, ALU.subtract).then_inc(low_done, 1)

                def split_at(h, n):
                    dve.wait_ge(a_t[h], n)
                    split_psum(atb[h][0][:, 0:HALF[h]], atb[h][1][:, 0:HALF[h]], L[h][:, 0:HALF[h]], ath[h], n, at[h])

                def split_x(par, n):
                    dve.wait_ge(mt, n)
                    split_psum(xm[par][0][:], xm[par][1][:], Lb[2][:, 0:DIM], mxh, n, mxt)

                def body(j, par, at_):
                    if at_ is None or at_ > 0:
                        split_at(1, j)
                    times_up(0, j + 1)
                    if at_ is None or at_ + 1 < TILES:
                        split_x(1 - par, j + 2)
                    split_at(0, j + 1)
                    times_up(1, j + 1)

                dve.wait_ge(high_part, 1)
                V.tensor_tensor(low_[:, 0:EXPERT_COLS], raw[0][:], high[:, 0:EXPERT_COLS], ALU.subtract)\
                 .then_inc(experts_ready, 1)
                split_x(0, 1)
                pair(dve, body, 0, TILES - 1, 2)
                body(TILES - 1, (TILES - 1) % 2, TILES - 1)
                split_at(1, TILES)
                ke = [128, 2 * GROUPS, EXPERTS]
                step(V.tensor_tensor(shift[:], cum[:], nt[:], ALU.subtract))
                step(V.scalar_tensor_tensor(shift[:], shift[:], float(TILE), rb[:], ALU.mult, ALU.subtract))
                step(V.tensor_tensor(own, bc(exp_all[:].rearrange("p g k -> p (g k)"), 2, ke), bc(eio[:], 1, ke), ALU.is_equal))
                step(V.tensor_tensor(own, own, bc(shift[:], 1, ke), ALU.mult))
                step(V.tensor_reduce(moved[:], own, AX.X, ALU.add))
                step(V.tensor_tensor(moved[:], moved[:], place_all[:].rearrange("p g k -> p (g k)"), ALU.add))
                step(V.tensor_copy(slot_all[:].rearrange("p g k -> p (g k)"), moved[:]))


            @block.tensor
            def _(pe):
                T.matmul(Lb[3][:, 0:EXPERTS], oneb[0:ROWS, :], totb[0:ROWS], start=True, stop=True).then_inc(counts_ready, 1)
                pe.sem_inc(y_ready, 1)

                def split_product(ps, x, at, n, start, stop):
                    w_high, w_low = (w[:, bass.ds(at, n)] for w in (high, low_))
                    T.matmul(ps, x[0], w_high, start=start, stop=False)
                    T.matmul(ps, x[0], w_low, start=False, stop=False)
                    return T.matmul(ps, x[1], w_high, start=False, stop=stop)

                def transpose_tile(par, n):
                    pe.wait_ge(x_loaded[par], 8 * n + 8 - 8 * par)
                    for t in range(KT):
                        last = T.transpose(Lb[2][:, t * TILE:(t + 1) * TILE], xg[par][:, t * 128:(t + 1) * 128], ident[:])
                    last.then_inc(mt, 1)

                def gate_up(par, h, n, col):
                    pe.wait_ge(mxt, n)
                    if past(n - 1):
                        pe.wait_ge(ac[h], n - 1)
                    for u in range(2):
                        for t in range(KT):
                            c0 = (2 * t + u) * FF + HEAD[h]
                            last = split_product(S[h][:, u, 0:HALF[h]], [x[:, t * 128:(t + 1) * 128] for x in xm[par]],
                                                 col + c0, HALF[h], t == 0, t == KT - 1)
                    last.then_inc(gu[h], 1)

                def transpose_act(h, n):
                    pe.wait_ge(ac[h], n)
                    for c in range(HALF[h] // 128):
                        last = T.transpose(L[h][:, c * 128:(c + 1) * 128], acb[h][:, c * 128:(c + 1) * 128], ident[:])
                    last.then_inc(a_t[h], 1)

                def down(h, n, col):
                    pe.wait_ge(at[h], n)
                    if h == 0:
                        if past(n - 1):
                            pe.wait_ge(y_copied, n - 1)
                    for c in range(HALF[h] // 128):
                        c0 = KT * 2 * FF + (HEAD[h] // 128 + c) * DIM
                        last = split_product(Lb[3][:, 0:DIM], [a[:, c * 128:(c + 1) * 128] for a in atb[h]],
                                             col + c0, DIM, h == 0 and c == 0, h == 1 and c == HALF[1] // 128 - 1)
                    if h == 1:
                        last.then_inc(y_ready, 1)

                def body(j, par, at_):
                    col = pe.value_load(col_tab[0:1, row_of(j, at_)], min_val=0, max_val=(RING - 1) * EXPERT_COLS)
                    need = pe.value_load(need_tab[0:1, row_of(j, at_)], min_val=1, max_val=EXPERTS)
                    pe.wait_ge(experts_ready, need)
                    gate_up(par, 0, j + 1, col)
                    if at_ is None or at_ > 0:
                        before_ = pe.value_load(col_tab[0:1, row_of(j - 1, at_)],
                                                min_val=0, max_val=(RING - 1) * EXPERT_COLS)
                        transpose_act(1, j)
                        down(0, j, before_)
                    if at_ is None or at_ + 1 < TILES:
                        transpose_tile(1 - par, j + 2)
                    gate_up(par, 1, j + 1, col)
                    transpose_act(0, j + 1)
                    if at_ is None or at_ > 0:
                        down(1, j, before_)

                pe.wait_ge(plan_ready, 1)
                transpose_tile(0, 1)
                pair(pe, body, 0, TILES - 1, 2)
                body(TILES - 1, (TILES - 1) % 2, TILES - 1)
                col = pe.value_load(col_tab[0:1, TILES - 1:TILES], min_val=0, max_val=(RING - 1) * EXPERT_COLS)
                transpose_act(1, TILES)
                down(0, TILES, col)
                down(1, TILES, col)

        def groups(eng, body):
            for g in range(2):
                body(g, g % 2, g)
            with eng.Fori(2, GROUPS - 3, 2) as g:
                body(g, 0, None)
                body(g + 1, 1, None)
            for g in range(GROUPS - 2, GROUPS):
                body(g, g % 2, g)

        def group_rows(at_):
            return LAST_ROWS if at_ == GROUPS - 1 else ROWS

        with nc.Block() as block:
            @block.gpsimd
            def _(pool):
                for i in range(2):
                    pool.wait_ge(y_stored[i], 16 * (TILES // 2 + (TILES % 2) * (1 - i)))

                def body(g, par, at_):
                    rows = group_rows(at_)
                    if past(2 * g - 2):
                        pool.wait_ge(summed, 2 * g - 2)
                    P.tensor_copy(cidx[par][0:rows], slot_all[0:rows, row_of(g, at_)].rearrange("p o k -> p (o k)"))\
                     .then_inc(idx_ready, 1)
                    pool.wait_ge(idx_ready, alone(pool, g + 1))
                    for k in range(2):
                        P.indirect_dma_start(yg[k][par][0:rows], None, ys,
                                             bass.IndirectOffsetOnAxis(cidx[par][0:rows, k:k + 1], 0))\
                         .then_inc(gathered[par], 16)

                groups(pool, body)

            @block.sync
            def _(sp):
                for i in range(2):
                    sp.wait_ge(res_stored[i], 8 * GROUPS)
                    sp.wait_ge(y_stored[i], 16 * (TILES // 2 + (TILES % 2) * (1 - i)))

                def load(g, par, at_):
                    rows = group_rows(at_)
                    sp.dma_start(bt[par][0:rows], residual[row_of(g * ROWS, at_, rows), :]).then_inc(base_loaded[par], 16)

                def body(g, par, at_):
                    rows = group_rows(at_)
                    if at_ is None or at_ + 1 < GROUPS:
                        if past(2 * g):
                            sp.wait_ge(summed, 2 * g)
                        load(g + 1, 1 - par, None if at_ is None else at_ + 1)
                    sp.wait_ge(out_ready, g + 1)
                    sp.dma_start(out[row_of(g * ROWS, at_, rows), :], ob[par][0:rows]).then_inc(out_stored[par], 16)

                load(0, 0, 0)
                groups(sp, body)
                for i in range(2):
                    sp.wait_ge(out_stored[i], 8 * GROUPS)

            @block.scalar
            def _(act):
                def body(g, par, at_):
                    rows = group_rows(at_)
                    n = g + 1
                    act.wait_ge(r_aggr, GROUPS + n)
                    q = nrm[2]
                    A.activation(q[0:rows, 1:2], mv[0:rows, 1:2], ACT.Ln, bias=eps[0:rows, 0:1]).then_inc(n_ln[2], 1)
                    act.wait_ge(n_ln[2], GROUPS + n)
                    A.activation(q[0:rows, 2:3], q[0:rows, 1:2], ACT.Exp, scale=-0.5).then_inc(n_y0[2], 1)

                A.preload_act_table_set("natural_log_exp_and_others")
                groups(act, body)

            @block.vector
            def _(dve):
                def body(g, par, at_):
                    rows = group_rows(at_)
                    n = g + 1
                    gs = row_of(g, at_)
                    dve.wait_ge(base_loaded[par], 8 * g + 16 - 8 * par)
                    dve.wait_ge(gathered[par], 16 * g + 32 - 16 * par)
                    for k in range(2):
                        if k:
                            dve.wait_ge(summed, 2 * n - 1)
                        V.scalar_tensor_tensor(acc[par][0:rows], yg[k][par][0:rows],
                                               w_all[0:rows, gs, k:k + 1].rearrange("p o k -> p (o k)"),
                                               (acc if k else bt)[par][0:rows], ALU.mult, ALU.add).then_inc(summed, 1)
                    dve.wait_ge(summed, 2 * n)
                    V.bn_stats(st[0:rows], acc[par][0:rows]).then_inc(r_stat, 1)
                    dve.wait_ge(r_stat, alone(dve, GROUPS + n))
                    V.bn_aggr(mv[0:rows], st[0:rows]).then_inc(r_aggr, 1)
                    dve.wait_ge(r_aggr, GROUPS + n)
                    q, m = nrm[2][0:rows], 4 * (GROUPS + n)
                    V.tensor_scalar(q[:, 3:4], mv[0:rows, 1:2], LN_EPS, None, ALU.add).then_inc(n_dve[2], 1)
                    dve.wait_ge(n_y0[2], GROUPS + n)
                    dve.wait_ge(n_dve[2], m - 3)
                    V.scalar_tensor_tensor(q[:, 4:5], q[:, 2:3], q[:, 2:3], q[:, 3:4], ALU.mult, ALU.mult).then_inc(n_dve[2], 1)
                    dve.wait_ge(n_dve[2], m - 2)
                    V.tensor_scalar(q[:, 5:6], q[:, 4:5], -0.5, 1.5, ALU.mult, ALU.add).then_inc(n_dve[2], 1)
                    dve.wait_ge(n_dve[2], m - 1)
                    V.tensor_tensor(q[:, 6:7], q[:, 5:6], q[:, 2:3], ALU.mult).then_inc(n_dve[2], 1)
                    dve.wait_ge(n_dve[2], m)
                    if past(8 * g - 8 * par):
                        dve.wait_ge(out_stored[par], 8 * g - 8 * par)
                    V.tensor_scalar(ob[par][0:rows], acc[par][0:rows], mv[0:rows, 0:1], q[:, 6:7],
                                    ALU.subtract, ALU.mult).then_inc(out_ready, 1)

                groups(dve, body)


def kernel(**inputs):
    import numpy as np
    import concourse.bacc as bacc
    from concourse.bass_utils import run_bass_kernel_spmd

    given = {k: np.asarray(v) for k, v in inputs.items()}
    rows = lambda v: np.ascontiguousarray(np.broadcast_to(v, (ROWS, v.shape[-1])))
    tiles = lambda w: np.ascontiguousarray(w.reshape(-1, 128, w.shape[1]).transpose(1, 0, 2))

    x, p = given["x"], 16
    x = x.reshape(IMAGES, 3, 6, p, 6, p).transpose(1, 3, 5, 0, 2, 4).reshape(PATCH_DIM, TOKENS)
    fill = GROUPS * ROWS - TOKENS
    x = np.concatenate([x, x[:, :fill]], 1)
    patches = np.ascontiguousarray(x.reshape(PT_TILES, 128, GROUPS, ROWS).transpose(1, 2, 0, 3)
                                   .reshape(128, GROUPS, PT_TILES * ROWS))

    rep = lambda w: np.repeat(w.reshape(DIM, 8, 1, HD), 2, 2).reshape(DIM, DIM)
    slots = np.arange(HEADS).reshape(2, 2, 4).transpose(1, 0, 2).reshape(-1)
    by_slot = (slots[:, None] * HD + np.arange(HD)).reshape(-1)
    bq, bk, bv = given["L0_ffn_wq"], rep(given["L0_ffn_wk"]), rep(given["L0_ffn_wv"])
    gate, up, down = (given[f"L0_ffn_w_{n}"] for n in ("gate", "up", "down"))
    gu = np.stack([gate, up], 2).reshape(EXPERTS, KT, 128, 2 * FF).transpose(2, 0, 1, 3).reshape(128, EXPERTS, -1)
    dn = down.reshape(EXPERTS, DOWN_TILES, 128, DIM).transpose(2, 0, 1, 3).reshape(128, EXPERTS, -1)

    f = np.float32
    row, ch, q = np.arange(ROWS), np.arange(128), np.arange(ROWS) % SEQ
    headmask4 = (ch[:, None] % 64 // HD == np.arange(4)).astype(f)
    headmask3 = (row[:, None] // SEQ == np.arange(HEADS) % 3).astype(f)
    imagemask = (row[:, None] // SEQ == np.arange(IPG)).astype(f)
    d = np.arange(SEQ)[None] - q[:, None]
    window = ((d <= 31) & (d >= -32)).astype(f)[:, [0, 1, 2, 32, 33, 34, 35]]
    causal = np.where(d <= 0, f(0), f(-3e38)).astype(f)
    inv = (f(1) / f(10000.0) ** (np.arange(0, HD, 2, dtype=f) / f(HD))).astype(f)
    ang = (np.arange(128) % SEQ).astype(f)[None] * inv[ch % 8][:, None]
    rotate = np.zeros((128, 128), f)
    for m in range(128):
        rotate[m + 8 if m % HD < 8 else m - 8, m] = -1 if m % HD < 8 else 1
    scaled = lambda t: np.stack([t * f(HD ** -0.5), t], 1)
    cols = [k % RING * EXPERT_COLS for k in range(EXPERTS)]
    col_step = np.array([[b - a for a, b in zip(cols, cols[1:])] + [0]], f)
    e = np.arange(EXPERTS)
    args = dict(
        col_step=col_step,
        patches=patches, tok_w=tiles(given["L0_tok_W"].T), tok_b=rows(given["L0_tok_b"]),
        pos=np.ascontiguousarray(np.tile(given["L0_tok_pos_embd"][0], (IPG, 1))),
        a_wqk=tiles(np.concatenate([given["L0_attn_Wq"], given["L0_attn_Wk"]], 1)),
        a_wv=tiles(given["L0_attn_Wv"][:, by_slot]), a_wo=tiles(given["L0_attn_Wo"][by_slot]),
        b_wqk=tiles(np.concatenate([bq, bk], 1)), b_wv=tiles(bv[:, by_slot]), b_wo=tiles(given["L0_ffn_wo"][by_slot]),
        ln1=rows(given["L0_ffn_ln1_w"]), ln2=rows(given["L0_ffn_ln2_w"]), router=tiles(given["L0_ffn_router_w"]),
        expert_w=np.ascontiguousarray(np.concatenate([gu, dn], 2)),
        headmask4=headmask4, headmask3=headmask3, imagemask=imagemask, window=window, causal=causal,
        rope_cos=scaled(np.cos(ang).astype(f)), rope_sin=scaled(np.sin(ang).astype(f)), rotate=rotate,
        identity=np.eye(128, dtype=f), lower=(row[:, None] < row[None]).astype(f),
        expert_iota=np.tile(e.astype(f), (128, 1)), region_base=np.tile((e * REGION).astype(f), (128, 1)),
        thresholds=np.tile((np.arange(TOKENS // TILE) * TILE).astype(f), (128, 1)), tile_ids=np.arange(TILES, dtype=f)[None],
        before=np.tile((e[None] <= e[:, None]).astype(f), (128, 1, 1)), partition_ids=np.arange(128, dtype=f)[:, None],
    )
    nc = bacc.Bacc("TRN2", target_bir_lowering=False, num_devices=1)
    aps = {n: nc.dram_tensor(f"in_{n}", a.shape, mybir.dt.from_np(a.dtype), kind="ExternalInput").ap()
           for n, a in args.items()}
    out = nc.dram_tensor("out", (TOKENS, DIM), mybir.dt.float32, kind="ExternalOutput").ap()
    program(nc, out=out, **aps)
    r = run_bass_kernel_spmd(nc, [{f"in_{n}": a for n, a in args.items()}], core_ids=[0])
    return r.results[0]["out"].reshape(IMAGES, SEQ, DIM)
```

```python
import concourse.bass as bass
from concourse import mybir
from contextlib import ExitStack

IMAGES, SEQ, DIM, HEADS, HD = 64, 36, 256, 16, 16
PATCH_DIM = 768
FF, EXPERTS = 896, 8
IPG = 3
ROWS = IPG * SEQ
GROUPS = -(-IMAGES // IPG)
LAST_ROWS = (IMAGES - IPG * (GROUPS - 1)) * SEQ
TOKENS = IMAGES * SEQ
KT = DIM // 128
PT_TILES = PATCH_DIM // 128
TILE = 128
TILES = (2 * TOKENS + EXPERTS * (TILE - 1)) // TILE
REGION = TOKENS + TILE
EMBED_FIRST = 3
SPARE_TILES = TILES - 2 * TOKENS // TILE
XS_ROWS = EXPERTS * REGION + SPARE_TILES * TILE
CHUNKS = 6
CH = 3 * SEQ
DOWN_TILES = FF // 128
EXPERT_COLS = KT * 2 * FF + DOWN_TILES * DIM
HALF = (512, FF - 512)
RING = 3
RAW = 2
FIRST_COLS = KT * 2 * FF
OUT_TILES = TOKENS // TILE
assert OUT_TILES * TILE == TOKENS
WORK_COLS = 20992
LN_EPS, RMS_EPS = 1e-5, 1e-6
PEEL = 6
STEPS = GROUPS + 5
LOOP_END = GROUPS - 2


def program(nc, patches, tok_w, tok_b, pos, a_wqk, a_wv, a_wo, b_wqk, b_wv, b_wo, ln1, ln2, router,
            expert_w, headmask4, headmask3, imagemask, window, causal, rope_cos, rope_sin, rotate,
            identity, lower, expert_iota, region_base, thresholds, tile_ids, before, col_step,
            out):
    f32, bf16, u32 = mybir.dt.float32, mybir.dt.bfloat16, mybir.dt.uint32
    f32r = mybir.dt.float32r
    ALU, ACT, AX = mybir.AluOpType, mybir.ActivationFunctionType, mybir.AxisListType
    V, P, T, A = nc.vector, nc.gpsimd, nc.tensor, nc.scalar
    xs = nc.dram_tensor("expert_rows_in", [XS_ROWS, DIM], f32, kind="Internal").ap()
    ys = nc.dram_tensor("expert_rows_out", [TILES * TILE, DIM], f32, kind="Internal").ap()
    routing = nc.dram_tensor("routing", [GROUPS * ROWS, 6], f32, kind="Internal").ap()
    residual = nc.dram_tensor("residual", [GROUPS * ROWS, DIM], f32, kind="Internal").ap()

    ctx = ExitStack()
    with ctx:
        def sb(name, shape, dt=f32):
            return ctx.enter_context(nc.sbuf_tensor(name, shape, dt))

        def sem(name):
            return ctx.enter_context(nc.semaphore(name))

        xa = [sb(f"xa_{i}", [128, DIM]) for i in range(2)]
        hb, h1, rr = sb("hb", [128, DIM]), sb("h1", [128, DIM]), sb("rr", [128, DIM])
        hc = [sb(f"hc_{i}", [128, DIM]) for i in range(2)]
        h2 = [sb(f"h2_{i}", [128, DIM]) for i in range(2)]
        res = [sb(f"res_{i}", [128, DIM]) for i in range(2)]
        kk = sb("kk", [128, KT, ROWS])
        junk = sb("junk", [128, DIM])
        ident = sb("ident", [128, 128])
        low, eio, rb = sb("low", [128, ROWS]), sb("eio", [128, EXPERTS]), sb("rb", [128, EXPERTS])
        lowb, oneb = sb("lowb", [128, ROWS], bf16), sb("oneb", [128, 128], bf16)
        mx, sm, ri = ([sb(f"{n}{i}", [128, HEADS]) for i in range(2)] for n in ("mx", "sm", "ri"))
        info = sb("info", [128, GROUPS, 6])
        w_all, place_all, exp_all = (info[:, :, c:c + 2] for c in (0, 2, 4))
        info_t = sb("info_t", [128, OUT_TILES, 6])
        slot_all = sb("slot_all", [128, OUT_TILES, 2], u32)
        eps = sb("eps", [128, 2])
        nil = sb("nil", [128, 1])
        st = sb("st", [128, 6])
        mv = sb("mv", [128, 2])
        nrm = [sb(f"nrm{i}", [128, 8]) for i in range(3)]
        top, topi = sb("top", [128, 8]), sb("topi", [128, 8], u32)
        topf = sb("topf", [128, 2])
        rt = sb("rt", [128, 8])
        oh = sb("oh", [128, 2, EXPERTS])
        cnt, cntb = sb("cnt", [128, EXPERTS]), sb("cntb", [128, EXPERTS], bf16)
        tot, totb = sb("tot", [128, EXPERTS]), sb("totb", [128, EXPERTS], bf16)
        place, hit = sb("place", [128, EXPERTS]), sb("hit", [128, 2, EXPERTS])
        slotf, slot = sb("slotf", [128, 2]), [sb(f"slot{i}", [128, 2], u32) for i in range(2)]

        raw = [sb(f"raw{i}", [128, EXPERT_COLS]) for i in range(RAW)]

        X, Y = (ctx.enter_context(nc.psum_tensor(n, [128, 2, 512], f32)) for n in ("X", "Y"))
        Lb = [ctx.enter_context(nc.psum_tensor(f"L{i}", [128, 512], f32)) for i in range(4)]
        S, L = [X, Y], Lb[0:2]

        names = ("x_t", "xt", "qk", "v", "qm", "kx", "vs", "vrep", "vx", "s", "mx", "z", "e", "sm", "ri",
                 "p_t", "pt", "o", "o0", "osel", "on", "o_t", "ot", "y")
        AB = [{n: sem(f"{'ab'[i]}_{n}") for n in names} for i in range(2)]
        consts_loaded, setup_dve, setup_pool = sem("consts_loaded"), sem("setup_dve"), sem("setup_pool")
        tokw_loaded = sem("tokw_loaded")
        pat_high, pat_low = sem("pat_high"), sem("pat_low")
        pat_loaded = [sem(f"pat_loaded{i}") for i in range(2)]
        embedded, x_ready = sem("embedded"), sem("x_ready")
        e1_done, masked = sem("e1_done"), sem("masked")
        r_res, r_stat, r_aggr, h1_ready = sem("r_res"), sem("r_stat"), sem("r_aggr"), sem("h1_ready")
        n_sq = [sem(f"n_sq{i}") for i in range(3)]
        n_ln = [sem(f"n_ln{i}") for i in range(3)]
        n_y0 = [sem(f"n_y0{i}") for i in range(3)]
        n_dve = [sem(f"n_dve{i}") for i in range(3)]
        hb_ready, qk_copied, rotated = sem("hb_ready"), sem("qk_copied"), sem("rotated")
        by_cos, by_sin, kk_ready = sem("by_cos"), sem("by_sin"), sem("kk_ready")
        rr_ready, res_ready, h2_ready = sem("rr_ready"), sem("res_ready"), sem("h2_ready")
        res_stored = [sem(f"res_stored{i}") for i in range(2)]
        h2_t, h2t, logits = sem("h2_t"), sem("h2t"), sem("logits")
        top_d, top_i, gap, gap_exp = sem("top_d"), sem("top_i"), sem("gap"), sem("gap_exp")
        gate_sum, index_float, gate_inv, one_hot = sem("gate_sum"), sem("index_float"), sem("gate_inv"), sem("one_hot")
        count_float, counted, ranked = sem("count_float"), sem("counted"), sem("ranked")
        placed, total_float, totalled, hits = sem("placed"), sem("total_float"), sem("totalled"), sem("hits")
        slot_sum, slots_ready, late_loaded, causal_done = sem("slot_sum"), sem("slots_ready"), sem("late_loaded"), sem("causal_done")
        scattered = [sem(f"scattered{i}") for i in range(2)]
        expert_loaded = [sem(f"expert_loaded{e}") for e in range(RAW)]
        counts_ready, tail_slots, zeroed = sem("counts_ready"), sem("tail_slots"), sem("zeroed")
        plan, plan_ready, experts_ready = sem("plan"), sem("plan_ready"), sem("experts_ready")
        high_part = sem("high_part")
        x_loaded = [sem(f"x_loaded{i}") for i in range(2)]
        mt, mxh, mxt = sem("mt"), sem("mxh"), sem("mxt")
        ath = [sem(f"ath{i}") for i in range(2)]
        gu, sg, ac, a_t, at = ([sem(f"{n}{i}") for i in range(2)] for n in ("gu", "sg", "ac", "a_t", "at"))
        y_ready, y_copied = sem("y_ready"), sem("y_copied")
        y_stored = [sem(f"y_stored{i}") for i in range(2)]
        idx_ready, summed = sem("idx_ready"), sem("summed")
        gathered = [sem(f"gathered{i}") for i in range(2)]
        spare_zeroed, base_loaded, info_moved, slots_moved, rows_ready = (sem(n) for n in ("spare_zeroed", "base_loaded", "info_moved", "slots_moved", "rows_ready"))
        out_ready, out_stored = sem("out_ready"), sem("out_stored")
        refined = sem("refined")
        xt_low, ot_low = ([sem(f"{n}_low{l}") for l in range(2)] for n in ("xt", "ot"))

        def past(value):
            return not isinstance(value, int) or value > 0

        def alone(eng, value):
            value = value if isinstance(value, int) else eng.compute_val(value)
            eng.wait_ge(setup_dve, 1)
            return value

        def bc(ap, dim, shape):
            return ap.unsqueeze(dim).to_broadcast(shape)

        def row_of(at, step, n=1):
            return bass.ds(at, n) if step is None else slice(at, at + n)

        E4 = [ROWS, HEADS, SEQ]
        xg = xa
        sgb = [sb("sg0", [128, HALF[0]]), sb("sg1", [128, HALF[1]])]
        acb = [sb("ac0", [128, HALF[0]]), sb("ac1", [128, HALF[1]])]
        yb = [rr, hc[0]]
        zero = sb("zero", [128, DIM])
        tails = sb("tails", [1, EXPERTS], u32)
        tailf = sb("tailf", [128, EXPERTS])
        thr, tid, bef = sb("thr", [128, TOKENS // TILE]), sb("tid", [1, TILES]), sb("bef", [128, EXPERTS, EXPERTS])
        over, nt = sb("over", [128, EXPERTS, TOKENS // TILE]), sb("nt", [128, EXPERTS])
        pre, cum = sb("pre", [128, EXPERTS, EXPERTS]), sb("cum", [128, EXPERTS])
        shift = sb("shift", [128, EXPERTS])
        own = sgb[0][:, 0:2 * OUT_TILES * EXPERTS].rearrange("p (g e) -> p g e", e=EXPERTS)
        moved = sb("moved", [128, OUT_TILES, 2])
        ge, gt = (x[0:1, 0:TILES * EXPERTS].rearrange("p (j e) -> p j e", e=EXPERTS) for x in (sgb[0], acb[0]))
        te, tb, tl, tr, tw = (sb(f"t_{n}", [1, TILES]) for n in ("e", "b", "l", "r", "w"))
        row_tab, col_tab, need_tab = (sb(n, [1, TILES], u32) for n in ("row_tab", "col_tab", "need_tab"))
        cstep, end_tab = sb("cstep", [1, EXPERTS]), sb("end_tab", [1, EXPERTS], u32)
        endf = sb("endf", [1, EXPERTS])
        attention = ctx.enter_context(ExitStack())
        work = attention.enter_context(nc.sbuf_tensor("work", [128, WORK_COLS], f32))
        used = [0]

        def parts(name, *free):
            return [attention.enter_context(nc.sbuf_tensor(f"{name}_{p}", [128, *free], f32r)) for p in ("high", "low")]

        pat_parts = [parts(f"pat{i}", PT_TILES, ROWS) for i in range(2)]
        tokw_parts = parts("tokw", PT_TILES, DIM)
        xt_parts, ot_parts = ([parts(f"{n}{l}", KT, ROWS) for l in range(2)] for n in ("xt", "ot"))
        wv_parts, wo_parts = ([parts(f"{n}{l}", KT, DIM) for l in range(2)] for n in ("wv", "wo"))

        def early(*free):
            n = 1
            for f in free:
                n *= f
            v = work[:, used[0]:used[0] + n]
            used[0] += n
            assert used[0] <= WORK_COLS
            names = " ".join(f"d{i}" for i in range(len(free)))
            return v.rearrange(f"p ({names}) -> p {names}", **{f"d{i}": f for i, f in enumerate(free)})

        pat = [early(PT_TILES, ROWS) for _ in range(2)]
        tokw = raw[0][:, 0:PT_TILES * DIM].rearrange("p (t d) -> p t d", d=DIM)
        wv, wo = ([raw[0][:, (PT_TILES + KT * (2 * i + l)) * DIM:(PT_TILES + KT * (2 * i + l + 1)) * DIM]
                   .rearrange("p (t d) -> p t d", d=DIM) for l in range(2)] for i in range(2))
        wqk = [early(KT, 512) for _ in range(2)]
        to_split = [(tokw, tokw_parts)] + [(w[l], p[l]) for l in range(2) for w, p in ((wv, wv_parts), (wo, wo_parts))]
        qm = [early(KT, IPG, ROWS) for _ in range(2)]
        vrep = [early(IPG, DIM) for _ in range(2)]
        vx = [early(IPG, CHUNKS * 48) for _ in range(2)]
        kx = [early(KT, 4, ROWS) for _ in range(2)]
        z = [early(HEADS, SEQ) for _ in range(2)]
        pr = [early(CHUNKS * CH) for _ in range(2)]
        posb, tokb, ln1w, ln2w = early(DIM), early(DIM), early(DIM), early(DIM)
        qk_sb, qk_cos, qk_sin = early(512), early(512), early(512)
        hm4, hm3, imk, win, cau = early(4), early(HEADS), early(IPG), early(7), early(SEQ)
        cosT, sinT, rotm = early(2, 128), early(2, 128), early(128)
        routw = early(KT, EXPERTS)
        xt = [early(KT, 128) for _ in range(3)]
        ot = [early(KT, ROWS) for _ in range(2)]
        vs = [early(DIM) for _ in range(2)]
        pt = [early(CHUNKS, ROWS) for _ in range(2)]
        sel = [early(3, CHUNKS * 48) for _ in range(2)]

        consts = [(wqk[0], a_wqk), (ident[:], identity), (tokb[0:ROWS], tok_b), (posb[0:ROWS], pos), (wv[0], a_wv),
                  (hm4, headmask4), (hm3[0:ROWS], headmask3), (imk[0:ROWS], imagemask), (low[0:ROWS], lower)]
        late_consts = [(wo[0], a_wo), (win[0:ROWS], window), (wqk[1], b_wqk), (wv[1], b_wv), (ln1w[0:ROWS], ln1),
                       (cosT, rope_cos), (sinT, rope_sin), (rotm, rotate), (wo[1], b_wo), (cau[0:ROWS], causal),
                       (ln2w[0:ROWS], ln2), (routw, router), (eio[:], expert_iota), (rb[:], region_base),
                       (thr[:], thresholds), (tid[:], tile_ids), (bef[:], before), (cstep[:], col_step)]

        def steps(eng, body):
            for s in range(PEEL):
                if s == 1:
                    eng.wait_ge(late_loaded, 16 * len(late_consts))
                body(s, s % 2, s)
            with eng.Fori(PEEL, LOOP_END - 1, 2) as s:
                body(s, 0, None)
                body(s + 1, 1, None)
            for s in range(LOOP_END, STEPS):
                body(s, s % 2, s)

        def split_count(g):
            return g - EMBED_FIRST + 1 + len(to_split)

        def live(step, lag):
            return step is None or lag <= step < GROUPS + lag

        def last_rows(step, lag):
            return LAST_ROWS if step == GROUPS - 1 + lag else ROWS

        with nc.Block() as block:
            @block.sync
            def _(sp):
                sp.dma_start(pat[0], patches[:, 0:1].rearrange("p o (t r) -> p (o t) r", r=ROWS)).then_inc(pat_loaded[0], 16)
                sp.dma_start(tokw, tok_w).then_inc(tokw_loaded, 16)
                sp.dma_start(pat[1], patches[:, 1:2].rearrange("p o (t r) -> p (o t) r", r=ROWS)).then_inc(pat_loaded[1], 16)
                for dst, src in consts[0::2]:
                    sp.dma_start(dst, src).then_inc(consts_loaded, 16)
                for dst, src in late_consts[0::2]:
                    sp.dma_start(dst, src).then_inc(late_loaded, 16)

                def spread_v(l):
                    for h in range(3):
                        for b in range(IPG):
                            sp.dma_start(vrep[l][SEQ * h:SEQ * (h + 1), b],
                                         vs[l][SEQ * b:SEQ * (b + 1)]).then_inc(AB[l]["vrep"], 16)

                def body(s, par, step):
                    if step is None or step + 2 < GROUPS:
                        if step is None or step >= EMBED_FIRST:
                            sp.wait_ge(pat_low, split_count(s))
                        else:
                            sp.wait_ge(embedded, s + 1)
                        sp.dma_start(pat[par], patches[:, row_of(s + 2, step)].rearrange("p o (t r) -> p (o t) r", r=ROWS))\
                          .then_inc(pat_loaded[par], 16)
                    if live(step, 4):
                        sp.wait_ge(res_ready, s - 3)
                        sp.dma_start(residual[row_of((s - 4) * ROWS, step, ROWS), :], res[par][0:ROWS]).then_inc(res_stored[par], 16)
                    if live(step, 0):
                        sp.wait_ge(AB[0]["vs"], s + 1)
                        if past(s):
                            sp.wait_ge(AB[0]["vx"], s)
                        spread_v(0)
                    if live(step, 2):
                        now, before_it = alone(sp, s - 1), alone(sp, s - 2)
                        sp.wait_ge(AB[1]["vs"], now)
                        if past(before_it):
                            sp.wait_ge(AB[1]["vx"], before_it)
                        spread_v(1)

                steps(sp, body)

            @block.gpsimd
            def _(pool):
                P.memset(nil[:], 0.0)
                for l in range(2):
                    P.memset(vx[l], 0.0).then_inc(setup_pool, 1)
                    P.memset(pr[l], 0.0).then_inc(setup_pool, 1)
                    P.memset(qm[l], 0.0).then_inc(setup_pool, 1)
                for i in range(3):
                    P.memset(xt[i], 0.0).then_inc(setup_pool, 1)
                P.memset(zero[:], 0.0).then_inc(setup_pool, 1)
                pool.wait_ge(setup_pool, 10)
                pool.wait_ge(consts_loaded, 16 * len(consts))

                def expand_v(l, n):
                    pool.wait_ge(AB[l]["vrep"], 144 * n)
                    if past(n - 1):
                        pool.wait_ge(AB[l]["o"], n - 1)
                    shape = [ROWS, IPG, HEADS, HD]
                    P.tensor_tensor(vx[l][0:ROWS, :, 0:DIM].rearrange("p b (h d) -> p b h d", d=HD),
                                    vrep[l][0:ROWS].rearrange("p b (h d) -> p b h d", d=HD),
                                    hm3[0:ROWS].unsqueeze(1).unsqueeze(3).to_broadcast(shape),
                                    ALU.mult).then_inc(AB[l]["vx"], 1)

                def low_x(l, n):
                    pool.wait_ge(AB[l]["xt"], 2 * n)
                    P.tensor_tensor(xt_parts[l][1][:], xt[l][:, :, 0:ROWS], xt_parts[l][0][:], ALU.subtract).then_inc(xt_low[l], 1)

                def low_o(l, n):
                    pool.wait_ge(AB[l]["ot"], 2 * n)
                    P.tensor_tensor(ot_parts[l][1][:], ot[l], ot_parts[l][0][:], ALU.subtract).then_inc(ot_low[l], 1)

                def body(s, par, step):
                    if live(step, 4):
                        low_o(1, s - 3)
                    if live(step, 3):
                        expand_v(1, s - 2)
                    if live(step, 0):
                        low_x(0, s + 1)
                    if live(step, 3):
                        pool.wait_ge(AB[1]["mx"], s - 2)
                        P.tensor_tensor(z[1][0:ROWS], z[1][0:ROWS], bc(mx[1][0:ROWS], 2, E4), ALU.subtract)\
                         .then_inc(AB[1]["z"], 1)
                    if live(step, 2):
                        if past(s - 3):
                            pool.wait_ge(res_ready, s - 3)
                        pool.wait_ge(h1_ready, s - 1)
                        P.tensor_tensor(hc[par][0:ROWS], h1[0:ROWS], nil[0:ROWS].to_broadcast([ROWS, DIM]), ALU.add)\
                         
                    if live(step, 2):
                        low_x(1, s - 1)
                    if live(step, 5):
                        rows = last_rows(step, 5)
                        pool.wait_ge(slots_ready, alone(pool, s - 4))
                        for k in range(2):
                            P.indirect_dma_start(xs, bass.IndirectOffsetOnAxis(slot[1 - par][0:rows, k:k + 1], 0),
                                                 h2[1 - par][0:rows], None).then_inc(scattered[1 - par], 16)
                    if live(step, 2):
                        pool.wait_ge(qk_copied, s - 1)
                        P.tensor_tensor(qk_cos.rearrange("p (w j t) -> p w j t", w=2, j=2),
                                        qk_sb.rearrange("p (w j t) -> p w j t", w=2, j=2),
                                        bc(cosT, 2, [128, 2, 2, 128]), ALU.mult).then_inc(by_cos, 1)
                    if live(step, 0):
                        expand_v(0, s + 1)
                    if live(step, 1):
                        low_o(0, s)
                    if live(step, 2):
                        pool.wait_ge(kk_ready, s - 1)
                        for t in range(KT):
                            P.tensor_tensor(kx[1][:, t], bc(kk[:, t], 1, [128, 4, ROWS]), bc(hm4, 2, [128, 4, ROWS]),
                                            ALU.mult).then_inc(AB[1]["kx"], 1)
                    if step == 1:
                        pool.wait_ge(tokw_loaded, 16)
                        for i, (w, w_parts) in enumerate(to_split):
                            pool.wait_ge(pat_high, i + 1)
                            P.tensor_tensor(w_parts[1][:], w, w_parts[0][:], ALU.subtract).then_inc(pat_low, 1)
                    if step is None or EMBED_FIRST <= step + 2 < GROUPS:
                        pool.wait_ge(pat_high, split_count(s + 2))
                        P.tensor_tensor(pat_parts[par][1][:], pat[par], pat_parts[par][0][:],
                                        ALU.subtract).then_inc(pat_low, 1)
                    if step == 3:
                        pool.wait_ge(AB[0]["v"], 3)
                        pool.wait_ge(AB[1]["v"], 1)
                        pool.wait_ge(AB[0]["y"], 2)
                        pool.wait_ge(pat_low, len(to_split))
                        for e in range(RAW):
                            pool.dma_start(raw[e][:], expert_w[:, e]).then_inc(expert_loaded[e], 16)
                    if step is not None and step >= LOOP_END:
                        for i in range(step - LOOP_END, SPARE_TILES, STEPS - LOOP_END):
                            r0 = EXPERTS * REGION + i * TILE
                            pool.dma_start(xs[r0:r0 + TILE, :], zero[:]).then_inc(spare_zeroed, 16)

                steps(pool, body)

            @block.scalar
            def _(act):
                for dst, src in consts[1::2]:
                    act.dma_start(dst, src).then_inc(consts_loaded, 16)
                for dst, src in late_consts[1::2]:
                    act.dma_start(dst, src).then_inc(late_loaded, 16)
                A.preload_act_table_set("natural_log_exp_and_others")
                act.wait_ge(consts_loaded, 16 * len(consts))
                act.wait_ge(setup_pool, 9)
                act.wait_ge(setup_dve, 1)

                def inv_sqrt(i, src, n, rows=ROWS):
                    if i != 2:
                        A.activation(junk[0:rows], src, ACT.Square, accum_out=nrm[i][0:rows, 0:1]).then_inc(n_sq[i], 1)
                        act.wait_ge(n_sq[i], n)
                        A.activation(nrm[i][0:rows, 1:2], nrm[i][0:rows, 0:1], ACT.Ln, bias=eps[0:rows, 1:2],
                                     scale=1.0 / DIM).then_inc(n_ln[i], 1)
                    else:
                        A.activation(nrm[i][0:rows, 1:2], mv[0:rows, 1:2], ACT.Ln, bias=eps[0:rows, 0:1]).then_inc(n_ln[i], 1)
                    act.wait_ge(n_ln[i], n)
                    A.activation(nrm[i][0:rows, 2:3], nrm[i][0:rows, 1:2], ACT.Exp, scale=-0.5).then_inc(n_y0[i], 1)

                def xt_copy(i, ps, ready, n, done, rows=ROWS):
                    if i < 2 and past(n - 1):
                        act.wait_ge(xt_low[i], n - 1)
                    act.wait_ge(ready, n)
                    A.activation(xt[i][:, :, 0:rows], ps[:, 0:KT * rows].rearrange("p (t r) -> p t r", t=KT),
                                 ACT.Copy).then_inc(done, 1)
                    if i < 2:
                        A.activation(xt_parts[i][0][:], ps[:, 0:KT * rows].rearrange("p (t r) -> p t r", t=KT),
                                     ACT.Copy).then_inc(done, 1)

                def diag(l):
                    v = qm[l].rearrange("p t b r -> p t (b r)")
                    return bass.AP(tensor=v.tensor, offset=v.offset,
                                   ap=[v.ap[0], [IPG * ROWS, KT], [ROWS + SEQ, IPG], [1, SEQ]])

                def exp_scores(l, n):
                    A.activation(pr[l][0:ROWS, 0:HEADS * SEQ].rearrange("p (h k) -> p h k", k=SEQ), z[l][0:ROWS],
                                 ACT.Exp).then_inc(AB[l]["e"], 1)

                def copy_pt(l, ps, n):
                    act.wait_ge(AB[l]["p_t"], n)
                    A.activation(pt[l][0:CH].rearrange("p (j c) r -> p j (c r)", j=2),
                                 ps[0:CH, :, 0:3 * ROWS], ACT.Copy).then_inc(AB[l]["pt"], 1)

                def first_image(l, ps, n):
                    act.wait_ge(AB[l]["o"], n)
                    A.activation(sel[l][0:ROWS, 0].rearrange("p (j d) -> p j d", j=2), ps[0:ROWS, :, 0:144],
                                 ACT.Copy, scale=imk[0:ROWS, 0:1]).then_inc(AB[l]["o0"], 1)

                def copy_ot(l, ps, n):
                    if past(n - 1):
                        act.wait_ge(ot_low[l], n - 1)
                    act.wait_ge(AB[l]["o_t"], n)
                    A.activation(ot[l], ps[:, 0:KT * ROWS].rearrange("p (t r) -> p t r", t=KT),
                                 ACT.Copy).then_inc(AB[l]["ot"], 1)
                    A.activation(ot_parts[l][0][:], ps[:, 0:KT * ROWS].rearrange("p (t r) -> p t r", t=KT),
                                 ACT.Copy).then_inc(AB[l]["ot"], 1)

                def body(s, par, step):
                    rrows = last_rows(step, 4)
                    if live(step, 1):
                        act.wait_ge(AB[0]["z"], s)
                        A.activation(z[0][0:ROWS], z[0][0:ROWS], ACT.Exp).then_inc(e1_done, 1)
                    if live(step, 2):
                        act.wait_ge(r_aggr, s - 1)
                        inv_sqrt(2, None, s - 1)
                    if live(step, 4):
                        copy_ot(1, Lb[1], s - 3)
                    if live(step, 1):
                        act.wait_ge(masked, 2 * s)
                        exp_scores(0, s)
                    if live(step, 2):
                        act.wait_ge(h1_ready, s - 1)
                        inv_sqrt(0, h1[0:ROWS], s - 1)
                    if live(step, 0):
                        xt_copy(0, Lb[0], AB[0]["x_t"], s + 1, AB[0]["xt"])
                    if live(step, 0):
                        act.wait_ge(AB[0]["qk"], s + 1)
                        A.activation(diag(0), Lb[3][:, 0:256].rearrange("p (t r) -> p t r", t=KT)[:, :, 0:ROWS]
                                     .rearrange("p t (b q) -> p t b q", b=IPG), ACT.Copy, scale=0.25)\
                         .then_inc(AB[0]["qm"], 1)
                    if live(step, 2):
                        xt_copy(1, Lb[2], AB[1]["x_t"], s - 1, AB[1]["xt"])
                    if live(step, 0):
                        if past(s):
                            act.wait_ge(AB[0]["vrep"], 144 * s)
                        act.wait_ge(AB[0]["v"], s + 1)
                        A.activation(vs[0][0:ROWS], Lb[0][0:ROWS, 0:DIM], ACT.Copy).then_inc(AB[0]["vs"], 1)
                    if live(step, 4):
                        act.wait_ge(rr_ready, s - 3)
                        inv_sqrt(1, rr[0:rrows], s - 3, rrows)
                    if live(step, 1):
                        copy_pt(0, X, s)
                    if live(step, 3):
                        act.wait_ge(AB[1]["z"], s - 2)
                        exp_scores(1, s - 2)
                    if live(step, 2):
                        act.wait_ge(AB[1]["qk"], s - 1)
                        A.activation(qk_sb, Lb[1][:], ACT.Copy).then_inc(qk_copied, 1)
                    if live(step, 1):
                        first_image(0, Y, s)
                    if live(step, 2):
                        if past(s - 2):
                            act.wait_ge(AB[1]["vrep"], 144 * s - 288)
                        act.wait_ge(AB[1]["v"], s - 1)
                        A.activation(vs[1][0:ROWS], Lb[2][0:ROWS, 0:DIM], ACT.Copy).then_inc(AB[1]["vs"], 1)
                    if live(step, 4):
                        xt_copy(2, Lb[3], h2_t, s - 3, h2t, rrows)
                    if live(step, 3):
                        copy_pt(1, X, s - 2)
                    if live(step, 3):
                        first_image(1, X, s - 2)
                    if live(step, 1):
                        copy_ot(0, Lb[0], s)
                    if step == 1:
                        for w, w_parts in to_split:
                            A.activation(w_parts[0][:], w, ACT.Copy).then_inc(pat_high, 1)
                    if step is None or EMBED_FIRST <= step + 2 < GROUPS:
                        if past(s):
                            act.wait_ge(embedded, s + 1)
                        act.wait_ge(pat_loaded[par], 8 * s + 32 - 8 * par)
                        A.activation(pat_parts[par][0][:], pat[par], ACT.Copy).then_inc(pat_high, 1)
                    if live(step, 4):
                        act.wait_ge(gap, s - 3)
                        A.activation(rt[0:rrows, 1:2], rt[0:rrows, 0:1], ACT.Exp).then_inc(gap_exp, 1)

                steps(act, body)

            @block.vector
            def _(dve):
                V.memset(eps[:, 0:1], LN_EPS)
                V.memset(oneb[:], 1.0)
                V.memset(tot[:], 0.0)
                V.memset(info[:], 0.0)
                V.memset(totb[:], 0.0)
                V.memset(eps[:, 1:2], RMS_EPS).then_inc(setup_dve, 1)
                dve.wait_ge(consts_loaded, 16 * len(consts))
                dve.wait_ge(setup_pool, 9)
                V.tensor_tensor(posb[0:ROWS], posb[0:ROWS], tokb[0:ROWS], ALU.add).then_inc(setup_dve, 1)
                V.tensor_copy(lowb[0:ROWS], low[0:ROWS]).then_inc(setup_dve, 1)
                dve.wait_ge(setup_dve, 3)

                def newton(i, n, rows=ROWS):
                    q = nrm[i][0:rows]
                    if i == 2:
                        V.tensor_scalar(q[:, 3:4], mv[0:rows, 1:2], LN_EPS, None, ALU.add).then_inc(n_dve[i], 1)
                    else:
                        dve.wait_ge(n_sq[i], n)
                        V.tensor_scalar(q[:, 3:4], q[:, 0:1], 1.0 / DIM, RMS_EPS, ALU.mult, ALU.add).then_inc(n_dve[i], 1)
                    dve.wait_ge(n_y0[i], n)
                    dve.wait_ge(n_dve[i], 4 * n - 3)
                    V.scalar_tensor_tensor(q[:, 4:5], q[:, 2:3], q[:, 2:3], q[:, 3:4], ALU.mult, ALU.mult).then_inc(n_dve[i], 1)
                    dve.wait_ge(n_dve[i], 4 * n - 2)
                    V.tensor_scalar(q[:, 5:6], q[:, 4:5], -0.5, 1.5, ALU.mult, ALU.add).then_inc(n_dve[i], 1)
                    dve.wait_ge(n_dve[i], 4 * n - 1)
                    V.tensor_tensor(q[:, 6:7], q[:, 5:6], q[:, 2:3], ALU.mult).then_inc(n_dve[i], 1)
                    dve.wait_ge(n_dve[i], 4 * n)

                def row_sum(l, n):
                    dve.wait_ge(AB[l]["e"], n)
                    V.tensor_reduce(sm[l][0:ROWS], pr[l][0:ROWS, 0:HEADS * SEQ].rearrange("p (h k) -> p h k", k=SEQ),
                                    AX.X, ALU.add).then_inc(AB[l]["sm"], 1)
                    dve.wait_ge(AB[l]["sm"], n)
                    V.reciprocal(ri[l][0:ROWS], sm[l][0:ROWS]).then_inc(AB[l]["ri"], 1)

                def select(l, ps, n):
                    for b in (1, 2):
                        if b == 1:
                            dve.wait_ge(AB[l]["o0"], n)
                        else:
                            dve.wait_ge(AB[l]["osel"], 2 * n - 1)
                        V.scalar_tensor_tensor(
                            sel[l][0:ROWS, b].rearrange("p (j d) -> p j d", j=2), ps[0:ROWS, :, 144 * b:144 * (b + 1)],
                            imk[0:ROWS, b:b + 1], sel[l][0:ROWS, b - 1].rearrange("p (j d) -> p j d", j=2),
                            ALU.mult, ALU.add).then_inc(AB[l]["osel"], 1)
                    dve.wait_ge(AB[l]["osel"], 2 * n)
                    dve.wait_ge(AB[l]["ri"], n)
                    V.tensor_tensor(sel[l][0:ROWS, 0, 0:DIM].rearrange("p (h d) -> p h d", d=HD),
                                    sel[l][0:ROWS, 2, 0:DIM].rearrange("p (h d) -> p h d", d=HD),
                                    bc(ri[l][0:ROWS], 2, [ROWS, HEADS, HD]), ALU.mult).then_inc(AB[l]["on"], 1)

                def body(s, par, step):
                    rows = last_rows(step, 4)
                    nR = s - 3
                    if live(step, 2):
                        dve.wait_ge(AB[0]["y"], s - 1)
                        V.tensor_tensor(xa[par][0:ROWS], Lb[0][0:ROWS, 0:DIM], xa[par][0:ROWS], ALU.add).then_inc(r_res, 1)
                        dve.wait_ge(r_res, s - 1)
                        V.bn_stats(st[0:ROWS], xa[par][0:ROWS]).then_inc(r_stat, 1)
                        dve.wait_ge(r_stat, alone(dve, s - 1))
                        V.bn_aggr(mv[0:ROWS], st[0:ROWS]).then_inc(r_aggr, 1)
                    if live(step, 1):
                        dve.wait_ge(e1_done, s)
                        V.tensor_tensor(z[0][0:ROWS, :, 0:3], z[0][0:ROWS, :, 0:3], bc(win[0:ROWS, 0:3], 1, [ROWS, HEADS, 3]),
                                        ALU.mult).then_inc(masked, 1)
                        V.tensor_tensor(z[0][0:ROWS, :, 32:36], z[0][0:ROWS, :, 32:36], bc(win[0:ROWS, 3:7], 1, [ROWS, HEADS, 4]),
                                        ALU.mult).then_inc(masked, 1)
                    if live(step, 2):
                        dve.wait_ge(r_aggr, s - 1)
                        newton(2, s - 1)
                        V.tensor_scalar(h1[0:ROWS], xa[par][0:ROWS], mv[0:ROWS, 0:1], nrm[2][0:ROWS, 6:7],
                                        ALU.subtract, ALU.mult).then_inc(h1_ready, 1)
                    if live(step, 0):
                        if past(s - 1):
                            dve.wait_ge(h1_ready, s - 1)
                        dve.wait_ge(embedded, s + 1)
                        V.tensor_tensor(xa[par][0:ROWS], Lb[3][0:ROWS, 0:DIM], posb[0:ROWS], ALU.add).then_inc(x_ready, 1)
                    if live(step, 5):
                        rows, nR, g = last_rows(step, 5), s - 4, row_of(s - 5, step)
                        dve.wait_ge(ranked, nR)
                        V.tensor_tensor(place[0:rows], Lb[2][0:rows, 264:264 + EXPERTS], rb[0:rows], ALU.add)\
                         .then_inc(placed, 1)
                        V.tensor_tensor(tot[0:rows], tot[0:rows], cnt[0:rows], ALU.add).then_inc(total_float, 1)
                        dve.wait_ge(placed, nR)
                        V.tensor_tensor(hit[0:rows], oh[0:rows], bc(place[0:rows], 1, [rows, 2, EXPERTS]), ALU.mult)\
                         .then_inc(hits, 1)
                        dve.wait_ge(total_float, nR)
                        V.tensor_copy(totb[0:rows], tot[0:rows]).then_inc(totalled, 1)
                        dve.wait_ge(hits, nR)
                        V.tensor_reduce(slotf[0:rows], hit[0:rows], AX.X, ALU.add).then_inc(slot_sum, 1)
                        V.tensor_copy(exp_all[0:rows, g].rearrange("p o k -> p (o k)"), topf[0:rows])
                        dve.wait_ge(slot_sum, nR)
                        V.tensor_copy(slot[1 - par][0:rows], slotf[0:rows]).then_inc(slots_ready, 1)
                        V.tensor_copy(place_all[0:rows, g].rearrange("p o k -> p (o k)"), slotf[0:rows])
                    if live(step, 2):
                        newton(0, s - 1)
                        V.scalar_tensor_tensor(hb[0:ROWS], h1[0:ROWS], nrm[0][0:ROWS, 6:7], ln1w[0:ROWS],
                                               ALU.mult, ALU.mult).then_inc(hb_ready, 1)
                    if live(step, 3):
                        dve.wait_ge(AB[1]["s"], s - 2)
                        V.tensor_tensor(z[1][0:ROWS].rearrange("p (j h) k -> p j h k", j=2),
                                        X[0:ROWS, :, 0:8 * SEQ].rearrange("p j (h k) -> p j h k", k=SEQ),
                                        cau[0:ROWS].unsqueeze(1).unsqueeze(1).to_broadcast([ROWS, 2, 8, SEQ]),
                                        ALU.add).then_inc(causal_done, 1)
                        dve.wait_ge(causal_done, s - 2)
                        V.tensor_reduce(mx[1][0:ROWS], z[1][0:ROWS], AX.X, ALU.max).then_inc(AB[1]["mx"], 1)
                    if live(step, 1):
                        row_sum(0, s)
                    if live(step, 4):
                        rows, nR = last_rows(step, 4), s - 3
                        dve.wait_ge(AB[1]["y"], nR)
                        V.tensor_tensor(rr[0:ROWS], Lb[1][0:ROWS, 0:DIM], hc[par][0:ROWS], ALU.add).then_inc(rr_ready, 1)
                        dve.wait_ge(rr_ready, nR)
                        if past(8 * s - 32 - 8 * par):
                            dve.wait_ge(res_stored[par], 8 * s - 32 - 8 * par)
                        V.tensor_tensor(res[par][0:ROWS], rr[0:ROWS], hc[par][0:ROWS], ALU.add).then_inc(res_ready, 1)
                        newton(1, nR, rows)
                        if past(16 * s - 64 - 16 * par):
                            dve.wait_ge(scattered[par], 16 * s - 64 - 16 * par)
                        V.scalar_tensor_tensor(h2[par][0:rows], rr[0:rows], nrm[1][0:rows, 6:7], ln2w[0:rows],
                                               ALU.mult, ALU.mult).then_inc(h2_ready, 1)
                    if live(step, 0):
                        dve.wait_ge(AB[0]["qm"], s + 1)
                        V.tensor_tensor(
                            kx[0], Lb[3][:, 256:512].rearrange("p (t r) -> p t r", t=KT)[:, :, 0:ROWS].unsqueeze(2)
                            .to_broadcast([128, KT, 4, ROWS]),
                            hm4.unsqueeze(1).unsqueeze(3).to_broadcast([128, KT, 4, ROWS]), ALU.mult)\
                         .then_inc(AB[0]["kx"], 2)
                    if live(step, 3):
                        row_sum(1, s - 2)
                    if live(step, 1):
                        select(0, Y, s)
                    if live(step, 2):
                        dve.wait_ge(rotated, s - 1)
                        V.tensor_tensor(qk_sin.rearrange("p (w j t) -> p w j t", w=2, j=2),
                                        Lb[3][:].rearrange("p (w j t) -> p w j t", w=2, j=2),
                                        bc(sinT, 2, [128, 2, 2, 128]), ALU.mult).then_inc(by_sin, 1)
                        dve.wait_ge(by_sin, s - 1)
                        dve.wait_ge(by_cos, s - 1)
                        c4, s4 = (x.rearrange("p (j t) -> p j t", j=4)[:, :, 0:ROWS] for x in (qk_cos, qk_sin))
                        v = qm[1].rearrange("p t b r -> p t (b r)")
                        dg = bass.AP(tensor=v.tensor, offset=v.offset,
                                     ap=[v.ap[0], [IPG * ROWS, KT], [ROWS + SEQ, IPG], [1, SEQ]])
                        V.tensor_tensor(kk[:], c4[:, 2:4], s4[:, 2:4], ALU.add).then_inc(kk_ready, 1)
                        V.tensor_tensor(dg, c4[:, 0:2].rearrange("p t (b q) -> p t b q", b=IPG),
                                        s4[:, 0:2].rearrange("p t (b q) -> p t b q", b=IPG), ALU.add).then_inc(AB[1]["qm"], 1)
                    if live(step, 4):
                        dve.wait_ge(logits, alone(dve, nR))
                        V.max(top[0:rows], Lb[2][0:rows, 256:256 + EXPERTS]).then_inc(top_d, 1)
                        dve.wait_ge(top_d, alone(dve, nR))
                        V.max_index(topi[0:rows], top[0:rows], Lb[2][0:rows, 256:256 + EXPERTS]).then_inc(top_i, 1)
                        V.tensor_tensor(rt[0:rows, 0:1], top[0:rows, 1:2], top[0:rows, 0:1], ALU.subtract).then_inc(gap, 1)
                    if live(step, 3):
                        select(1, X, s - 2)
                    if live(step, 4):
                        dve.wait_ge(gap_exp, nR)
                        V.tensor_scalar(rt[0:rows, 2:3], rt[0:rows, 1:2], 1.0, None, ALU.add).then_inc(gate_sum, 1)
                        dve.wait_ge(top_i, nR)
                        V.tensor_copy(topf[0:rows], topi[0:rows, 0:2]).then_inc(index_float, 1)
                        dve.wait_ge(gate_sum, nR)
                        V.reciprocal(rt[0:rows, 3:4], rt[0:rows, 2:3]).then_inc(gate_inv, 1)
                        dve.wait_ge(index_float, nR)
                        for k in range(2):
                            V.tensor_scalar(oh[0:rows, k], eio[0:rows], topf[0:rows, k:k + 1], None, ALU.is_equal)\
                             .then_inc(one_hot, 1)
                        dve.wait_ge(one_hot, 2 * nR)
                        V.tensor_tensor(cnt[0:rows], oh[0:rows, 0], oh[0:rows, 1], ALU.add).then_inc(count_float, 1)
                        g = row_of(s - 4, step)
                        dve.wait_ge(gate_inv, nR)
                        V.tensor_copy(w_all[0:rows, g, 0], rt[0:rows, 3:4])
                        dve.wait_ge(count_float, nR)
                        V.tensor_copy(cntb[0:rows], cnt[0:rows]).then_inc(counted, 1)
                        V.tensor_tensor(w_all[0:rows, g, 1], rt[0:rows, 3:4], rt[0:rows, 1:2], ALU.mult)
                    if live(step, 0):
                        dve.wait_ge(AB[0]["s"], s + 1)
                        s4 = Y[0:ROWS, :, 0:8 * SEQ].rearrange("p j (h k) -> p j h k", k=SEQ)
                        V.tensor_reduce(mx[0][0:ROWS].rearrange("p (j h) -> p j h", j=2), s4, AX.X, ALU.max)\
                         .then_inc(AB[0]["mx"], 1)
                        dve.wait_ge(AB[0]["mx"], s + 1)
                        V.tensor_tensor(z[0][0:ROWS].rearrange("p (j h) k -> p j h k", j=2), s4,
                                        mx[0][0:ROWS].rearrange("p (j h) -> p j h", j=2).unsqueeze(3)
                                        .to_broadcast([ROWS, 2, 8, SEQ]), ALU.subtract).then_inc(AB[0]["z"], 1)

                steps(dve, body)

            @block.tensor
            def _(pe):
                pe.wait_ge(tokw_loaded, 16)

                def split_product(ps, x, w, start, stop):
                    T.matmul(ps, x[0], w[0], start=start, stop=False)
                    T.matmul(ps, x[0], w[1], start=False, stop=False)
                    return T.matmul(ps, x[1], w[0], start=False, stop=stop)

                def embed_first(g):
                    pe.wait_ge(pat_loaded[g % 2], 16 * (g // 2 + 1))
                    for t in range(PT_TILES):
                        last = T.matmul(Lb[3][0:ROWS, 0:DIM], pat[g % 2][:, t], tokw[:, t], start=t == 0, stop=t == PT_TILES - 1)
                    last.then_inc(embedded, 1)

                def transpose_x(ps, src, ready, n, done, rows=ROWS):
                    pe.wait_ge(ready, n)
                    for t in range(KT):
                        last = T.transpose(ps[:, t * rows:(t + 1) * rows], src[0:rows, t * 128:(t + 1) * 128],
                                           ident[0:rows, 0:rows])
                    last.then_inc(done, 1)

                def project(l, qk_bank, n):
                    pe.wait_ge(AB[l]["xt"], 2 * n)
                    for j in range(4):
                        for t in range(KT):
                            last = T.matmul(qk_bank[:, j * 128:(j + 1) * 128], wqk[l][:, t, j * 128:(j + 1) * 128], xt[l][:, t],
                                            start=t == 0, stop=t == KT - 1)
                    last.then_inc(AB[l]["qk"], 1)

                def project_v(l, v_bank, n, early):
                    if not early:
                        pe.wait_ge(xt_low[l], n)
                    for t in range(KT):
                        if early:
                            last = T.matmul(v_bank[0:ROWS, 0:DIM], xt[l][:, t, 0:ROWS], wv[l][:, t],
                                            start=t == 0, stop=t == KT - 1)
                        else:
                            last = split_product(v_bank[0:ROWS, 0:DIM], [x[:, t] for x in xt_parts[l]],
                                                 [w[:, t] for w in wv_parts[l]], t == 0, t == KT - 1)
                    last.then_inc(AB[l]["v"], 1)

                def scores(l, ps, n):
                    pe.wait_ge(AB[l]["qm"], n)
                    pe.wait_ge(AB[l]["kx"], 2 * n)
                    for t in range(KT):
                        for r in range(2):
                            for b in range(IPG):
                                last = T.matmul(ps[0:ROWS, r, t * 144:(t + 1) * 144], qm[l][64 * r:64 * r + 64, t, b],
                                                kx[l][64 * r:64 * r + 64, t, :, SEQ * b:SEQ * (b + 1)],
                                                start=b == 0, stop=b == IPG - 1)
                    last.then_inc(AB[l]["s"], 1)

                def transpose_p(l, ps, n):
                    pe.wait_ge(AB[l]["e"], n)
                    for c in range(CHUNKS):
                        last = T.transpose(ps[0:CH, c // 3, (c % 3) * ROWS:(c % 3 + 1) * ROWS],
                                           pr[l][0:ROWS, c * CH:(c + 1) * CH], ident[0:ROWS, 0:ROWS])
                    last.then_inc(AB[l]["p_t"], 1)

                def values(l, ps, n):
                    pe.wait_ge(AB[l]["pt"], n)
                    pe.wait_ge(AB[l]["vx"], n)
                    for c in range(CHUNKS):
                        last = T.matmul(ps[0:ROWS, c // 3, 0:432].rearrange("p (b c d) -> p b c d", b=3, c=3)[:, :, c % 3],
                                        pt[l][0:CH, c], vx[l][0:CH, :, 48 * c:48 * (c + 1)], start=True, stop=True)
                    last.then_inc(AB[l]["o"], 1)

                def transpose_o(l, ps, n):
                    pe.wait_ge(AB[l]["on"], n)
                    for t in range(KT):
                        last = T.transpose(ps[:, t * ROWS:(t + 1) * ROWS], sel[l][0:ROWS, 0, t * 128:(t + 1) * 128],
                                           ident[0:ROWS, 0:ROWS])
                    last.then_inc(AB[l]["o_t"], 1)

                def project_out(l, ps, n, early):
                    if early:
                        pe.wait_ge(AB[l]["ot"], 2 * n)
                    else:
                        pe.wait_ge(ot_low[l], n)
                    for t in range(KT):
                        if early:
                            last = T.matmul(ps[0:ROWS, 0:DIM], ot[l][:, t], wo[l][:, t], start=t == 0, stop=t == KT - 1)
                        else:
                            last = split_product(ps[0:ROWS, 0:DIM], [o[:, t] for o in ot_parts[l]],
                                                 [w[:, t] for w in wo_parts[l]], t == 0, t == KT - 1)
                    last.then_inc(AB[l]["y"], 1)

                def rank(n, rows):
                    pe.wait_ge(counted, n)
                    if past(n - 1):
                        pe.wait_ge(totalled, n - 1)
                    o = Lb[2][0:rows, 264:264 + EXPERTS]
                    T.matmul(o, lowb[0:rows, 0:rows], cntb[0:rows], start=True, stop=False)
                    T.matmul(o, oneb[0:ROWS, 0:rows], totb[0:ROWS], start=False, stop=True).then_inc(ranked, 1)

                def draining(step):
                    return step is not None and step >= GROUPS

                def body(s, par, step):
                    rows = last_rows(step, 4)
                    nR = s - 3
                    early = step is not None and step < 3
                    if live(step, 4):
                        transpose_o(1, Lb[1], nR)
                    if live(step, 5) and draining(s - 1 if step is not None else None):
                        rank(s - 4, last_rows(step, 5))
                    if live(step, 3):
                        scores(1, X, s - 2)
                    if live(step, 0):
                        if past(s - 1):
                            pe.wait_ge(r_res, s - 1)
                        transpose_x(Lb[0], xa[par], x_ready, s + 1, AB[0]["x_t"])
                    if live(step, 4):
                        project_out(1, Lb[1], nR, early)
                    if live(step, 0):
                        project(0, Lb[3], s + 1)
                    if live(step, 2):
                        if past(s - 4):
                            pe.wait_ge(placed, s - 4)
                        transpose_x(Lb[2], hb, hb_ready, s - 1, AB[1]["x_t"])
                    if live(step, 0):
                        project_v(0, Lb[0], s + 1, early)
                    if live(step, 1):
                        if past(s - 2):
                            pe.wait_ge(causal_done, s - 2)
                        transpose_p(0, X, s)
                    if live(step, 2):
                        if past(s - 3):
                            pe.wait_ge(rr_ready, s - 3)
                        project(1, Lb[1], s - 1)
                    if live(step, 1):
                        if past(s):
                            pe.wait_ge(AB[0]["z"], s)
                        values(0, Y, s)
                    if live(step, 2):
                        project_v(1, Lb[2], s - 1, early)
                    if live(step, 4):
                        if live(step, 0):
                            pe.wait_ge(AB[0]["kx"], 2 * s + 2)
                        transpose_x(Lb[3], h2[par], h2_ready, nR, h2_t, rows)
                    if live(step, 3):
                        if live(step, 1):
                            pe.wait_ge(AB[0]["pt"], s)
                        transpose_p(1, X, s - 2)
                    if live(step, 2):
                        pe.wait_ge(qk_copied, s - 1)
                        if live(step, 4):
                            pe.wait_ge(h2t, nR)
                        if live(step, 0):
                            pe.wait_ge(AB[0]["kx"], 2 * s + 2)
                        T.matmul(Lb[3][:], rotm, qk_sb, start=True, stop=True).then_inc(rotated, 1)
                    if live(step, 4):
                        pe.wait_ge(h2t, nR)
                        if live(step, 2):
                            pe.wait_ge(AB[1]["vs"], s - 1)
                        for t in range(KT):
                            last = T.matmul(Lb[2][0:rows, 256:256 + EXPERTS], xt[2][:, t, 0:rows], routw[:, t],
                                            start=t == 0, stop=t == KT - 1)
                        last.then_inc(logits, 1)
                    if live(step, 3):
                        values(1, X, s - 2)
                    if live(step, 1):
                        if live(step, 0):
                            pe.wait_ge(AB[0]["vs"], s + 1)
                        transpose_o(0, Lb[0], s)
                    if live(step, 0):
                        if past(s):
                            pe.wait_ge(AB[0]["on"], s)
                        scores(0, Y, s + 1)
                    if live(step, 4) and not draining(step):
                        rank(nR, rows)
                    if live(step, 1):
                        project_out(0, Lb[0], s, early)
                    if step is None or step + 1 < GROUPS:
                        if past(s - 1):
                            pe.wait_ge(AB[1]["qm"], s - 1)
                        if step is not None and step + 1 < EMBED_FIRST:
                            embed_first(s + 1)
                        else:
                            pe.wait_ge(pat_low, split_count(s + 1))
                            for t in range(PT_TILES):
                                last = split_product(Lb[3][0:ROWS, 0:DIM], [x[:, t] for x in pat_parts[1 - par]],
                                                     [w[:, t] for w in tokw_parts], t == 0, t == PT_TILES - 1)
                            last.then_inc(embedded, 1)

                embed_first(0)
                pe.wait_ge(consts_loaded, 16 * len(consts))
                pe.wait_ge(setup_pool, 9)
                pe.wait_ge(setup_dve, 3)
                steps(pe, body)

        attention.close()
        high, low_ = (ctx.enter_context(nc.sbuf_tensor(n, [128, RING * EXPERT_COLS], f32r)) for n in ("w_high", "w_low"))
        xm = [tuple(sb(f"x{n}{i}", [128, DIM], f32r) for n in ("high", "low")) for i in range(2)]
        atb = [tuple(sb(f"act_{n}{i}", [128, HALF[i]], f32r) for n in ("high", "low")) for i in range(2)]
        HEAD = (0, HALF[0])
        N_PLAN = 12

        sums = raw[0][:, 0:OUT_TILES * DIM].rearrange("p (g d) -> p g d", d=DIM)
        ys_in = [[raw[1][:, (4 * i + 2 * k) * DIM:(4 * i + 2 * k + 2) * DIM].rearrange("p (g d) -> p g d", d=DIM)
                  for k in range(2)] for i in range(2)]
        stats = [sb(f"stats{i}", [128, 2, 6]) for i in range(2)]
        mvs = [sb(f"mvs{i}", [128, 2, 2]) for i in range(2)]
        lnv, root, ve, tq, uq, inv = ([sb(f"{n}{i}", [128, 2, 1]) for i in range(2)]
                                      for n in ("lnv", "root", "ve", "tq", "uq", "inv"))
        cidx = [sb(f"cidx{i}", [128, 2, 2], u32) for i in range(2)]
        BATCHES = OUT_TILES // 2
        assert BATCHES * 2 == OUT_TILES

        def batches(eng, body):
            for b in range(2):
                body(b, b % 2, b)
            with eng.Fori(2, BATCHES - 2, 2) as b:
                body(b, 0, None)
                body(b + 1, 1, None)
            body(BATCHES - 1, (BATCHES - 1) % 2, BATCHES - 1)

        def zero_tails(eng, half, done):
            eng.wait_ge(tail_slots, 1)
            for e in range(half, EXPERTS, 2):
                row = eng.value_load(tails[0:1, e:e + 1], min_val=0, max_val=EXPERTS * REGION - TILE)
                eng.dma_start(xs[bass.ds(row, TILE), :], zero[:]).then_inc(done, 16)

        def pair(eng, body, first, last, start):
            for j in range(first, start):
                body(j, j % 2, j)
            with eng.Fori(start, last - 1, 2) as j:
                body(j, start % 2, None)
                body(j + 1, 1 - start % 2, None)

        with nc.Block() as block:
            @block.sync
            def _(sp):
                zero_tails(sp, 0, zeroed)
                sp.wait_ge(rows_ready, 1)
                sp.wait_ge(zeroed, 16 * EXPERTS // 2)
                sp.wait_ge(spare_zeroed, 16 * (SPARE_TILES + EXPERTS // 2))
                for i in range(2):
                    sp.wait_ge(scattered[i], 16 * GROUPS)

                def load(j, par, at):
                    row = sp.value_load(row_tab[0:1, row_of(j, at)], min_val=0, max_val=XS_ROWS - TILE)
                    sp.dma_start(xg[par][:], xs[bass.ds(row, TILE), :]).then_inc(x_loaded[par], 16)

                def body(j, par, at):
                    if at is None or at + 2 < TILES:
                        sp.wait_ge(mt, alone(sp, j + 1))
                        load(j + 2, par, None if at is None else at + 2)
                    if at is None or at > 0:
                        store(j - 1, 1 - par, at)

                def store(j, par, at):
                    sp.wait_ge(y_copied, j + 1)
                    sp.dma_start(ys[row_of(j * TILE, at, TILE), :], yb[par][:]).then_inc(y_stored[par], 16)

                load(0, 0, 0)
                load(1, 1, 1)
                pair(sp, body, 0, TILES - 3, 2)
                for j in range(TILES - 3, TILES - 1):
                    body(j, j % 2, j)
                body(TILES - 1, (TILES - 1) % 2, TILES - 1)
                store(TILES - 1, (TILES - 1) % 2, 0)

                def put(b, par, at_):
                    sp.wait_ge(out_ready, 2 * b + 2)
                    sp.dma_start(out[row_of(b * 2 * TILE, at_, 2 * TILE), :].rearrange("(g r) d -> r g d", r=TILE),
                                 sums[:, row_of(2 * b, at_, 2)]).then_inc(out_stored, 16)

                batches(sp, put)
                sp.wait_ge(out_stored, 16 * BATCHES)

            @block.gpsimd
            def _(pool):

                def load(e):
                    pool.wait_ge(experts_ready, e - RAW + 2)
                    pool.dma_start(raw[e % RAW][:], expert_w[:, e]).then_inc(expert_loaded[e % RAW], 16)

                def split(e):
                    if e >= RING:
                        end = pool.value_load(end_tab[0:1, e - RING:e - RING + 1], min_val=1, max_val=TILES + 1)
                    h, l = (x[:, e % RING * EXPERT_COLS:(e % RING + 1) * EXPERT_COLS] for x in (high, low_))
                    pool.wait_ge(expert_loaded[e % RAW], 16 * (e // RAW + 1))
                    if e >= RING:
                        pool.wait_ge(y_ready, end)
                    P.tensor_tensor(h, raw[e % RAW][:], nil[:].to_broadcast([128, EXPERT_COLS]), ALU.add).then_inc(high_part, 1)
                    pool.wait_ge(high_part, e + 1)
                    P.tensor_tensor(l, raw[e % RAW][:], h, ALU.subtract).then_inc(experts_ready, 1)

                zero_tails(pool, 1, spare_zeroed)
                pool.dma_start(routing.rearrange("(g r) c -> r g c", r=ROWS), info[0:ROWS]).then_inc(info_moved, 16)
                pool.wait_ge(high_part, 1)
                P.tensor_tensor(low_[:, FIRST_COLS:EXPERT_COLS], raw[0][:, FIRST_COLS:], high[:, FIRST_COLS:EXPERT_COLS],
                                ALU.subtract).then_inc(experts_ready, 1)
                pool.wait_ge(info_moved, 16)
                pool.dma_start(info_t[:], routing[0:TOKENS, :].rearrange("(g r) c -> r g c", r=TILE)).then_inc(info_moved, 16)
                pool.wait_ge(plan_ready, 1)
                for e in range(1, EXPERTS):
                    if e + 1 < EXPERTS:
                        load(e + 1)
                    split(e)

                pool.wait_ge(experts_ready, EXPERTS + 1)
                for i in range(2):
                    pool.wait_ge(res_stored[i], 8 * GROUPS)
                pool.dma_start(sums, residual[0:TOKENS, :].rearrange("(g r) d -> r g d", r=TILE)).then_inc(base_loaded, 16)
                for i in range(2):
                    pool.wait_ge(y_stored[i], 16 * (TILES // 2 + (TILES % 2) * (1 - i)))

                pool.wait_ge(slots_moved, 1)

                def gather(b, par, at_):
                    if past(4 * b - 4):
                        pool.wait_ge(summed, 4 * b - 4)
                    P.tensor_copy(cidx[par][:].rearrange("p g k -> p (g k)"),
                                  slot_all[:, row_of(2 * b, at_, 2)].rearrange("p g k -> p (g k)")).then_inc(idx_ready, 1)
                    pool.wait_ge(idx_ready, alone(pool, b + 1))
                    for i in range(2):
                        for k, y in enumerate(ys_in[par]):
                            P.indirect_dma_start(y[:, i], None, ys,
                                                 bass.IndirectOffsetOnAxis(cidx[par][:, i, k:k + 1], 0))\
                             .then_inc(gathered[par], 16)

                batches(pool, gather)

            @block.scalar
            def _(act):
                act.wait_ge(expert_loaded[0], 16)
                A.activation(high[:, 0:EXPERT_COLS], raw[0][:], ACT.Copy).then_inc(high_part, 1)

                def silu(h, n):
                    act.wait_ge(gu[h], n)
                    A.activation(sgb[h][:], S[h][:, 0, 0:HALF[h]], ACT.Silu).then_inc(sg[h], 1)

                def copy_y(par, n):
                    act.wait_ge(y_ready, n + 1)
                    if past(8 * n - 8 - 8 * par):
                        act.wait_ge(y_stored[par], 8 * n - 8 - 8 * par)
                    A.activation(yb[par][:], Lb[3][:, 0:DIM], ACT.Copy).then_inc(y_copied, 1)

                def body(j, par, at):
                    silu(0, j + 1)
                    silu(1, j + 1)
                    if at is None or at > 0:
                        copy_y(1 - par, j)

                pair(act, body, 0, TILES - 1, 2)
                body(TILES - 1, (TILES - 1) % 2, TILES - 1)
                copy_y((TILES - 1) % 2, TILES)

                def root_of(b, par, at_):
                    act.wait_ge(r_aggr, GROUPS + 2 * b + 2)
                    A.activation(lnv[par][:], mvs[par][:, :, 1:2], ACT.Ln, bias=eps[:, 0:1]).then_inc(n_ln[2], 1)
                    act.wait_ge(n_ln[2], GROUPS + b + 1)
                    A.activation(root[par][:], lnv[par][:], ACT.Exp, scale=-0.5).then_inc(n_y0[2], 1)

                A.preload_act_table_set("natural_log_exp_and_others")
                batches(act, root_of)

            @block.vector
            def _(dve):
                done = [0]

                def step(ins):
                    done[0] += 1
                    ins.then_inc(plan, 1)
                    dve.wait_ge(plan, done[0])

                dve.wait_ge(counts_ready, 1)
                n_e = Lb[3][:, 0:EXPERTS]
                step(V.tensor_tensor(tailf[:], n_e, rb[:], ALU.add))
                V.tensor_copy(tails[:], tailf[0:1]).then_inc(tail_slots, 1)
                eq, ee = [128, EXPERTS, TOKENS // TILE], [128, EXPERTS, EXPERTS]
                step(V.tensor_tensor(over[:], bc(n_e, 2, eq), bc(thr[:], 1, eq), ALU.is_gt))
                step(V.tensor_reduce(nt[:], over[:], AX.X, ALU.add))
                step(V.tensor_tensor(pre[:], bc(nt[:], 1, ee), bef[:], ALU.mult))
                step(V.tensor_reduce(cum[:], pre[:], AX.X, ALU.add))
                je = [1, TILES, EXPERTS]
                step(V.tensor_tensor(ge, bc(tid[:], 2, je), bc(cum[0:1], 1, je), ALU.is_ge))
                step(V.tensor_reduce(te[:], ge, AX.X, ALU.add))
                step(V.tensor_tensor(gt, ge, bc(nt[0:1], 1, je), ALU.mult))
                step(V.tensor_reduce(tb[:], gt, AX.X, ALU.add))
                step(V.tensor_tensor(tl[:], tid[:], tb[:], ALU.subtract))
                step(V.tensor_scalar(tl[:], tl[:], float(TILE), None, ALU.mult))
                step(V.scalar_tensor_tensor(tr[:], te[:], float(REGION), tl[:], ALU.mult, ALU.add))
                V.tensor_copy(row_tab[:], tr[:]).then_inc(rows_ready, 1)
                step(V.tensor_tensor(gt, ge, bc(cstep[:], 1, je), ALU.mult))
                step(V.tensor_reduce(tw[:], gt, AX.X, ALU.add))
                step(V.tensor_copy(col_tab[:], tw[:]))
                step(V.tensor_scalar(endf[:], cum[0:1], 1.0, None, ALU.add))
                step(V.tensor_copy(end_tab[:], endf[:]))
                step(V.tensor_scalar(tw[:], te[:], float(EXPERTS - 1), 2.0, ALU.min, ALU.add))
                V.tensor_copy(need_tab[:], tw[:]).then_inc(plan_ready, 1)
                def times_up(h, n):
                    dve.wait_ge(sg[h], n)
                    V.tensor_tensor(acb[h][:], sgb[h][:], S[h][:, 1, 0:HALF[h]], ALU.mult).then_inc(ac[h], 1)

                def split_psum(high, low, src, high_done, n, low_done):
                    V.tensor_copy(high, src).then_inc(high_done, 1)
                    dve.wait_ge(high_done, n)
                    V.tensor_tensor(low, src, high, ALU.subtract).then_inc(low_done, 1)

                def split_at(h, n):
                    dve.wait_ge(a_t[h], n)
                    split_psum(atb[h][0][:, 0:HALF[h]], atb[h][1][:, 0:HALF[h]], L[h][:, 0:HALF[h]], ath[h], n, at[h])

                def split_x(par, n):
                    dve.wait_ge(mt, n)
                    split_psum(xm[par][0][:], xm[par][1][:], Lb[2][:, 0:DIM], mxh, n, mxt)

                def body(j, par, at_):
                    if at_ is None or at_ > 0:
                        split_at(1, j)
                    times_up(0, j + 1)
                    if at_ is None or at_ + 1 < TILES:
                        split_x(1 - par, j + 2)
                    split_at(0, j + 1)
                    times_up(1, j + 1)

                dve.wait_ge(high_part, 1)
                V.tensor_tensor(low_[:, 0:FIRST_COLS], raw[0][:, 0:FIRST_COLS], high[:, 0:FIRST_COLS], ALU.subtract)\
                 .then_inc(experts_ready, 1)
                split_x(0, 1)
                pair(dve, body, 0, TILES - 1, 2)
                body(TILES - 1, (TILES - 1) % 2, TILES - 1)
                split_at(1, TILES)
                own4 = own.rearrange("p (g k) e -> p g k e", k=2)
                step(V.tensor_tensor(shift[:], cum[:], nt[:], ALU.subtract))
                step(V.scalar_tensor_tensor(shift[:], shift[:], float(TILE), rb[:], ALU.mult, ALU.subtract))
                dve.wait_ge(info_moved, 32)
                for k in range(2):
                    step(V.tensor_tensor(own4[:, :, k], info_t[:, :, 4 + k:5 + k].to_broadcast([128, OUT_TILES, EXPERTS]),
                                         bc(eio[:], 1, [128, OUT_TILES, EXPERTS]), ALU.is_equal))
                step(V.tensor_tensor(own, own, bc(shift[:], 1, [128, 2 * OUT_TILES, EXPERTS]), ALU.mult))
                step(V.tensor_reduce(moved[:].rearrange("p g k -> p (g k)"), own, AX.X, ALU.add))
                step(V.tensor_tensor(moved[:], moved[:], info_t[:, :, 2:4], ALU.add))
                V.tensor_copy(slot_all[:], moved[:]).then_inc(slots_moved, 1)

                dve.wait_ge(base_loaded, 16)
                def add_experts(b, par, at_):
                    if past(2 * b - 2):
                        dve.wait_ge(out_ready, 2 * b - 2)
                    dve.wait_ge(gathered[par], 32 * b + 64 - 32 * par)
                    for k, y in enumerate(ys_in[par]):
                        for i in range(2):
                            g = row_of(2 * b + i, at_)
                            if k:
                                dve.wait_ge(summed, 4 * b + 1 + i)
                            V.scalar_tensor_tensor(sums[:, g].rearrange("p o d -> p (o d)"),
                                                   y[:, i],
                                                   info_t[:, g, k:k + 1].rearrange("p o k -> p (o k)"),
                                                   sums[:, g].rearrange("p o d -> p (o d)"),
                                                   ALU.mult, ALU.add).then_inc(summed, 1)
                    for i in range(2):
                        g = row_of(2 * b + i, at_)
                        n = alone(dve, 4 * b + 3 + i)
                        dve.wait_ge(summed, n)
                        V.bn_stats(stats[par][:, i], sums[:, g].rearrange("p o d -> p (o d)"))\
                         .then_inc(r_stat, 1)
                    for i in range(2):
                        n = alone(dve, GROUPS + 2 * b + 1 + i)
                        dve.wait_ge(r_stat, n)
                        V.bn_aggr(mvs[par][:, i], stats[par][:, i]).then_inc(r_aggr, 1)

                def normalise(b, par, at_):
                    v, t, u, r, y = (x[par][:] for x in (ve, tq, uq, inv, root))
                    dve.wait_ge(r_aggr, GROUPS + 2 * b + 2)
                    V.tensor_scalar(v, mvs[par][:, :, 1:2], LN_EPS, None, ALU.add).then_inc(refined, 1)
                    dve.wait_ge(n_y0[2], GROUPS + b + 1)
                    V.tensor_tensor(t, y, y, ALU.mult).then_inc(refined, 1)
                    dve.wait_ge(refined, 5 * b + 2)
                    V.tensor_tensor(t, t, v, ALU.mult).then_inc(refined, 1)
                    dve.wait_ge(refined, 5 * b + 3)
                    V.tensor_scalar(u, t, -0.5, 1.5, ALU.mult, ALU.add).then_inc(refined, 1)
                    dve.wait_ge(refined, 5 * b + 4)
                    V.tensor_tensor(r, u, y, ALU.mult).then_inc(refined, 1)
                    dve.wait_ge(refined, 5 * b + 5)
                    for i in range(2):
                        g = row_of(2 * b + i, at_)
                        x = sums[:, g].rearrange("p o d -> p (o d)")
                        V.tensor_scalar(x, x, mvs[par][:, i, 0:1], inv[par][:, i], ALU.subtract, ALU.mult).then_inc(out_ready, 1)

                def combine(b, par, at_):
                    add_experts(b, par, at_)
                    if at_ is None or at_ > 0:
                        normalise(b - 1, 1 - par, None if at_ is None else at_ - 1)

                batches(dve, combine)
                normalise(BATCHES - 1, (BATCHES - 1) % 2, BATCHES - 1)

            @block.tensor
            def _(pe):
                T.matmul(Lb[3][:, 0:EXPERTS], oneb[0:ROWS, :], totb[0:ROWS], start=True, stop=True).then_inc(counts_ready, 1)
                pe.sem_inc(y_ready, 1)

                def split_product(ps, x, at, n, start, stop):
                    w_high, w_low = (w[:, bass.ds(at, n)] for w in (high, low_))
                    T.matmul(ps, x[0], w_high, start=start, stop=False)
                    T.matmul(ps, x[0], w_low, start=False, stop=False)
                    return T.matmul(ps, x[1], w_high, start=False, stop=stop)

                def transpose_tile(par, n):
                    pe.wait_ge(x_loaded[par], 8 * n + 8 - 8 * par)
                    for t in range(KT):
                        last = T.transpose(Lb[2][:, t * TILE:(t + 1) * TILE], xg[par][:, t * 128:(t + 1) * 128], ident[:])
                    last.then_inc(mt, 1)

                def gate_up(par, h, n, col):
                    pe.wait_ge(mxt, n)
                    if past(n - 1):
                        pe.wait_ge(ac[h], n - 1)
                    for u in range(2):
                        for t in range(KT):
                            c0 = (2 * t + u) * FF + HEAD[h]
                            last = split_product(S[h][:, u, 0:HALF[h]], [x[:, t * 128:(t + 1) * 128] for x in xm[par]],
                                                 col + c0, HALF[h], t == 0, t == KT - 1)
                    last.then_inc(gu[h], 1)

                def transpose_act(h, n):
                    pe.wait_ge(ac[h], n)
                    for c in range(HALF[h] // 128):
                        last = T.transpose(L[h][:, c * 128:(c + 1) * 128], acb[h][:, c * 128:(c + 1) * 128], ident[:])
                    last.then_inc(a_t[h], 1)

                def down(h, n, col):
                    pe.wait_ge(at[h], n)
                    if h == 0:
                        if past(n - 1):
                            pe.wait_ge(y_copied, n - 1)
                    for c in range(HALF[h] // 128):
                        c0 = KT * 2 * FF + (HEAD[h] // 128 + c) * DIM
                        last = split_product(Lb[3][:, 0:DIM], [a[:, c * 128:(c + 1) * 128] for a in atb[h]],
                                             col + c0, DIM, h == 0 and c == 0, h == 1 and c == HALF[1] // 128 - 1)
                    if h == 1:
                        last.then_inc(y_ready, 1)

                def body(j, par, at_):
                    col = pe.value_load(col_tab[0:1, row_of(j, at_)], min_val=0, max_val=(RING - 1) * EXPERT_COLS)
                    need = pe.value_load(need_tab[0:1, row_of(j, at_)], min_val=2, max_val=EXPERTS + 1)
                    pe.wait_ge(experts_ready, need)
                    gate_up(par, 0, j + 1, col)
                    if at_ is None or at_ > 0:
                        before_ = pe.value_load(col_tab[0:1, row_of(j - 1, at_)],
                                                min_val=0, max_val=(RING - 1) * EXPERT_COLS)
                        transpose_act(1, j)
                        down(0, j, before_)
                    if at_ is None or at_ + 1 < TILES:
                        transpose_tile(1 - par, j + 2)
                    gate_up(par, 1, j + 1, col)
                    transpose_act(0, j + 1)
                    if at_ is None or at_ > 0:
                        down(1, j, before_)

                pe.wait_ge(plan_ready, 1)
                transpose_tile(0, 1)
                pair(pe, body, 0, TILES - 1, 2)
                body(TILES - 1, (TILES - 1) % 2, TILES - 1)
                col = pe.value_load(col_tab[0:1, TILES - 1:TILES], min_val=0, max_val=(RING - 1) * EXPERT_COLS)
                transpose_act(1, TILES)
                down(0, TILES, col)
                down(1, TILES, col)


def kernel(**inputs):
    import numpy as np
    import concourse.bacc as bacc
    from concourse.bass_utils import run_bass_kernel_spmd

    given = {k: np.asarray(v) for k, v in inputs.items()}
    rows = lambda v: np.ascontiguousarray(np.broadcast_to(v, (ROWS, v.shape[-1])))
    tiles = lambda w: np.ascontiguousarray(w.reshape(-1, 128, w.shape[1]).transpose(1, 0, 2))

    x, p = given["x"], 16
    x = x.reshape(IMAGES, 3, 6, p, 6, p).transpose(1, 3, 5, 0, 2, 4).reshape(PATCH_DIM, TOKENS)
    fill = GROUPS * ROWS - TOKENS
    x = np.concatenate([x, x[:, :fill]], 1)
    patches = np.ascontiguousarray(x.reshape(PT_TILES, 128, GROUPS, ROWS).transpose(1, 2, 0, 3)
                                   .reshape(128, GROUPS, PT_TILES * ROWS))

    rep = lambda w: np.repeat(w.reshape(DIM, 8, 1, HD), 2, 2).reshape(DIM, DIM)
    slots = np.arange(HEADS).reshape(2, 2, 4).transpose(1, 0, 2).reshape(-1)
    by_slot = (slots[:, None] * HD + np.arange(HD)).reshape(-1)
    bq, bk, bv = given["L0_ffn_wq"], rep(given["L0_ffn_wk"]), rep(given["L0_ffn_wv"])
    gate, up, down = (given[f"L0_ffn_w_{n}"] for n in ("gate", "up", "down"))
    gu = np.stack([gate, up], 2).reshape(EXPERTS, KT, 128, 2 * FF).transpose(2, 0, 1, 3).reshape(128, EXPERTS, -1)
    dn = down.reshape(EXPERTS, DOWN_TILES, 128, DIM).transpose(2, 0, 1, 3).reshape(128, EXPERTS, -1)

    f = np.float32
    row, ch, q = np.arange(ROWS), np.arange(128), np.arange(ROWS) % SEQ
    headmask4 = (ch[:, None] % 64 // HD == np.arange(4)).astype(f)
    headmask3 = (row[:, None] // SEQ == np.arange(HEADS) % 3).astype(f)
    imagemask = (row[:, None] // SEQ == np.arange(IPG)).astype(f)
    d = np.arange(SEQ)[None] - q[:, None]
    window = ((d <= 31) & (d >= -32)).astype(f)[:, [0, 1, 2, 32, 33, 34, 35]]
    causal = np.where(d <= 0, f(0), f(-3e38)).astype(f)
    inv = (f(1) / f(10000.0) ** (np.arange(0, HD, 2, dtype=f) / f(HD))).astype(f)
    ang = (np.arange(128) % SEQ).astype(f)[None] * inv[ch % 8][:, None]
    rotate = np.zeros((128, 128), f)
    for m in range(128):
        rotate[m + 8 if m % HD < 8 else m - 8, m] = -1 if m % HD < 8 else 1
    scaled = lambda t: np.stack([t * f(HD ** -0.5), t], 1)
    cols = [k % RING * EXPERT_COLS for k in range(EXPERTS)]
    col_step = np.array([[b - a for a, b in zip(cols, cols[1:])] + [0]], f)
    e = np.arange(EXPERTS)
    args = dict(
        col_step=col_step,
        patches=patches, tok_w=tiles(given["L0_tok_W"].T), tok_b=rows(given["L0_tok_b"]),
        pos=np.ascontiguousarray(np.tile(given["L0_tok_pos_embd"][0], (IPG, 1))),
        a_wqk=tiles(np.concatenate([given["L0_attn_Wq"], given["L0_attn_Wk"]], 1)),
        a_wv=tiles(given["L0_attn_Wv"][:, by_slot]), a_wo=tiles(given["L0_attn_Wo"][by_slot]),
        b_wqk=tiles(np.concatenate([bq, bk], 1)), b_wv=tiles(bv[:, by_slot]), b_wo=tiles(given["L0_ffn_wo"][by_slot]),
        ln1=rows(given["L0_ffn_ln1_w"]), ln2=rows(given["L0_ffn_ln2_w"]), router=tiles(given["L0_ffn_router_w"]),
        expert_w=np.ascontiguousarray(np.concatenate([gu, dn], 2)),
        headmask4=headmask4, headmask3=headmask3, imagemask=imagemask, window=window, causal=causal,
        rope_cos=scaled(np.cos(ang).astype(f)), rope_sin=scaled(np.sin(ang).astype(f)), rotate=rotate,
        identity=np.eye(128, dtype=f), lower=(row[:, None] < row[None]).astype(f),
        expert_iota=np.tile(e.astype(f), (128, 1)), region_base=np.tile((e * REGION).astype(f), (128, 1)),
        thresholds=np.tile((np.arange(TOKENS // TILE) * TILE).astype(f), (128, 1)), tile_ids=np.arange(TILES, dtype=f)[None],
        before=np.tile((e[None] <= e[:, None]).astype(f), (128, 1, 1)),
    )
    nc = bacc.Bacc("TRN2", target_bir_lowering=False, num_devices=1)
    aps = {n: nc.dram_tensor(f"in_{n}", a.shape, mybir.dt.from_np(a.dtype), kind="ExternalInput").ap()
           for n, a in args.items()}
    out = nc.dram_tensor("out", (TOKENS, DIM), mybir.dt.float32, kind="ExternalOutput").ap()
    program(nc, out=out, **aps)
    r = run_bass_kernel_spmd(nc, [{f"in_{n}": a for n, a in args.items()}], core_ids=[0])
    return r.results[0]["out"].reshape(IMAGES, SEQ, DIM)
```
